# Optimizing a Trainium2 kernel written in Bass

```python
import numpy as np
import jax
import jax.numpy as jnp

def _softmax(x, axis=-1):
    return jax.nn.softmax(x, axis=axis)

def _gelu(x):
    return jax.nn.gelu(x, approximate=True)

def _silu(x):
    return jax.nn.silu(x)

def _sigmoid(x):
    return jax.nn.sigmoid(x)

def _layernorm(x, axis=-1, eps=1e-05):
    m = jnp.mean(x, axis=axis, keepdims=True)
    v = jnp.var(x, axis=axis, keepdims=True)
    return (x - m) / jnp.sqrt(v + eps)

def _scatter_add(tgt, idx, src, axis=0):
    return tgt.at[idx].add(src)

def _segment_sum(src, seg, n):
    return jax.ops.segment_sum(src, seg, n)
kernel_name = 'mk_decoder_preln_d1_seqx_r2_4a93a6'

def setup_inputs(seed: int=0):
    np.random.seed(seed)
    _w = jnp.asarray

    def _rec_inputs():
        import jax
        import jax.numpy as jnp
        _rk = jax.random.key(seed)
        x = 7.22e-05 + 1 * jax.random.normal(jax.random.fold_in(_rk, 1), (2, 1024, 512), jnp.float32)
        _lenS = 1024 - jax.random.randint(jax.random.fold_in(_rk, 7), (2,), 0, max(1, 1024 // 4) + 1, jnp.int32)
        _lenS2 = 2048 - jax.random.randint(jax.random.fold_in(_rk, 8), (2,), 0, max(1, 2048 // 4) + 1, jnp.int32)
        _ctx_1024P = jax.random.normal(jax.random.fold_in(_rk, 11), (2, 16, 512), jnp.float32)
        _ctx_1024c = jax.random.dirichlet(jax.random.fold_in(_rk, 511), 0.3 * jnp.ones((16,), jnp.float32), (2, 2048))
        _ctx_1024t = jnp.einsum('bsk,bkd->bsd', _ctx_1024c, _ctx_1024P)
        _ctx_1024t = _ctx_1024t * jax.lax.rsqrt(jnp.mean(jnp.square(_ctx_1024t)) + 1e-12) * 0.953939
        ctx_1024 = 4.13588e-05 + 0.999923 * (_ctx_1024t + 0.3 * jax.random.normal(jax.random.fold_in(_rk, 611), (2, 2048, 512), jnp.float32))
        _validS = jnp.arange(1024)[None, :] < _lenS[:, None]
        _validS2 = jnp.arange(2048)[None, :] < _lenS2[:, None]
        _causal = jnp.tril(jnp.ones((1024, 1024), dtype=bool))
        mask_BxSxS2_if1 = jnp.where(jnp.ones((2, 1024, 2048), dtype=bool), 1, 0).astype(jnp.int32)
        return (x, ctx_1024, mask_BxSxS2_if1)
    x, ctx_1024, mask_BxSxS2_if1 = _rec_inputs()

    def _L0_attn_setup():
        import jax, jax.numpy as jnp
        import numpy as np
        B, N, DIM = (2, 1024, 512)
        H, DH = (16, 64)
        EPS = 1e-12

        def _l2norm(t):
            n = jnp.sqrt(jnp.sum(t * t, axis=-1, keepdims=True))
            return t / jnp.maximum(n, EPS)
        key = jax.random.key(seed)
        ks = jax.random.split(key, 8)
        inner = H * DH
        s = 0.02
        return {'x': jax.random.normal(ks[0], (B, N, DIM), dtype=jnp.float32), 'Wq': jax.random.normal(ks[1], (inner, DIM), dtype=jnp.float32) * s, 'Wk': jax.random.normal(ks[2], (inner, DIM), dtype=jnp.float32) * s, 'Wv': jax.random.normal(ks[3], (inner, DIM), dtype=jnp.float32) * s, 'Wo': jax.random.normal(ks[4], (DIM, inner), dtype=jnp.float32) * s, 'bo': jnp.zeros((DIM,), dtype=jnp.float32), 'q_scale': jnp.ones((H, 1, DH), dtype=jnp.float32), 'k_scale': jnp.ones((H, 1, DH), dtype=jnp.float32)}
    _L0_attn_all = _L0_attn_setup()
    _L0_attn_in = {k: v for k, v in _L0_attn_all.items() if k in ('Wq', 'Wk', 'Wv', 'Wo', 'bo', 'q_scale', 'k_scale')}
    del _L0_attn_all

    def _L0_xattn_setup():
        import jax, jax.numpy as jnp
        import numpy as np
        N_HEAD = 16
        D_MODEL = 512
        D_K = D_MODEL // N_HEAD
        NEG = -1000000000.0
        key = jax.random.key(seed)
        ks = jax.random.split(key, 7)
        B, L = (4, 1024)
        q = jax.random.normal(ks[0], (B, L, D_MODEL), dtype=jnp.float32)
        k = jax.random.normal(ks[1], (B, L, D_MODEL), dtype=jnp.float32)
        v = jax.random.normal(ks[2], (B, L, D_MODEL), dtype=jnp.float32)
        mask = jnp.ones((B, L, L), dtype=jnp.int32)
        s = 1.0 / np.sqrt(D_MODEL)
        w_q = jax.random.normal(ks[3], (D_MODEL, D_MODEL), dtype=jnp.float32) * s
        w_k = jax.random.normal(ks[4], (D_MODEL, D_MODEL), dtype=jnp.float32) * s
        w_v = jax.random.normal(ks[5], (D_MODEL, D_MODEL), dtype=jnp.float32) * s
        w_o = jax.random.normal(ks[6], (D_MODEL, D_MODEL), dtype=jnp.float32) * s
        return {'q': q, 'k': k, 'v': v, 'w_q': w_q, 'w_k': w_k, 'w_v': w_v, 'w_o': w_o, 'mask': mask}
    _L0_xattn_all = _L0_xattn_setup()
    _L0_xattn_in = {k: v for k, v in _L0_xattn_all.items() if k in ('w_q', 'w_k', 'w_v', 'w_o')}
    del _L0_xattn_all

    def _L0_ffn_setup():
        import jax, jax.numpy as jnp
        import numpy as np
        D_MODEL = 512
        M = 64
        INNER = 16
        key = jax.random.key(seed)
        ks = jax.random.split(key, 9)

        def init(k, shape, fan_in):
            bound = 1.0 / np.sqrt(fan_in)
            return jax.random.uniform(k, shape, jnp.float32, -bound, bound)
        x = jax.random.normal(ks[0], (16, 2048, D_MODEL), dtype=jnp.float32)
        Win = init(ks[1], (D_MODEL, M), D_MODEL)
        bin_ = init(ks[2], (M,), D_MODEL)
        W1 = init(ks[3], (M, INNER), 1)
        b1 = init(ks[4], (M, INNER), 1)
        W2 = init(ks[5], (M, INNER), INNER)
        b2 = init(ks[6], (M,), INNER)
        Wout = init(ks[7], (M, D_MODEL), M)
        bout = init(ks[8], (D_MODEL,), M)
        return {'x': x, 'Win': Win, 'bin_': bin_, 'W1': W1, 'b1': b1, 'W2': W2, 'b2': b2, 'Wout': Wout, 'bout': bout}
    _L0_ffn_all = _L0_ffn_setup()
    _L0_ffn_in = {k: v for k, v in _L0_ffn_all.items() if k in ('Win', 'bin_', 'W1', 'b1', 'W2', 'b2', 'Wout', 'bout')}
    del _L0_ffn_all
    return {'x': x, 'ctx_1024': ctx_1024, 'mask_BxSxS2_if1': mask_BxSxS2_if1, 'L0_attn_Wq': _L0_attn_in['Wq'], 'L0_attn_Wk': _L0_attn_in['Wk'], 'L0_attn_Wv': _L0_attn_in['Wv'], 'L0_attn_Wo': _L0_attn_in['Wo'], 'L0_attn_bo': _L0_attn_in['bo'], 'L0_attn_q_scale': _L0_attn_in['q_scale'], 'L0_attn_k_scale': _L0_attn_in['k_scale'], 'L0_xattn_w_q': _L0_xattn_in['w_q'], 'L0_xattn_w_k': _L0_xattn_in['w_k'], 'L0_xattn_w_v': _L0_xattn_in['w_v'], 'L0_xattn_w_o': _L0_xattn_in['w_o'], 'L0_ffn_Win': _L0_ffn_in['Win'], 'L0_ffn_bin_': _L0_ffn_in['bin_'], 'L0_ffn_W1': _L0_ffn_in['W1'], 'L0_ffn_b1': _L0_ffn_in['b1'], 'L0_ffn_W2': _L0_ffn_in['W2'], 'L0_ffn_b2': _L0_ffn_in['b2'], 'L0_ffn_Wout': _L0_ffn_in['Wout'], 'L0_ffn_bout': _L0_ffn_in['bout']}

def reference(x, ctx_1024, mask_BxSxS2_if1, L0_attn_Wq, L0_attn_Wk, L0_attn_Wv, L0_attn_Wo, L0_attn_bo, L0_attn_q_scale, L0_attn_k_scale, L0_xattn_w_q, L0_xattn_w_k, L0_xattn_w_v, L0_xattn_w_o, L0_ffn_Win, L0_ffn_bin_, L0_ffn_W1, L0_ffn_b1, L0_ffn_W2, L0_ffn_b2, L0_ffn_Wout, L0_ffn_bout):
    import jax
    import jax.numpy as jnp

    def _L0_attn_ref(x, Wq, Wk, Wv, Wo, bo, q_scale, k_scale):
        import jax, jax.numpy as jnp
        import numpy as np
        B, N, DIM = (2, 1024, 512)
        H, DH = (16, 64)
        EPS = 1e-12

        def _l2norm(t):
            n = jnp.sqrt(jnp.sum(t * t, axis=-1, keepdims=True))
            return t / jnp.maximum(n, EPS)
        b, n, _ = x.shape
        q = jnp.einsum('bnd,ed->bne', x, Wq).reshape(b, n, H, DH).transpose(0, 2, 1, 3)
        k = jnp.einsum('bnd,ed->bne', x, Wk).reshape(b, n, H, DH).transpose(0, 2, 1, 3)
        v = jnp.einsum('bnd,ed->bne', x, Wv).reshape(b, n, H, DH).transpose(0, 2, 1, 3)
        q = _l2norm(q) * q_scale
        k = _l2norm(k) * k_scale
        attn = jnp.einsum('bhid,bhjd->bhij', q, k) * DH ** (-0.5)
        attn = jax.nn.softmax(attn, axis=-1)
        out = jnp.einsum('bhij,bhjd->bhid', attn, v)
        out = out.transpose(0, 2, 1, 3).reshape(b, n, H * DH)
        return jnp.einsum('bne,de->bnd', out, Wo) + bo

    def _L0_xattn_ref(q, k, v, w_q, w_k, w_v, w_o, mask):
        import jax, jax.numpy as jnp
        import numpy as np
        N_HEAD = 16
        D_MODEL = 512
        D_K = D_MODEL // N_HEAD
        NEG = -1000000000.0
        B, Lq, _ = q.shape
        temperature = jnp.asarray(D_K, q.dtype) ** 0.5
        qh = (q @ w_q.T).reshape(B, Lq, N_HEAD, D_K).transpose(0, 2, 1, 3)
        kh = (k @ w_k.T).reshape(B, -1, N_HEAD, D_K).transpose(0, 2, 1, 3)
        vh = (v @ w_v.T).reshape(B, -1, N_HEAD, D_K).transpose(0, 2, 1, 3)
        attn = jnp.einsum('bhqd,bhkd->bhqk', qh / temperature, kh)
        attn = jnp.where(mask[:, None, :, :] == 0, NEG, attn)
        attn = jax.nn.softmax(attn, axis=-1)
        out = jnp.einsum('bhqk,bhkd->bhqd', attn, vh)
        out = out.transpose(0, 2, 1, 3).reshape(B, Lq, D_MODEL)
        return out @ w_o.T

    def _L0_ffn_ref(x, Win, bin_, W1, b1, W2, b2, Wout, bout):
        import jax, jax.numpy as jnp
        import numpy as np
        D_MODEL = 512
        M = 64
        INNER = 16
        s = jnp.einsum('btd,dm->btm', x, Win) + bin_
        h = jax.nn.relu(s[..., None] * W1 + b1)
        g = jnp.einsum('btmh,mh->btm', h, W2) + b2
        out = jnp.einsum('btm,md->btd', g, Wout) + bout
        return out
    x = x + _L0_attn_ref(_layernorm(x, axis=-1), L0_attn_Wq, L0_attn_Wk, L0_attn_Wv, L0_attn_Wo, L0_attn_bo, L0_attn_q_scale, L0_attn_k_scale)
    x = x + _L0_xattn_ref(_layernorm(x, axis=-1), ctx_1024, ctx_1024, L0_xattn_w_q, L0_xattn_w_k, L0_xattn_w_v, L0_xattn_w_o, mask_BxSxS2_if1)
    x = x + _L0_ffn_ref(_layernorm(x, axis=-1), L0_ffn_Win, L0_ffn_bin_, L0_ffn_W1, L0_ffn_b1, L0_ffn_W2, L0_ffn_b2, L0_ffn_Wout, L0_ffn_bout)
    return x

_drawn_inputs = setup_inputs


def setup_inputs(seed=0):
    import zlib

    import numpy as np

    out = dict(_drawn_inputs(seed))
    spreads = {'L0_attn_bo': (0.0, 0.1), 'L0_attn_q_scale': (1.0, 0.6), 'L0_attn_k_scale': (1.0, 0.6)}
    factors = {'L0_attn_Wq': 8.0,
     'L0_attn_Wk': 8.0,
     'L0_attn_Wv': 7.577,
     'L0_attn_Wo': 7.51,
     'L0_ffn_bin_': 24.319}
    for name, (base, spread) in spreads.items():
        noise = np.random.default_rng([zlib.crc32(name.encode()), seed]).standard_normal(out[name].shape)
        drawn = base * np.exp(spread * noise) if base else spread * noise
        out[name] = jnp.asarray(drawn.astype(out[name].dtype))
    for name, factor in factors.items():
        out[name] = (out[name] * factor).astype(out[name].dtype)
    return out
```

```python
from contextlib import ExitStack

import concourse.bass as bass
from concourse import mybir

P = 128
B, N, D = 2, 1024, 512
L = 2048
H, DH = 16, 64
DK = 32
INNER = H * DH
T = B * N
M, HID = 64, 16
LN_EPS = 1e-5
NORM_EPS = 1e-12
CONSTS = 5 + 4
SAFE = 60.0

DC = D // P
EC = INNER // P
PAIRS = H // 2
GROUPS = H // 4
TT = N // P
JT = L // P
HALF = 512
NH = N // HALF

ALU = mybir.AluOpType
ACT = mybir.ActivationFunctionType
F32 = mybir.dt.float32
F32R = mybir.dt.float32r
AX_X = mybir.AxisListType.X


def words(ap):
    return ap.bitcast(F32)


def decoder_layer(nc, x, ctxT, mask, wqkv, woT, bo, qk_scale, xwqT, xwkvT, xwoT,
                  win, bin_, w1, b1, w2, b2, wout, bout, out):
    top = ExitStack()
    with top:
        def sem(name):
            return top.enter_context(nc.semaphore(name))

        def scratch(name, shape, dt=F32):
            return nc.dram_tensor(name, shape, dt, kind="Internal").ap()

        attnT_dram = scratch("attnT_dram", (B, PAIRS, P, N))
        sum1_dram = scratch("sum1_dram", (B, PAIRS, 2, N))
        rsum1_dram = scratch("rsum1_dram", (B, PAIRS, 2, N))
        x1_dram = scratch("x1_dram", (B, N, D))
        q2_dram = scratch("q2_dram", (B * GROUPS, 4, 2, DK, N))
        k2_dram = scratch("k2_dram", (B * GROUPS, 4, 2, DK, L))
        v2_dram = scratch("v2_dram", (B * GROUPS, P, JT, P))
        attn2T_dram = scratch("attn2T_dram", (B, GROUPS, P, N))
        sum2_dram = scratch("sum2_dram", (B, GROUPS, 4, N))
        rsum2_dram = scratch("rsum2_dram", (B, GROUPS, 4, N))

        ident = top.enter_context(nc.sbuf_tensor("ident", [P, P], F32))
        ones = top.enter_context(nc.sbuf_tensor("ones", [P, 32], F32))
        ones_block = top.enter_context(nc.sbuf_tensor("ones_block", [P, P], F32R))
        norm2_k = top.enter_context(nc.sbuf_tensor("norm2_k", [P, B, L // HALF, GROUPS], F32))
        norm2_q = top.enter_context(nc.sbuf_tensor("norm2_q", [P, B, NH, GROUPS], F32))
        mask_min = top.enter_context(nc.sbuf_tensor("mask_min", [P, B * L // HALF], F32))
        flags = top.enter_context(nc.sbuf_tensor("flags", [P, 2], mybir.dt.int32))
        flag = [flags[0:1, i:i + 1] for i in range(2)]
        s_const = sem("s_const")

        self_sems = []

        def self_sem(name):
            self_sems.append(nc.alloc_semaphore(name=name))
            return self_sems[-1]

        self_attention(nc, self_sem, x, wqkv, qk_scale, attnT_dram, sum1_dram, ident, ones, ones_block, s_const,
                       scratch, flags, flag[0])
        nc.clear_and_free_semaphores(self_sems)
        nc.all_engine_barrier()
        context_projections(nc, sem, ctxT, mask, xwkvT, k2_dram, v2_dram, ones_block, norm2_k, mask_min)
        output_projection(nc, sem, "b", attnT_dram, sum1_dram, rsum1_dram, woT, bo, x, x1_dram, ident,
                          query=(xwqT, q2_dram, ones_block, norm2_q))
        cross_attention(nc, sem, q2_dram, k2_dram, v2_dram, attn2T_dram, sum2_dram, ones)
        cross_flag(nc, sem, norm2_q, norm2_k, mask_min, flags)
        stacked = [slice(i * 2 * DK, (i + 1) * 2 * DK) for i in range(2)]
        exact_attention(
            nc, sem, "exact_x_", flag[1], GROUPS, 4, P, DK, JT, DK ** -0.5,
            lambda b, g, h, f, t: [(t[rows, :], q2_dram.rearrange("(b g) h s q t -> b g h (s q) t", g=GROUPS)
                                    [b, g, h, :, f * HALF:(f + 1) * HALF]) for rows in stacked],
            lambda b, g, h, j, t: [(t[64 * i + 32 * c:64 * i + 32 * c + 32, :],
                                    k2_dram.rearrange("(b g) h s q t -> b g h s q t", g=GROUPS)
                                    [b, g, h, i, :, bass.ds(j * P, P)]) for i in range(2) for c in range(2)],
            lambda b, g, h, j: v2_dram.rearrange("(b g) q j e -> b g j q e", g=GROUPS)[b, g, j, :, h * DK:(h + 1) * DK],
            mask,
            lambda b, g, h, f: attn2T_dram[b, g, h * DK:(h + 1) * DK, f * HALF:(f + 1) * HALF],
            lambda b, g, h, f: sum2_dram[b, g, h:h + 1, f * HALF:(f + 1) * HALF], ones)
        output_projection(nc, sem, "e", attn2T_dram, sum2_dram, rsum2_dram, xwoT, None,
                          x1_dram, None, ident, ffn=(win, bin_, w1, b1, w2, b2, wout, bout, out))


def self_attention(nc, sem, x, wqkv, qk_scale, attnT_dram, sum1_dram, ident, ones, ones_block, s_const,
                   scratch, flags, flag):
    with ExitStack() as outer:
        def sbo(name, shape, dt=F32):
            return outer.enter_context(nc.sbuf_tensor(name, shape, dt))

        xnT_hi = sbo("xnT_hi", [P, DC, T], F32R)
        xnT_lo = sbo("xnT_lo", [P, DC, T], F32R)

        with ExitStack() as ctx:
            tiles = T // P
            xt = ctx.enter_context(nc.sbuf_tensor("ln_x", [P, tiles, D], F32))
            xn = ctx.enter_context(nc.sbuf_tensor("ln_xn", [P, 2, D], F32))
            stats = ctx.enter_context(nc.sbuf_tensor("ln_stats", [P, tiles, 6], F32))
            mv = ctx.enter_context(nc.sbuf_tensor("ln_mv", [P, tiles, 2], F32))
            var = ctx.enter_context(nc.sbuf_tensor("ln_var", [P, tiles], F32))
            rstd = ctx.enter_context(nc.sbuf_tensor("ln_rstd", [P, tiles], F32))
            mhalf = ctx.enter_context(nc.sbuf_tensor("ln_mhalf", [P, tiles], F32))
            blocks = ctx.enter_context(nc.sbuf_tensor("ln_blocks", [P, P], F32))
            both_scales = ctx.enter_context(nc.sbuf_tensor("ln_scales", [P, PAIRS, 2], F32))
            prod = ctx.enter_context(nc.sbuf_tensor("ln_prod", [P, PAIRS], F32))
            prod2 = ctx.enter_context(nc.sbuf_tensor("ln_prod2", [P, PAIRS], F32))
            peak = ctx.enter_context(nc.sbuf_tensor("ln_peak", [P, 2], F32))
            tp = ctx.enter_context(nc.psum_tensor("ln_tp", [P, 2, HALF], F32))
            s_scales, s_prod, s_peak, s_flag = sem("ln_scales"), sem("ln_prod"), sem("ln_peak"), sem("ln_flag")
            s_x = [sem(f"ln_x{i}") for i in range(4)]
            s_stat, s_aggr, s_var, s_rstd = sem("ln_stat"), sem("ln_aggr"), sem("ln_var"), sem("ln_rstd")
            s_xn, s_tr, s_hi, s_lo = sem("ln_xn"), sem("ln_tr"), sem("ln_hi"), sem("ln_lo")
            block = ctx.enter_context(nc.Block())

            @block.sync
            def _(sp):
                for i in range(4):
                    sp.dma_start(xt[:, 4 * i:4 * i + 4, :],
                                 x.rearrange("b (n p) d -> p (b n) d", p=P)[:, 4 * i:4 * i + 4, :]).then_inc(s_x[i], 16)
                sp.dma_start(both_scales[:], qk_scale.rearrange("p q s -> q p s")).then_inc(s_scales, 16)

            @block.gpsimd
            def _(pool):
                pool.memset(ident[:], 0.0).then_inc(s_const, 1)
                pool.memset(ones[:], 1.0).then_inc(s_const, 1)
                pool.memset(mhalf[:], -0.5).then_inc(s_const, 1)
                pool.memset(blocks[:], 0.0).then_inc(s_const, 1)
                pool.wait_ge(s_const, 4)
                pool.affine_select(out=ident[:], in_=ident[:], compare_op=ALU.not_equal, fill=1.0, base=0,
                                   pattern=[[-1, P]], channel_multiplier=1).then_inc(s_const, 1)
                for h in range(4):
                    pool.wait_ge(s_const, 5 + h)
                    pool.memset(blocks[32 * h:32 * h + 32, 32 * h:32 * h + 32], 1.0).then_inc(s_const, 1)
                pool.wait_ge(s_const, CONSTS)
                for i in range(4):
                    pool.wait_ge(s_var, i + 1)
                    pool.tensor_tensor(rstd[:, 4 * i:4 * i + 4], var[:, 4 * i:4 * i + 4], mhalf[:, 0:4],
                                       ALU.pow).then_inc(s_rstd, 1)
                pool.wait_ge(s_rstd, 4)
                pool.wait_ge(s_prod, 3)
                pool.partition_all_reduce(peak[:, 1:2], peak[:, 0:1], P, bass.bass_isa.ReduceOp.max).then_inc(s_peak, 1)

            @block.vector
            def _(dve):
                def low(n):
                    dve.wait_ge(s_hi, n + 1)
                    dve.tensor_tensor(xnT_lo[:, :, n * P:(n + 1) * P],
                                      tp[:, n % 2, :].rearrange("p (c t) -> p c t", c=DC),
                                      xnT_hi[:, :, n * P:(n + 1) * P].bitcast(F32), ALU.subtract).then_inc(s_lo, 1)

                def statistics(i):
                    dve.wait_ge(s_x[i], 16)
                    for n in range(4 * i, 4 * i + 4):
                        dve.bn_stats(stats[:, n, :], xt[:, n, :]).then_inc(s_stat, 1)
                        dve.wait_ge(s_stat, n + 1)
                        dve.bn_aggr(mv[:, n, :], stats[:, n, :]).then_inc(s_aggr, 1)
                    dve.wait_ge(s_aggr, 4 * i + 4)
                    dve.tensor_scalar(var[:, 4 * i:4 * i + 4], mv[:, 4 * i:4 * i + 4, 1], LN_EPS, None,
                                      ALU.add).then_inc(s_var, 1)

                statistics(0)
                for i in range(4):
                    if i < 3:
                        statistics(i + 1)
                    dve.wait_ge(s_rstd, i + 1)
                    for n in range(4 * i, 4 * i + 4):
                        if n >= 2:
                            dve.wait_ge(s_tr, n - 1)
                        dve.tensor_scalar(xn[:, n % 2, :], xt[:, n, :], mv[:, n, 0:1], rstd[:, n:n + 1],
                                          ALU.subtract, ALU.mult).then_inc(s_xn, 1)
                        if n >= 1:
                            low(n - 1)
                low(tiles - 1)
                dve.wait_ge(s_scales, 16)
                dve.tensor_tensor(prod[:], both_scales[:, :, 0], both_scales[:, :, 1], ALU.mult).then_inc(s_prod, 1)
                dve.wait_ge(s_prod, 1)
                dve.tensor_tensor(prod2[:], prod[:], prod[:], ALU.mult).then_inc(s_prod, 1)
                dve.wait_ge(s_prod, 2)
                dve.tensor_reduce(peak[:, 0:1], prod2[:], AX_X, ALU.max).then_inc(s_prod, 1)
                dve.wait_ge(s_peak, 1)
                dve.tensor_scalar(flags[:, 0:1], peak[:, 1:2], (SAFE * DH ** 0.5) ** 2, None, ALU.is_gt).then_inc(s_flag, 1)
                dve.wait_ge(s_flag, 1)

            @block.tensor
            def _(pe):
                pe.wait_ge(s_const, CONSTS)
                for n in range(tiles):
                    pe.wait_ge(s_xn, n + 1)
                    if n >= 2:
                        pe.wait_ge(s_lo, n - 1)
                    for c in range(DC):
                        last = pe.transpose(tp[:, n % 2, c * P:(c + 1) * P], xn[:, n % 2, c * P:(c + 1) * P], ident[:])
                    last.then_inc(s_tr, 1)

            @block.scalar
            def _(act):
                act.wait_ge(s_const, CONSTS)
                act.activation(ones_block[:], blocks[:], ACT.Copy)
                for n in range(tiles):
                    act.wait_ge(s_tr, n + 1)
                    act.activation(xnT_hi[:, :, n * P:(n + 1) * P],
                                   tp[:, n % 2, :].rearrange("p (c t) -> p c t", c=DC), ACT.Copy).then_inc(s_hi, 1)

        with ExitStack() as inner:
            def sb(name, shape, dt=F32):
                return inner.enter_context(nc.sbuf_tensor(name, shape, dt))

            W3 = 3 * P
            w_raw = sb("w_raw", [P, DC, W3])
            w_hi = sb("w_hi", [P, DC, W3], F32R)
            w_lo = sb("w_lo", [P, DC, W3], F32R)
            scales_raw = sb("scales_raw", [P, 2])
            scales = sb("scales", [P, 2])
            qkv = [sb(f"qkv{i}", [P, TT, W3]) for i in range(2)]
            sq = sb("sq", [P, 2, 2, 2 * P])
            ss = sb("ss", [P, 2, 8])
            nrm = sb("nrm", [P, 2, 8])
            nmax = sb("nmax", [P, 2, 8])
            rn = sb("rn", [P, 2, 8])
            half8 = sb("half8", [P, 8])
            q_st = [[sb(f"q_st{i}{h}", [P, N], F32R) for h in range(2)] for i in range(2)]
            kh_st = [[sb(f"kh_st{i}{h}", [P, N], F32R) for h in range(2)] for i in range(2)]
            kl_st = [[sb(f"kl_st{i}{h}", [P, N], F32R) for h in range(2)] for i in range(2)]
            probs = [[sb(f"probs{i}{h}", [P, N]) for h in range(2)] for i in range(2)]
            psum_acc = [[sb(f"pacc{i}{h}", [P, N]) for h in range(2)] for i in range(2)]
            o_sb = sb("o_sb", [P, N])
            den_sb = sb("den_sb", [P, HALF])

            sc_ps = [inner.enter_context(nc.psum_tensor(f"sc_ps{h}", [P, N], F32)) for h in range(2)]
            o_ps = inner.enter_context(nc.psum_tensor("o_ps", [P, N], F32))
            m_ps = [inner.enter_context(nc.psum_tensor(f"m_ps{i}", [P, HALF], F32)) for i in range(2)]

            s_half = sem("a_half")
            s_wraw = sem("a_wraw")
            s_whi = sem("a_whi")
            s_wlo = sem("a_wlo")
            s_proj = sem("a_proj")
            s_qkv = sem("a_qkv")
            s_ss = sem("a_ss")
            s_nrm = sem("a_nrm")
            s_rn = sem("a_rn")
            s_unit = sem("a_unit")
            s_tr = sem("a_tr")
            s_hi = sem("a_hi")
            s_lo = sem("a_lo")
            s_dup = sem("a_dup")
            s_sc = sem("a_sc")
            s_pr = sem("a_pr")
            s_pv = sem("a_pv")
            s_acc = sem("a_acc")
            s_den = sem("a_den")
            s_dsb = sem("a_dsb")
            s_osb = sem("a_osb")
            s_ost = sem("a_ost")
            s_dst = sem("a_dst")
            block = inner.enter_context(nc.Block())


            @block.sync
            def _(sp):
                def load_weights(p):
                    sp.dma_start(w_raw[:], wqkv[p].rearrange("(c q) e -> q c e", q=P)).then_inc(s_wraw, 16)
                    sp.dma_start(scales_raw[:], qk_scale[p]).then_inc(s_wraw, 16)

                def duplicate(v, par, k):
                    cols = slice(k * HALF, (k + 1) * HALF)
                    sp.wait_ge(s_hi, 8 * v + 4 * k + 4)
                    sp.wait_ge(s_lo, 8 * v + 4 * k + 4)
                    for st in (kh_st, kl_st):
                        sp.dma_start(words(st[par][0][64:128, cols]), words(st[par][0][0:64, cols])).then_inc(s_dup, 16)
                        sp.dma_start(words(st[par][1][0:64, cols]), words(st[par][1][64:128, cols])).then_inc(s_dup, 16)

                def store(u, p, b):
                    sp.wait_ge(s_osb, u + 1)
                    sp.dma_start(attnT_dram[b, p],
                                 o_sb[:]).then_inc(s_ost, 16)
                    sp.wait_ge(s_dsb, u + 1)
                    for h in range(2):
                        for f in range(NH):
                            r = 32 * (2 * f + h)
                            sp.dma_start(sum1_dram[b, p, h:h + 1, f * HALF:(f + 1) * HALF],
                                         den_sb[r:r + 1, :]).then_inc(s_dst, 16)

                def body(p, first, last):
                    u = 2 * p
                    duplicate(u + 1, 1, 0)
                    duplicate(u + 1, 1, 1)
                    if not last:
                        sp.wait_ge(s_whi, p + 2)
                        sp.wait_ge(s_wlo, p + 2)
                    store(u, p, 0)
                    if not last:
                        load_next(p)
                        duplicate(u + 2, 0, 0)
                        duplicate(u + 2, 0, 1)
                    store(u + 1, p, 1)

                def load_next(p):
                    load_weights((p + 2) % PAIRS)

                load_weights(0)
                sp.wait_ge(s_whi, 1)
                sp.wait_ge(s_wlo, 1)
                load_weights(1)
                duplicate(0, 0, 0)
                duplicate(0, 0, 1)
                body(0, True, False)
                with sp.Fori(1, PAIRS - 1) as p:
                    body(p, False, False)
                body(PAIRS - 1, False, True)
                sp.wait_ge(s_ost, 16 * 2 * PAIRS)
                sp.wait_ge(s_dst, 64 * 2 * PAIRS)
                sp.wait_ge(s_wraw, 32 * (PAIRS + 1))

            @block.gpsimd
            def _(pool):
                pool.memset(half8[:], 0.5).then_inc(s_half, 1)
                pool.wait_ge(s_half, 1)

                def root(v, k):
                    pool.wait_ge(s_ss, 4 * v + k + 1)
                    pool.tensor_tensor(nrm[:, k % 2, :], ss[:, k % 2, :], half8[:], ALU.pow).then_inc(s_nrm, 1)

                with pool.Fori(0, 2 * PAIRS) as v:
                    for k in range(4):
                        root(v, k)

            @block.tensor
            def _(pe):
                def project(v, par, p, b, t, first=False):
                    m = m_ps[t % 2]
                    if t in (0, 1):
                        if t == 0:
                            pe.wait_ge(s_whi, p + 1)
                            pe.wait_ge(s_wlo, p + 1)
                        if not first:
                            pe.wait_ge(s_lo, 8 * v)
                    elif t in (2, 3):
                        pe.wait_ge(s_qkv, 8 * v + t - 1)
                        if t == 2 and not (isinstance(v, int) and v < 2):
                            pe.wait_ge(s_dsb, v - 1)
                    elif t in (4, 5):
                        pe.wait_ge(s_qkv, 8 * v + t - 1)
                    else:
                        pe.wait_ge(s_lo, 8 * v + 4)
                    tok = slice(b * N + t * P, b * N + (t + 1) * P)
                    for c in range(DC):
                        pe.matmul(m[:, 0:W3], xnT_hi[:, c, tok], w_hi[:, c, :], start=(c == 0), stop=False)
                        pe.matmul(m[:, 0:W3], xnT_hi[:, c, tok], w_lo[:, c, :], start=False, stop=False)
                        last = pe.matmul(m[:, 0:W3], xnT_lo[:, c, tok], w_hi[:, c, :], start=False, stop=(c == DC - 1))
                    last.then_inc(s_proj, 1)

                def turn(v, par, k):
                    pe.wait_ge(s_unit, 4 * v + 2 * k + 2)
                    pe.wait_ge(s_qkv, 8 * v + (6 if k == 0 else 8))
                    for i in range(2):
                        for t in range(4):
                            last = pe.transpose(m_ps[i][:, t * P:(t + 1) * P],
                                                qkv[par][:, 4 * k + t, i * P:(i + 1) * P], ident[:])
                        last.then_inc(s_tr, 1)

                def scores(u, par, j, first=False):
                    if j == 0:
                        pe.wait_ge(s_hi, 8 * u + 8)
                        pe.wait_ge(s_lo, 8 * u + 8)
                        pe.wait_ge(s_dup, 128 * u + 128)
                    for h in range(2):
                        if not (first and j == 0):
                            pe.wait_ge(s_pr, 16 * u + 2 * j + h - 1)
                        keys = slice(j * P, (j + 1) * P)
                        for st, k_st in enumerate((kh_st, kl_st)):
                            for f in range(NH):
                                q = slice(f * HALF, (f + 1) * HALF)
                                last = pe.matmul(sc_ps[h][:, q], k_st[par][h][:, keys], q_st[par][h][:, q],
                                                 start=(st == 0), stop=(st == 1))
                        last.then_inc(s_sc, 1)

                def values(u, par, j, first=False):
                    pe.wait_ge(s_pr, 16 * u + 2 * j + 2)
                    if j == 0 and not first:
                        pe.wait_ge(s_osb, u)
                    for f in range(NH):
                        q = slice(f * HALF, (f + 1) * HALF)
                        for h in range(2):
                            last = pe.matmul(o_ps[64 * h:64 * h + 64, q],
                                             qkv[par][:, j, 2 * P + 64 * h:2 * P + 64 * h + 64], probs[j % 2][h][:, q],
                                             start=(j == 0), stop=(j == TT - 1), skip_group_check=True)
                    last.then_inc(s_pv, 1)

                def sums(u, par):
                    pe.wait_ge(s_acc, 14 * (u + 1))
                    if isinstance(u, int) and u >= 2 * PAIRS - 2:
                        pe.wait_ge(s_lo, 8 * 2 * PAIRS)
                    else:
                        pe.wait_ge(s_qkv, 8 * (u + 2) + 1)
                    for f in range(NH):
                        for h in range(2):
                            r = 32 * (2 * f + h)
                            last = pe.matmul(m_ps[0][r:r + 32, :], ones[:, 0:32],
                                             psum_acc[par][h][:, f * HALF:(f + 1) * HALF],
                                             start=True, stop=True, skip_group_check=True)
                    last.then_inc(s_den, 1)

                def body(p, first, last):
                    for b in range(2):
                        u = 2 * p + b
                        nxt = not (last and b == 1)
                        pn, bn = (p, 1) if b == 0 else (p + 1, 0)
                        for j in range(1, TT):
                            scores(u, b, j)
                            values(u, b, j - 1, first and b == 0)
                            if nxt:
                                if j in (1, 2):
                                    project(u + 1, 1 - b, pn, bn, 2 * j)
                                    project(u + 1, 1 - b, pn, bn, 2 * j + 1)
                                if j == 3:
                                    turn(u + 1, 1 - b, 0)
                                    project(u + 1, 1 - b, pn, bn, 6)
                                    project(u + 1, 1 - b, pn, bn, 7)
                                if j == 5:
                                    turn(u + 1, 1 - b, 1)
                        if nxt:
                            scores(u + 1, 1 - b, 0)
                        values(u, b, TT - 1)
                        if not last:
                            project(u + 2, b, p + 1, b, 0)
                            project(u + 2, b, p + 1, b, 1)
                        sums(u, b)

                for t in range(6):
                    project(0, 0, 0, 0, t, first=True)
                turn(0, 0, 0)
                project(0, 0, 0, 0, 6)
                project(0, 0, 0, 0, 7)
                turn(0, 0, 1)
                project(1, 1, 0, 1, 0)
                project(1, 1, 0, 1, 1)
                scores(0, 0, 0, first=True)
                body(0, True, False)
                with pe.Fori(1, PAIRS - 1) as p:
                    body(p, False, False)
                body(PAIRS - 1, False, True)

            @block.scalar
            def _(act):
                def split_weights(p):
                    act.wait_ge(s_wraw, 32 * (p + 1))
                    act.activation(scales[:], scales_raw[:], ACT.Copy)
                    act.activation(w_hi[:], w_raw[:], ACT.Copy).then_inc(s_whi, 1)

                def keep(v, par, t, first=False):
                    act.wait_ge(s_proj, 8 * v + t + 1)
                    k = t // 2
                    if not (first and k < 2):
                        act.wait_ge(s_ss, 4 * v + k - 1)
                    act.activation(sq[:, k % 2, t % 2, :], m_ps[t % 2][:, 0:2 * P], ACT.Square)
                    act.activation(qkv[par][:, t, :], m_ps[t % 2][:, 0:W3], ACT.Copy).then_inc(s_qkv, 1)

                def high(v, par, p, k):
                    cols = slice(k * HALF, (k + 1) * HALF)
                    for i, st in enumerate((q_st, kh_st)):
                        act.wait_ge(s_tr, 4 * v + 2 * k + i + 1)
                        for h in range(2):
                            rows = slice(64 * h, 64 * h + 64)
                            act.activation(st[par][h][rows, cols], m_ps[i][rows, :], ACT.Copy,
                                           scale=scales[rows, i:i + 1]).then_inc(s_hi, 1)

                def exps(u, par, j, first=False):
                    for h in range(2):
                        act.wait_ge(s_sc, 16 * u + 2 * j + h + 1)
                        if not (first and j < 2):
                            act.wait_ge(s_pv, 8 * u + j - 1)
                            act.wait_ge(s_acc, 14 * u + {0: -4, 1: -2, 2: 0, 3: 0}.get(j, 2 * (j - 3)) + h + 1)
                        act.activation(probs[j % 2][h][:], sc_ps[h][:], ACT.Exp, scale=DH ** -0.5).then_inc(s_pr, 1)

                def collect(u, par, first=False):
                    act.wait_ge(s_pv, 8 * u + 8)
                    if not first:
                        act.wait_ge(s_ost, 16 * u)
                    act.activation(o_sb[:], o_ps[:], ACT.Copy).then_inc(s_osb, 1)

                def collect_sums(u, first=False):
                    act.wait_ge(s_den, u + 1)
                    if not first:
                        act.wait_ge(s_dst, 64 * u)
                    act.activation(den_sb[:], m_ps[0][:], ACT.Copy).then_inc(s_dsb, 1)

                def body(p, first, last):
                    for b in range(2):
                        u = 2 * p + b
                        f0 = first and b == 0
                        nxt = not (last and b == 1)
                        pn = p if b == 0 else p + 1
                        for j in range(1, TT):
                            exps(u, b, j, f0)
                            if nxt:
                                if j in (1, 2):
                                    keep(u + 1, 1 - b, 2 * j)
                                    keep(u + 1, 1 - b, 2 * j + 1)
                                if j == 3:
                                    high(u + 1, 1 - b, pn, 0)
                                    keep(u + 1, 1 - b, 6)
                                    keep(u + 1, 1 - b, 7)
                                if j == 5:
                                    high(u + 1, 1 - b, pn, 1)
                                if j == 6 and b == 0 and not last:
                                    act.wait_ge(s_proj, 8 * (u + 2))
                                    act.wait_ge(s_lo, 8 * (u + 2))
                                    split_weights(p + 1)
                        if nxt:
                            exps(u + 1, 1 - b, 0)
                        collect(u, b, f0)
                        if not last:
                            keep(u + 2, b, 0)
                            keep(u + 2, b, 1)
                        collect_sums(u, f0)

                split_weights(0)
                for t in range(6):
                    keep(0, 0, t, first=True)
                high(0, 0, 0, 0)
                keep(0, 0, 6)
                keep(0, 0, 7)
                high(0, 0, 0, 1)
                keep(1, 1, 0)
                keep(1, 1, 1)
                exps(0, 0, 0, first=True)
                body(0, True, False)
                with act.Fori(1, PAIRS - 1) as p:
                    body(p, False, False)
                body(PAIRS - 1, False, True)

            @block.vector
            def _(dve):
                def split_weights(p):
                    dve.wait_ge(s_whi, p + 1)
                    dve.tensor_tensor(w_lo[:], w_raw[:], w_hi[:].bitcast(F32), ALU.subtract).then_inc(s_wlo, 1)

                def squares(v, k, first=False):
                    dve.wait_ge(s_qkv, 8 * v + 2 * k + 2)
                    if not (first and k < 2):
                        dve.wait_ge(s_nrm, 4 * v + k - 1)
                    dve.tensor_reduce(ss[:, k % 2, :], sq[:, k % 2, :, :].rearrange("p t (h d) -> p (t h) d", d=DH),
                                      AX_X, ALU.add).then_inc(s_ss, 1)

                def normalise(v, par, k):
                    dve.wait_ge(s_nrm, 4 * v + k + 1)
                    dve.tensor_scalar(nmax[:, k % 2, :], nrm[:, k % 2, :], NORM_EPS, None, ALU.max).then_inc(s_rn, 1)
                    dve.wait_ge(s_rn, 8 * v + 2 * k + 1)
                    dve.reciprocal(rn[:, k % 2, :], nmax[:, k % 2, :]).then_inc(s_rn, 1)
                    dve.wait_ge(s_rn, 8 * v + 2 * k + 2)
                    for t in range(2):
                        qk = qkv[par][:, 2 * k + t, 0:2 * P].rearrange("p (h d) -> p h d", d=DH)
                        last = dve.tensor_tensor(qk, qk,
                                                 rn[:, k % 2, 4 * t:4 * t + 4].unsqueeze(2).to_broadcast([P, 4, DH]),
                                                 ALU.mult)
                    last.then_inc(s_unit, 1)

                def low(v, par, p, k):
                    cols = slice(k * HALF, (k + 1) * HALF)
                    for i, (st, dst) in enumerate(((q_st, q_st), (kh_st, kl_st))):
                        for h in range(2):
                            rows = slice(64 * h, 64 * h + 64)
                            to = slice(64 - 64 * h, 128 - 64 * h) if i == 0 else rows
                            dve.wait_ge(s_hi, 8 * v + 4 * k + 2 * i + h + 1)
                            dve.scalar_tensor_tensor(out=dst[par][h][to, cols], in0=m_ps[i][rows, :],
                                                     scalar=scales[rows, i:i + 1],
                                                     in1=st[par][h][rows, cols].bitcast(F32),
                                                     op0=ALU.mult, op1=ALU.subtract).then_inc(s_lo, 1)

                def add(u, par, j, first=False):
                    for h in range(2):
                        dve.wait_ge(s_pr, 16 * u + 2 * j + h + 1)
                        acc = psum_acc[par][h]
                        if j == 1:
                            if not first:
                                dve.wait_ge(s_den, u - 1)
                            dve.tensor_tensor(acc[:], probs[0][h][:], probs[1][h][:], ALU.add).then_inc(s_acc, 1)
                        else:
                            dve.wait_ge(s_acc, 14 * u + 2 * (j - 2) + h + 1)
                            dve.tensor_tensor(acc[:], acc[:], probs[j % 2][h][:], ALU.add).then_inc(s_acc, 1)

                def body(p, first, last):
                    for b in range(2):
                        u = 2 * p + b
                        nxt = not (last and b == 1)
                        pn = p if b == 0 else p + 1
                        for j in range(1, TT):
                            add(u, b, j, first)
                            if nxt:
                                if j == 1:
                                    normalise(u + 1, 1 - b, 0)
                                    squares(u + 1, 1)
                                if j == 2:
                                    normalise(u + 1, 1 - b, 1)
                                    squares(u + 1, 2)
                                if j == 3:
                                    low(u + 1, 1 - b, pn, 0)
                                    normalise(u + 1, 1 - b, 2)
                                    squares(u + 1, 3)
                                if j == 4:
                                    normalise(u + 1, 1 - b, 3)
                                if j == 5:
                                    low(u + 1, 1 - b, pn, 1)
                                if j == 6 and b == 0 and not last:
                                    split_weights(p + 1)
                        if not last:
                            squares(u + 2, 0)

                split_weights(0)
                squares(0, 0, first=True)
                squares(0, 1, first=True)
                normalise(0, 0, 0)
                normalise(0, 0, 1)
                squares(0, 2, first=True)
                normalise(0, 0, 2)
                low(0, 0, 0, 0)
                squares(0, 3, first=True)
                normalise(0, 0, 3)
                low(0, 0, 0, 1)
                squares(1, 0)
                body(0, True, False)
                with dve.Fori(1, PAIRS - 1) as p:
                    body(p, False, False)
                body(PAIRS - 1, False, True)

        gq_dram = scratch("gq_dram", (B, PAIRS, P, N))
        gk_dram = scratch("gk_dram", (B, PAIRS, P, N))
        gv_dram = scratch("gv_dram", (B, PAIRS, N, P))
        exact_inputs(nc, sem, xnT_hi, xnT_lo, wqkv, qk_scale, gq_dram, gk_dram, gv_dram, ident, flag)
        exact_attention(
            nc, sem, "exact_s_", flag, PAIRS, 2, DH, DH, TT, DH ** -0.5,
            lambda b, g, h, f, t: [(t[:], gq_dram[b, g, h * DH:(h + 1) * DH, f * HALF:(f + 1) * HALF])],
            lambda b, g, h, j, t: [(t[:], gk_dram[b, g, h * DH:(h + 1) * DH, bass.ds(j * P, P)])],
            lambda b, g, h, j: gv_dram[b, g, bass.ds(j * P, P), h * DH:(h + 1) * DH],
            None,
            lambda b, g, h, f: attnT_dram[b, g, h * DH:(h + 1) * DH, f * HALF:(f + 1) * HALF],
            lambda b, g, h, f: sum1_dram[b, g, h:h + 1, f * HALF:(f + 1) * HALF], ones)


def exact_inputs(nc, sem, xnT_hi, xnT_lo, wqkv, qk_scale, gq_dram, gk_dram, gv_dram, ident, flag):
    with ExitStack() as ctx:
        def sb(name, shape, dt=F32):
            return ctx.enter_context(nc.sbuf_tensor("gi_" + name, shape, dt))

        W3 = 3 * P
        w_raw = sb("wraw", [P, DC, W3])
        w_hi = sb("whi", [P, DC, W3], F32R)
        w_lo = sb("wlo", [P, DC, W3], F32R)
        scales = sb("scales", [P, 2])
        x_hi = sb("xhi", [P, DC, P], F32R)
        x_lo = sb("xlo", [P, DC, P], F32R)
        qkv = sb("qkv", [P, W3])
        sq = sb("sq", [P, 2 * P])
        ss, nrm, nmax, rn, half4 = (sb(k, [P, 4]) for k in ("ss", "nrm", "nmax", "rn", "half4"))
        qkT = sb("qkT", [P, 2 * P])
        m_ps = ctx.enter_context(nc.psum_tensor("gi_m", [P, HALF], F32))
        t_ps = ctx.enter_context(nc.psum_tensor("gi_t", [P, HALF], F32))
        s_w, s_whi, s_wlo, s_half = sem("gi_w"), sem("gi_whi"), sem("gi_wlo"), sem("gi_half")
        s_cur, s_mm, s_qkv, s_ss, s_nrm = sem("gi_cur"), sem("gi_mm"), sem("gi_qkv"), sem("gi_ss"), sem("gi_nrm")
        s_rn, s_unit, s_tr, s_out, s_st = sem("gi_rn"), sem("gi_unit"), sem("gi_tr"), sem("gi_out"), sem("gi_st")
        block = ctx.enter_context(nc.Block())


        @block.sync
        def _(sp):
            taken = sp.value_load(flag, min_val=0, max_val=1)
            with sp.If(taken > 0):
                sp.nop().then_inc(s_st, 48)
                with sp.Fori(0, PAIRS) as p:
                    sp.wait_ge(s_st, 48 * B * TT * p + 48)
                    sp.dma_start(w_raw[:], wqkv[p].rearrange("(c q) e -> q c e", q=P)).then_inc(s_w, 16)
                    sp.dma_start(scales[:], qk_scale[p]).then_inc(s_w, 16)
                    for b in range(B):
                        with sp.Fori(0, TT) as t:
                            sp.wait_ge(s_out, 2 * (B * TT * p + TT * b + t) + 2)
                            sp.dma_start(gq_dram[b, p, :, bass.ds(t * P, P)], qkT[:, 0:P]).then_inc(s_st, 16)
                            sp.dma_start(gk_dram[b, p, :, bass.ds(t * P, P)], qkT[:, P:2 * P]).then_inc(s_st, 16)
                            sp.dma_start(gv_dram[b, p, bass.ds(t * P, P), :], qkv[:, 2 * P:]).then_inc(s_st, 16)
                sp.wait_ge(s_st, 48 * B * TT * PAIRS + 48)

        @block.scalar
        def _(act):
            taken = act.value_load(flag, min_val=0, max_val=1)
            with act.If(taken > 0):
                with act.Fori(0, PAIRS) as p:
                    act.wait_ge(s_w, 32 * p + 32)
                    act.activation(w_hi[:], w_raw[:], ACT.Copy).then_inc(s_whi, 1)
                    for b in range(B):
                        with act.Fori(0, TT) as t:
                            s = B * TT * p + TT * b + t
                            act.wait_ge(s_st, 48 * s + 48)
                            act.activation(x_hi[:], words(xnT_hi[:, :, bass.ds(t * P + b * N, P)]), ACT.Copy)
                            act.activation(x_lo[:], words(xnT_lo[:, :, bass.ds(t * P + b * N, P)]), ACT.Copy)\
                                .then_inc(s_cur, 1)
                            act.wait_ge(s_mm, s + 1)
                            act.activation(qkv[:], m_ps[:, 0:W3], ACT.Copy)
                            act.activation(sq[:], m_ps[:, 0:2 * P], ACT.Square).then_inc(s_qkv, 1)
                            act.wait_ge(s_tr, s + 1)
                            for i in range(2):
                                act.activation(qkT[:, i * P:(i + 1) * P], t_ps[:, i * P:(i + 1) * P], ACT.Copy,
                                               scale=scales[:, i:i + 1]).then_inc(s_out, 1)

        @block.gpsimd
        def _(pool):
            taken = pool.value_load(flag, min_val=0, max_val=1)
            with pool.If(taken > 0):
                pool.memset(half4[:], 0.5).then_inc(s_half, 1)
                pool.wait_ge(s_half, 1)
                with pool.Fori(0, PAIRS * B * TT) as s:
                    pool.wait_ge(s_ss, s + 1)
                    pool.tensor_tensor(nrm[:], ss[:], half4[:], ALU.pow).then_inc(s_nrm, 1)

        @block.vector
        def _(dve):
            taken = dve.value_load(flag, min_val=0, max_val=1)
            with dve.If(taken > 0):
                with dve.Fori(0, PAIRS) as p:
                    dve.wait_ge(s_whi, p + 1)
                    dve.tensor_tensor(w_lo[:], w_raw[:], w_hi[:].bitcast(F32), ALU.subtract).then_inc(s_wlo, 1)
                    with dve.Fori(0, B * TT) as t:
                        s = B * TT * p + t
                        dve.wait_ge(s_qkv, s + 1)
                        dve.tensor_reduce(ss[:], sq[:].rearrange("p (h d) -> p h d", d=DH), AX_X, ALU.add)\
                            .then_inc(s_ss, 1)
                        dve.wait_ge(s_nrm, s + 1)
                        dve.tensor_scalar(nmax[:], nrm[:], NORM_EPS, None, ALU.max).then_inc(s_rn, 1)
                        dve.wait_ge(s_rn, 2 * s + 1)
                        dve.reciprocal(rn[:], nmax[:]).then_inc(s_rn, 1)
                        dve.wait_ge(s_rn, 2 * s + 2)
                        qk = qkv[:, 0:2 * P].rearrange("p (h d) -> p h d", d=DH)
                        dve.tensor_tensor(qk, qk, rn[:].unsqueeze(2).to_broadcast([P, 4, DH]), ALU.mult)\
                            .then_inc(s_unit, 1)

        @block.tensor
        def _(pe):
            taken = pe.value_load(flag, min_val=0, max_val=1)
            with pe.If(taken > 0):
                with pe.Fori(0, PAIRS) as p:
                    with pe.Fori(0, B * TT) as t:
                        s = B * TT * p + t
                        pe.wait_ge(s_wlo, p + 1)
                        pe.wait_ge(s_cur, s + 1)
                        for c in range(DC):
                            pe.matmul(m_ps[:, 0:W3], x_hi[:, c, :], w_hi[:, c, :], start=(c == 0), stop=False)
                            pe.matmul(m_ps[:, 0:W3], x_hi[:, c, :], w_lo[:, c, :], start=False, stop=False)
                            last = pe.matmul(m_ps[:, 0:W3], x_lo[:, c, :], w_hi[:, c, :], start=False, stop=(c == DC - 1))
                        last.then_inc(s_mm, 1)
                        pe.wait_ge(s_unit, s + 1)
                        for i in range(2):
                            last = pe.transpose(t_ps[:, i * P:(i + 1) * P], qkv[:, i * P:(i + 1) * P], ident[:])
                        last.then_inc(s_tr, 1)


def exact_attention(nc, sem, tag, flag, G, HG, K, W, KT, scale, load_q, load_k, load_v, mask, store_o, store_sums, ones):
    with ExitStack() as ctx:
        def sb(name, shape, dt=F32):
            return ctx.enter_context(nc.sbuf_tensor(tag + name, shape, dt))

        q_sb = sb("q", [K, HALF])
        k_sb = sb("k", [K, P])
        v_sb = sb("v", [P, W])
        mask_sb = sb("mask", [P, HALF], mybir.dt.int32)
        keep = sb("keep", [P, HALF])
        penalty = sb("penalty", [P, HALF])
        logits = sb("logits", [P, HALF])
        kept = sb("kept", [P, HALF])
        final = sb("final", [P, HALF])
        top = sb("top", [P, HALF])
        top_bc = sb("topbc", [P, HALF])
        below = sb("below", [P, HALF])
        probs = sb("probs", [P, HALF])
        zero = sb("zero", [P, HALF])
        o_sb = sb("o", [W, HALF])
        den_sb = sb("den", [32, HALF])
        sc_ps = ctx.enter_context(nc.psum_tensor(tag + "sc_ps", [P, HALF], F32))
        o_ps = ctx.enter_context(nc.psum_tensor(tag + "o_ps", [P, HALF], F32))
        den_ps = ctx.enter_context(nc.psum_tensor(tag + "den_ps", [P, HALF], F32))

        def s(name):
            return sem(tag + name)

        s_q, s_in1, s_in2 = s("q"), s("in1"), s("in2")
        s_sc, s_v, s_max, s_mbc = s("sc"), s("v"), s("max"), s("mbc")
        s_below, s_p, s_pv, s_osb, s_st, s_top, s_zero = s("below"), s("p"), s("pv"), s("osb"), s("st"), s("top"), s("zero")
        block = ctx.enter_context(nc.Block())
        NV = 1 if mask is None else 5
        Q1 = 16 * len(load_q(0, 0, 0, 0, q_sb))
        N1 = 16 * (len(load_k(0, 0, 0, 0, k_sb)) + (0 if mask is None else 1))
        N2 = N1 + 16
        UNITS = B * G * HG * NH

        def unit(b, g, h, f):
            return NH * HG * (G * b + g) + NH * h + f

        def over_units(eng, work):
            for b in range(B):
                with eng.Fori(0, G) as g:
                    for h in range(HG):
                        for f in range(NH):
                            work(b, g, h, f, unit(b, g, h, f))

        @block.sync
        def _(sp):
            taken = sp.value_load(flag, min_val=0, max_val=1)
            with sp.If(taken > 0):
                sp.nop().then_inc(s_max, 1)
                sp.nop().then_inc(s_pv, 1)
                sp.nop().then_inc(s_st, 32)

                def work(b, g, h, f, c):
                    sp.wait_ge(s_pv, KT * c + 1)
                    for ap, src in load_q(b, g, h, f, q_sb):
                        sp.dma_start(ap, src).then_inc(s_q, 16)
                    with sp.Fori(0, KT) as j:
                        sp.wait_ge(s_max, KT * c + j + 1)
                        if mask is not None:
                            sp.dma_start(mask_sb[:], mask[b, bass.ds(j * P, P), f * HALF:(f + 1) * HALF]).then_inc(s_in1, 16)
                        for ap, src in load_k(b, g, h, j, k_sb):
                            sp.dma_start(ap, src).then_inc(s_in1, 16)
                    with sp.Fori(0, KT) as j:
                        sp.wait_ge(s_max, KT * c + KT + 1)
                        sp.wait_ge(s_pv, KT * c + j + 1)
                        if mask is not None:
                            sp.dma_start(mask_sb[:], mask[b, bass.ds(j * P, P), f * HALF:(f + 1) * HALF]).then_inc(s_in2, 16)
                        for ap, src in load_k(b, g, h, j, k_sb):
                            sp.dma_start(ap, src).then_inc(s_in2, 16)
                        sp.dma_start(v_sb[:], load_v(b, g, h, j)).then_inc(s_in2, 16)
                    sp.wait_ge(s_osb, 2 * c + 2 + 1)
                    sp.dma_start(store_o(b, g, h, f), o_sb[:]).then_inc(s_st, 16)
                    sp.dma_start(store_sums(b, g, h, f), den_sb[0:1, :]).then_inc(s_st, 16)

                over_units(sp, work)
                sp.wait_ge(s_st, 32 * UNITS + 32)

        @block.tensor
        def _(pe):
            taken = pe.value_load(flag, min_val=0, max_val=1)
            with pe.If(taken > 0):
                pe.wait_ge(s_zero, 1)

                def work(b, g, h, f, c):
                    pe.wait_ge(s_q, Q1 * c + Q1)
                    pe.wait_ge(s_osb, 2 * c + 1)
                    pe.matmul(o_ps[0:W, :], zero[:, 0:W], zero[:], start=True, stop=False, skip_group_check=True)
                    pe.matmul(den_ps[0:32, :], zero[:, 0:32], zero[:], start=True, stop=False, skip_group_check=True)
                    with pe.Fori(0, KT) as j:
                        pe.wait_ge(s_in1, N1 * (KT * c + j) + N1)
                        pe.matmul(sc_ps[:], k_sb[:], q_sb[:], start=True, stop=True).then_inc(s_sc, 1)
                    with pe.Fori(0, KT) as j:
                        pe.wait_ge(s_in2, N2 * (KT * c + j) + N2)
                        pe.matmul(sc_ps[:], k_sb[:], q_sb[:], start=True, stop=True).then_inc(s_sc, 1)
                        pe.wait_ge(s_p, KT * c + j + 1)
                        pe.matmul(o_ps[0:W, :], v_sb[:], probs[:], start=False, stop=False, skip_group_check=True)
                        pe.matmul(den_ps[0:32, :], ones[:, 0:32], probs[:], start=False, stop=False,
                                  skip_group_check=True).then_inc(s_pv, 1)

                over_units(pe, work)

        @block.vector
        def _(dve):
            taken = dve.value_load(flag, min_val=0, max_val=1)
            with dve.If(taken > 0):

                def masked(step):
                    dve.wait_ge(s_sc, step + 1)
                    dve.tensor_scalar(logits[:], sc_ps[:], scale, None, ALU.mult).then_inc(s_v, 1)
                    if mask is None:
                        dve.wait_ge(s_v, step + 1)
                        return logits
                    dve.tensor_scalar(keep[:], mask_sb[:], 0.0, None, ALU.not_equal).then_inc(s_v, 1)
                    dve.wait_ge(s_v, NV * step + 2)
                    dve.tensor_scalar(penalty[:], keep[:], 1.0, 1e9, ALU.subtract, ALU.mult).then_inc(s_v, 1)
                    dve.tensor_tensor(kept[:], logits[:], keep[:], ALU.mult).then_inc(s_v, 1)
                    dve.wait_ge(s_v, NV * step + 4)
                    dve.tensor_tensor(final[:], kept[:], penalty[:], ALU.add).then_inc(s_v, 1)
                    dve.wait_ge(s_v, NV * step + 5)
                    return final

                def work(b, g, h, f, c):
                    dve.wait_ge(s_zero, 1)
                    dve.wait_ge(s_mbc, c + 1)
                    dve.tensor_scalar(top[:], zero[:], -3e38, None, ALU.add).then_inc(s_top, 1)
                    with dve.Fori(0, KT) as j:
                        tile = masked(2 * KT * c + j)
                        dve.wait_ge(s_top, c + 1)
                        dve.tensor_tensor(top[:], top[:], tile[:], ALU.max).then_inc(s_max, 1)
                        dve.wait_ge(s_max, KT * c + j + 2)
                    with dve.Fori(0, KT) as j:
                        tile = masked(2 * KT * c + KT + j)
                        dve.wait_ge(s_mbc, c + 2)
                        dve.tensor_tensor(below[:], tile[:], top_bc[:], ALU.subtract).then_inc(s_below, 1)

                over_units(dve, work)

        @block.gpsimd
        def _(pool):
            taken = pool.value_load(flag, min_val=0, max_val=1)
            with pool.If(taken > 0):
                pool.memset(zero[:], 0.0).then_inc(s_zero, 1)
                pool.nop().then_inc(s_mbc, 1)
                for c in range(UNITS):
                    pool.wait_ge(s_max, KT * c + KT + 1)
                    pool.partition_all_reduce(top_bc[:], top[:], P, bass.bass_isa.ReduceOp.max).then_inc(s_mbc, 1)

        @block.scalar
        def _(act):
            taken = act.value_load(flag, min_val=0, max_val=1)
            with act.If(taken > 0):
                act.nop().then_inc(s_osb, 1)

                def work(b, g, h, f, c):
                    with act.Fori(0, KT) as j:
                        act.wait_ge(s_below, KT * c + j + 1)
                        act.activation(probs[:], below[:], ACT.Exp).then_inc(s_p, 1)
                    act.wait_ge(s_pv, KT * c + KT + 1)
                    act.wait_ge(s_st, 32 * c + 32)
                    act.activation(o_sb[:], o_ps[0:W, :], ACT.Copy).then_inc(s_osb, 1)
                    act.activation(den_sb[:], den_ps[0:32, :], ACT.Copy).then_inc(s_osb, 1)

                over_units(act, work)


def cross_flag(nc, sem, norm2_q, norm2_k, mask_min, flags):
    with ExitStack() as ctx:
        def sb(name, shape):
            return ctx.enter_context(nc.sbuf_tensor("f_" + name, shape, F32))

        top_q, top_k, prod = (sb(k, [P, B, GROUPS]) for k in ("top_q", "top_k", "prod"))
        low = sb("low", [P, 1])
        worst = sb("worst", [P, 2])
        worst_all = sb("worst_all", [P, 2])
        over = sb("over", [P, 2])
        s_red, s_worst, s_all, s_over, s_flag = sem("f_red"), sem("f_worst"), sem("f_all"), sem("f_over"), sem("f_flag")
        block = ctx.enter_context(nc.Block())

        @block.vector
        def _(dve):
            dve.tensor_reduce(top_q[:], norm2_q[:].rearrange("p b c g -> p b g c"), AX_X, ALU.max).then_inc(s_red, 1)
            dve.tensor_reduce(top_k[:], norm2_k[:].rearrange("p b c g -> p b g c"), AX_X, ALU.max).then_inc(s_red, 1)
            dve.tensor_reduce(low[:], mask_min[:], AX_X, ALU.min).then_inc(s_red, 1)
            dve.wait_ge(s_red, 3)
            dve.tensor_tensor(prod[:], top_q[:], top_k[:], ALU.mult).then_inc(s_red, 1)
            dve.tensor_scalar(worst[:, 1:2], low[:], 0.5, None, ALU.is_lt).then_inc(s_worst, 1)
            dve.wait_ge(s_red, 4)
            dve.tensor_reduce(worst[:, 0:1], prod[:].rearrange("p b g -> p (b g)"), AX_X, ALU.max).then_inc(s_worst, 1)
            dve.wait_ge(s_all, 1)
            dve.tensor_scalar(over[:, 0:1], worst_all[:, 0:1], (SAFE * DK ** 0.5) ** 2, None, ALU.is_gt).then_inc(s_over, 1)
            dve.wait_ge(s_over, 1)
            dve.tensor_tensor(over[:, 1:2], over[:, 0:1], worst_all[:, 1:2], ALU.add).then_inc(s_over, 1)
            dve.wait_ge(s_over, 2)
            dve.tensor_scalar(flags[:, 1:2], over[:, 1:2], 0.5, None, ALU.is_gt).then_inc(s_flag, 1)
            dve.wait_ge(s_flag, 1)

        @block.gpsimd
        def _(pool):
            pool.wait_ge(s_worst, 2)
            pool.partition_all_reduce(worst_all[:], worst[:], P, bass.bass_isa.ReduceOp.max).then_inc(s_all, 1)


def context_projections(nc, sem, ctxT, mask, xwkvT, k2_dram, v2_dram, ones_block, norm2_k, mask_min):
    CH = L // HALF
    with ExitStack() as ctx:
        def sb(name, shape, dt=F32):
            return ctx.enter_context(nc.sbuf_tensor(name, shape, dt))

        w_raw = sb("c_wraw", [P, 2, DC, D])
        w_hi = sb("c_whi", [P, 2, DC, D], F32R)
        w_lo = sb("c_wlo", [P, 2, DC, D], F32R)
        c_raw = [sb(f"c_raw{i}", [P, DC, HALF]) for i in range(2)]
        c_hi = [sb(f"c_hi{i}", [P, DC, HALF], F32R) for i in range(2)]
        c_lo = [sb(f"c_lo{i}", [P, DC, HALF], F32R) for i in range(2)]
        k_hi = sb("c_khi", [P, GROUPS, HALF], F32R)
        k_lo = sb("c_klo", [P, GROUPS, HALF], F32R)
        v_sb = sb("c_v", [P, 4, D])
        k_sq = sb("c_ksq", [P, GROUPS, HALF], F32R)
        CHUNKS = B * CH
        mask_rows = mask.rearrange("b l t -> (b l t)").rearrange("(n p v) -> n p v", n=CHUNKS, p=P)
        mask_sb = [sb(f"c_mask{i}", [P, B * L * N // (CHUNKS * P)], mybir.dt.int32) for i in range(2)]
        ps = [ctx.enter_context(nc.psum_tensor(f"c_ps{i}", [P, HALF], F32)) for i in range(8)]

        s_w, s_whi, s_wlo = sem("c_w"), sem("c_whi"), sem("c_wlo")
        s_raw = [sem(f"c_raw{i}") for i in range(2)]
        s_hi, s_lo = sem("c_hi"), sem("c_lo")
        s_mm = sem("c_mm")
        s_khi, s_klo, s_v = sem("c_khi"), sem("c_klo"), sem("c_v")
        s_kst, s_vst = sem("c_kst"), sem("c_vst")
        s_ksq = sem("c_ksq")
        s_norm, s_top = sem("c_norm"), sem("c_top")
        s_mask = [sem(f"c_mask{i}") for i in range(2)]
        s_min = sem("c_min")
        block = ctx.enter_context(nc.Block())


        @block.sync
        def _(sp):
            sp.nop().then_inc(s_kst, 128)
            sp.nop().then_inc(s_vst, 64)
            for i in range(2):
                sp.dma_start(w_raw[:, i], xwkvT[i].rearrange("(c q) e -> q c e", q=P)).then_inc(s_w, 16)
            for b in range(B):
                sp.dma_start(c_raw[b][:], ctxT[b, 0].rearrange("(c q) t -> q c t", q=P)).then_inc(s_raw[b], 16)
            for b in range(B):
                sp.dma_start(mask_sb[b][:], mask_rows[b]).then_inc(s_mask[b], 16)
            with sp.Fori(0, CH) as jc:
                for b in range(B):
                    n = B * jc + b
                    sp.wait_ge(s_hi, n + 1)
                    sp.wait_ge(s_lo, n + 1)
                    sp.dma_start(c_raw[b][:], ctxT[b, (jc + 1) % CH].rearrange("(c q) t -> q c t", q=P))\
                        .then_inc(s_raw[b], 16)
                    sp.wait_ge(s_min, n + 1)
                    sp.dma_start(mask_sb[b][:], mask_rows[B * ((jc + 1) % CH) + b]).then_inc(s_mask[b], 16)
                    sp.wait_ge(s_klo, GROUPS * n + GROUPS)
                    for g in range(GROUPS):
                        for i, part in enumerate((k_hi, k_lo)):
                            sp.dma_start(k2_dram[GROUPS * b + g, :, i, :, bass.ds(jc * HALF, HALF)],
                                         words(part[:, g, :])).then_inc(s_kst, 16)
                    sp.wait_ge(s_v, 4 * n + 8)
                    for t in range(4):
                        sp.dma_start(v2_dram[GROUPS * b:GROUPS * (b + 1)].rearrange("g q t e -> t q g e")[4 * jc + t],
                                     v_sb[:, t, :].rearrange("p (g e) -> p g e", e=P)).then_inc(s_vst, 16)
            sp.wait_ge(s_kst, 128 + 128 * B * CH)
            sp.wait_ge(s_vst, 64 + 64 * B * CH)
            for b in range(B):
                sp.wait_ge(s_raw[b], 16 * (CH + 1))
                sp.wait_ge(s_mask[b], 16 * (CH + 1))

        @block.scalar
        def _(act):
            act.nop().then_inc(s_v, 4)
            act.nop().then_inc(s_top, GROUPS)
            act.nop().then_inc(s_norm, GROUPS)
            act.wait_ge(s_w, 32)
            act.activation(w_hi[:], w_raw[:], ACT.Copy).then_inc(s_whi, 1)
            act.wait_ge(s_raw[0], 16)
            act.activation(c_hi[0][:], c_raw[0][:], ACT.Copy).then_inc(s_hi, 1)
            with act.Fori(0, CH) as jc:
                for b in range(B):
                    n = B * jc + b
                    act.wait_ge(s_raw[1 - b], 16 * jc + 16 + 16 * b)
                    act.wait_ge(s_mm, 8 * n + 16)
                    act.activation(c_hi[1 - b][:], c_raw[1 - b][:], ACT.Copy).then_inc(s_hi, 1)
                    act.wait_ge(s_kst, 128 * n + 128)
                    for g in range(GROUPS):
                        act.wait_ge(s_mm, 8 * n + g + 17)
                        act.activation(k_hi[:, g, :], ps[g][:], ACT.Copy).then_inc(s_khi, 1)
                    act.wait_ge(s_norm, GROUPS * n + GROUPS)
                    for g in range(GROUPS):
                        act.wait_ge(s_khi, GROUPS * n + g + 1)
                        act.activation(k_sq[:, g, :], words(k_hi[:, g, :]), ACT.Square).then_inc(s_ksq, 1)
                    act.wait_ge(s_vst, 64 * n + 64)
                    for t in range(4):
                        act.wait_ge(s_mm, 8 * n + 4 + t + 17)
                        act.activation(v_sb[:, t, :], ps[4 + t][:], ACT.Copy).then_inc(s_v, 1)

        @block.vector
        def _(dve):
            dve.wait_ge(s_whi, 1)
            dve.tensor_tensor(w_lo[:], w_raw[:], w_hi[:].bitcast(F32), ALU.subtract).then_inc(s_wlo, 1)
            dve.wait_ge(s_hi, 1)
            dve.tensor_tensor(c_lo[0][:], c_raw[0][:], c_hi[0][:].bitcast(F32), ALU.subtract).then_inc(s_lo, 1)
            with dve.Fori(0, CH) as jc:
                for b in range(B):
                    n = B * jc + b
                    dve.wait_ge(s_hi, n + 2)
                    dve.tensor_tensor(c_lo[1 - b][:], c_raw[1 - b][:], c_hi[1 - b][:].bitcast(F32),
                                      ALU.subtract).then_inc(s_lo, 1)
                    dve.wait_ge(s_kst, 128 * n + 128)
                    for g in range(GROUPS):
                        dve.wait_ge(s_khi, GROUPS * n + g + 1)
                        dve.tensor_tensor(k_lo[:, g, :], ps[g][:], k_hi[:, g, :].bitcast(F32),
                                          ALU.subtract).then_inc(s_klo, 1)
                    dve.wait_ge(s_mask[b], 16 * jc + 16)
                    dve.tensor_reduce(mask_min[:, bass.ds(n, 1)], mask_sb[b][:].bitcast(mybir.dt.uint32), AX_X,
                                      ALU.min).then_inc(s_min, 1)
                    for g in range(GROUPS):
                        dve.wait_ge(s_norm, GROUPS * n + g + 1 + GROUPS)
                        dve.tensor_reduce(norm2_k[:, b, bass.ds(jc, 1), g], ps[g][:], AX_X, ALU.max).then_inc(s_top, 1)

        @block.tensor
        def _(pe):
            pe.nop().then_inc(s_mm, 16)
            pe.wait_ge(s_whi, 1)
            pe.wait_ge(s_wlo, 1)
            with pe.Fori(0, CH) as jc:
                for b in range(B):
                    n = B * jc + b
                    pe.wait_ge(s_hi, n + 1)
                    pe.wait_ge(s_lo, n + 1)
                    for g in range(GROUPS):
                        pe.wait_ge(s_top, GROUPS * n + g + 1)
                        e = slice(g * P, (g + 1) * P)
                        for c in range(DC):
                            pe.matmul(ps[g][:], w_hi[:, 0, c, e], c_hi[b][:, c, :], start=(c == 0), stop=False)
                            pe.matmul(ps[g][:], w_hi[:, 0, c, e], c_lo[b][:, c, :], start=False, stop=False)
                            last = pe.matmul(ps[g][:], w_lo[:, 0, c, e], c_hi[b][:, c, :], start=False, stop=(c == DC - 1))
                        last.then_inc(s_mm, 1)
                    for t in range(4):
                        pe.wait_ge(s_v, 4 * n + t + 1)
                        tok = slice(t * P, (t + 1) * P)
                        for c in range(DC):
                            pe.matmul(ps[4 + t][:], c_hi[b][:, c, tok], w_hi[:, 1, c, :], start=(c == 0), stop=False)
                            pe.matmul(ps[4 + t][:], c_hi[b][:, c, tok], w_lo[:, 1, c, :], start=False, stop=False)
                            last = pe.matmul(ps[4 + t][:], c_lo[b][:, c, tok], w_hi[:, 1, c, :], start=False,
                                             stop=(c == DC - 1))
                        last.then_inc(s_mm, 1)
                        if t == 1:
                            pe.wait_ge(s_klo, GROUPS * n + GROUPS)
                            for g in range(GROUPS):
                                pe.wait_ge(s_ksq, GROUPS * n + g + 1)
                                pe.matmul(ps[g][:], ones_block[:], k_sq[:, g, :], start=True, stop=True).then_inc(s_norm, 1)


def cross_attention(nc, sem, q2_dram, k2_dram, v2_dram, attn2T_dram, sum2_dram, ones):
    with ExitStack() as ctx:
        def sb(name, shape, dt=F32):
            return ctx.enter_context(nc.sbuf_tensor(name, shape, dt))

        k_st = [[sb(f"d_k{i}{h}", [P, L], F32R) for h in range(4)] for i in range(2)]
        q_st = [[sb(f"d_q{i}{h}", [P, N], F32R) for h in range(4)] for i in range(2)]
        v_sb = [sb(f"d_v{i}", [P, JT, P]) for i in range(2)]
        probs = [sb(f"d_p{i}", [P, 4 * HALF]) for i in range(2)]
        acc = [sb(f"d_acc{f}", [P, 4 * HALF]) for f in range(NH)]
        o_sb = [sb(f"d_o{f}", [P, HALF]) for f in range(NH)]
        den_sb = [sb(f"d_den{f}", [P, HALF]) for f in range(NH)]
        sc_ps = [ctx.enter_context(nc.psum_tensor(f"d_sc{i}", [P, 2 * HALF], F32)) for i in range(2)]
        o_ps = [ctx.enter_context(nc.psum_tensor(f"d_ops{f}", [P, HALF], F32)) for f in range(NH)]
        den_ps = [ctx.enter_context(nc.psum_tensor(f"d_dps{f}", [P, HALF], F32)) for f in range(NH)]

        s_in = [sem(f"d_in{i}") for i in range(2)]
        s_sc, s_pr, s_pv = sem("d_sc"), sem("d_pr"), sem("d_pv")
        s_acc, s_den = sem("d_acc"), sem("d_den")
        s_osb, s_dsb = sem("d_osb"), sem("d_dsb")
        s_ost, s_dst = ([sem(f"d_{k}{f}") for f in range(NH)] for k in ("ost", "dst"))
        block = ctx.enter_context(nc.Block())

        ITS, STEPS = B * GROUPS, NH * JT
        LOADS = 16 * (4 * 3 + 1)
        on_pe = [j for j in range(JT) if j % 4 == 3]
        on_dve = [j for j in range(1, JT) if j not in on_pe]
        ADDS = 2 * len(on_dve)

        def added(it, f, j, pair):
            return 2 + NH * ADDS * it + ADDS * f + 2 * on_dve.index(max(j, 1)) + pair + 1

        @block.sync
        def _(sp):
            for f in range(NH):
                sp.nop().then_inc(s_ost[f], 16)
                sp.nop().then_inc(s_dst[f], 16)

            def load(it, par):
                for h in range(4):
                    for i in range(2):
                        sp.dma_start(words(k_st[par][h][64 * i:64 * i + 64, :]),
                                     k2_dram[it, h, i].unsqueeze(0).to_broadcast([2, DK, L])).then_inc(s_in[par], 16)
                    sp.dma_start(words(q_st[par][h][:]), q2_dram[it, h].rearrange("s q t -> (s q) t").unsqueeze(0)
                                 .to_broadcast([2, 2 * DK, N])).then_inc(s_in[par], 16)
                sp.dma_start(v_sb[par][:], v2_dram[it]).then_inc(s_in[par], 16)

            def store(it, f):
                sp.wait_ge(s_osb, NH * it + f + 3)
                sp.dma_start(attn2T_dram.rearrange("b g q t -> (b g) q t")[it, :, f * HALF:(f + 1) * HALF],
                             o_sb[f][:]).then_inc(s_ost[f], 16)
                sp.wait_ge(s_dsb, NH * it + f + 3)
                sp.dma_start(sum2_dram.rearrange("b g h t -> (b g) h t")[it, :, f * HALF:(f + 1) * HALF],
                             den_sb[f][0:P:32, :]).then_inc(s_dst[f], 16)

            def body(i, last):
                for par in range(2):
                    it = 2 * i + par
                    store(it, 0)
                    store(it, 1)
                    if not last:
                        load(it + 2, par)

            load(0, 0)
            load(1, 1)
            with sp.Fori(0, ITS // 2 - 1) as i:
                body(i, False)
            body(ITS // 2 - 1, True)
            for f in range(NH):
                sp.wait_ge(s_ost[f], 16 + 16 * ITS)
                sp.wait_ge(s_dst[f], 16 + 16 * ITS)

        @block.tensor
        def _(pe):
            pe.nop().then_inc(s_pv, 2)

            def scores(it, par, s, nth=None, first=False):
                f, j = divmod(s, JT)
                if s == 0:
                    pe.wait_ge(s_in[par], LOADS * nth)
                for pair in range(2):
                    if not first:
                        pe.wait_ge(s_pr, 2 * STEPS * it + 2 * s + pair - 1)
                    for h in range(2):
                        last = pe.matmul(sc_ps[pair][:, h * HALF:(h + 1) * HALF],
                                         k_st[par][2 * pair + h][:, j * P:(j + 1) * P],
                                         q_st[par][2 * pair + h][:, f * HALF:(f + 1) * HALF], start=True, stop=True)
                    last.then_inc(s_sc, 1)

            def values(it, par, s):
                f, j = divmod(s, JT)
                pe.wait_ge(s_pr, 2 * STEPS * it + 2 * s + 2)
                if j == 0:
                    pe.wait_ge(s_osb, NH * it + f + 1)
                for h in range(4):
                    last = pe.matmul(o_ps[f][32 * h:32 * h + 32, :], v_sb[par][:, j, 32 * h:32 * h + 32],
                                     probs[s % 2][:, h * HALF:(h + 1) * HALF],
                                     start=(j == 0), stop=(j == JT - 1), skip_group_check=True)
                if j in on_pe:
                    if j == on_pe[0]:
                        pe.wait_ge(s_dsb, NH * it + f + 1)
                    for h in range(4):
                        last = pe.matmul(den_ps[f][32 * h:32 * h + 32, :], ones[:], probs[s % 2][:, h * HALF:(h + 1) * HALF],
                                         start=(j == on_pe[0]), stop=False, skip_group_check=True)
                last.then_inc(s_pv, 1)

            def sums(it, f):
                pe.wait_ge(s_acc, added(it, f, on_dve[-1], 1))
                for h in range(4):
                    last = pe.matmul(den_ps[f][32 * h:32 * h + 32, :], ones[:], acc[f][:, h * HALF:(h + 1) * HALF],
                                     start=False, stop=True, skip_group_check=True)
                last.then_inc(s_den, 1)

            def body(i, last):
                for par in range(2):
                    it = 2 * i + par
                    for s in range(1, STEPS):
                        scores(it, par, s)
                        values(it, par, s - 1)
                        if s == JT + 1:
                            sums(it, 0)
                    if not (last and par == 1):
                        scores(it + 1, 1 - par, 0, nth=i + 1 + par)
                    values(it, par, STEPS - 1)
                    sums(it, 1)

            scores(0, 0, 0, nth=1, first=True)
            with pe.Fori(0, ITS // 2 - 1) as i:
                body(i, False)
            body(ITS // 2 - 1, True)

        @block.scalar
        def _(act):
            act.nop().then_inc(s_osb, 2)
            act.nop().then_inc(s_dsb, 2)

            def exps(it, s):
                f, j = divmod(s, JT)
                for pair in range(2):
                    act.wait_ge(s_sc, 2 * STEPS * it + 2 * s + pair + 1)
                    act.wait_ge(s_pv, STEPS * it + s + 1)
                    if s >= 2:
                        ff, jj = divmod(s - 2, JT)
                    else:
                        ff, jj = NH - 1, JT + s - 2
                    if jj not in on_pe:
                        act.wait_ge(s_acc, added(it if s >= 2 else it - 1, ff, jj, pair))
                    act.activation(probs[s % 2][:, pair * 2 * HALF:(pair + 1) * 2 * HALF], sc_ps[pair][:],
                                   ACT.Exp, scale=DK ** -0.5).then_inc(s_pr, 1)

            def collect(it, f):
                act.wait_ge(s_pv, STEPS * it + JT * (f + 1) + 2)
                act.wait_ge(s_ost[f], 16 * (it + 1))
                act.activation(o_sb[f][:], o_ps[f][:], ACT.Copy).then_inc(s_osb, 1)

            def collect_sums(it, f):
                act.wait_ge(s_den, NH * it + f + 1)
                act.wait_ge(s_dst[f], 16 * (it + 1))
                act.activation(den_sb[f][:], den_ps[f][:], ACT.Copy).then_inc(s_dsb, 1)

            def body(i, last):
                for par in range(2):
                    it = 2 * i + par
                    for s in range(1, STEPS):
                        exps(it, s)
                        if s == JT:
                            collect(it, 0)
                        if s == JT + 1:
                            collect_sums(it, 0)
                    if not (last and par == 1):
                        exps(it + 1, 0)
                    collect(it, 1)
                    collect_sums(it, 1)

            exps(0, 0)
            with act.Fori(0, ITS // 2 - 1) as i:
                body(i, False)
            body(ITS // 2 - 1, True)

        @block.vector
        def _(dve):
            dve.nop().then_inc(s_acc, 2)

            def add(it, f, j):
                s = JT * f + j
                for pair in range(2):
                    cols = slice(pair * 2 * HALF, (pair + 1) * 2 * HALF)
                    dve.wait_ge(s_pr, 2 * STEPS * it + 2 * s + pair + 1)
                    if j == 1:
                        dve.wait_ge(s_dsb, NH * it + f + 1)
                        dve.tensor_tensor(acc[f][:, cols], probs[(s - 1) % 2][:, cols], probs[s % 2][:, cols],
                                          ALU.add).then_inc(s_acc, 1)
                    else:
                        dve.wait_ge(s_acc, added(it, f, on_dve[on_dve.index(j) - 1], pair))
                        dve.tensor_tensor(acc[f][:, cols], acc[f][:, cols], probs[s % 2][:, cols],
                                          ALU.add).then_inc(s_acc, 1)

            with dve.Fori(0, ITS) as it:
                for f in range(NH):
                    for j in on_dve:
                        add(it, f, j)


def output_projection(nc, sem, tag, attn_dram, sum_dram, rsum_dram, w_dram, bias, res_dram, keep_dram, ident,
                      query=None, ffn=None):
    C, HP = sum_dram.shape[1], sum_dram.shape[2]
    W = P // HP
    CH = N // HALF
    TC = HALF // P
    VALS = B * H * N // P
    with ExitStack() as ctx:
        def sb(name, shape, dt=F32):
            return ctx.enter_context(nc.sbuf_tensor(tag + name, shape, dt))

        w_raw = sb("wraw", [P, DC, D])
        w_hi = sb("whi", [P, C, D], F32R)
        w_lo = sb("wlo", [P, C, D], F32R)
        den = sb("den", [P, VALS])
        rden = sb("rden", [P, VALS])
        o_raw = [sb(f"oraw{i}", [P, C, HALF]) for i in range(2)]
        r_bc = sb("rbc", [P, C, HALF])
        o_hi = sb("ohi", [P, C, HALF], F32R)
        o_lo = sb("olo", [P, C, HALF], F32R)
        res = sb("res", [P, TC, D])
        y = sb("y", [P, TC, D])
        xn = sb("xn", [P, 2, D])
        stats = sb("stats", [P, TC, 6])
        mv = sb("mv", [P, TC, 2])
        var = sb("var", [P, TC])
        rstd = sb("rstd", [P, TC])
        mhalf = sb("mhalf", [P, TC])
        xT_hi = sb("xThi", [P, DC, HALF], F32R)
        xT_lo = sb("xTlo", [P, DC, HALF], F32R)
        o_ps = [ctx.enter_context(nc.psum_tensor(f"{tag}o_ps{i}", [P, HALF], F32)) for i in range(TC)]
        t_ps = [ctx.enter_context(nc.psum_tensor(f"{tag}t_ps{i}", [P, HALF], F32)) for i in range(2)]
        z_ps = [ctx.enter_context(nc.psum_tensor(f"{tag}z_ps{i}", [P, HALF], F32)) for i in range(2)]
        if bias is not None:
            bias_bc = sb("bias", [P, D])
        NW = C // DC
        if query is not None:
            xwqT, q2_dram, ones_block, norm2_q = query
            wq_hi = sb("wqhi", [P, DC, D], F32R)
            wq_lo = sb("wqlo", [P, DC, D], F32R)
            q_hi = sb("qhi", [P, GROUPS, HALF], F32R)
            q_lo = sb("qlo", [P, GROUPS, HALF], F32R)
            q_sq = sb("qsq", [P, GROUPS, HALF], F32R)
        else:
            win, bin_, w1, b1, w2, b2, wout, bout, out = ffn
            HH = HID // 2
            wi_raw = sb("wiraw", [P, DC, P])
            wi_hi = sb("wihi", [P, DC, P], F32R)
            wi_lo = sb("wilo", [P, DC, P], F32R)
            small = sb("small", [P, 3 * HH])
            bin_sb = sb("binsb", [P, 1])
            b2_sb = sb("b2sb", [P, 1])
            wo2 = sb("wo2", [P, D])
            bout_bc = sb("bout", [P, D])
            s_sb = sb("ssb", [P, HALF])
            relu = sb("relu", [P, 2, HALF])
            g_sb = sb("gsb", [P, HALF])
            fin = sb("fin", [P, 2, D])

        def s(name):
            return sem(tag + "_" + name)

        s_den, s_rden, s_rst = s("den"), s("rden"), s("rst")
        s_w, s_whi, s_wlo, s_bias, s_small, s_b2z = s("w"), s("whi"), s("wlo"), s("bias"), s("small"), s("b2z")
        s_o = [s(f"o{i}") for i in range(2)]
        s_rb, s_res = s("rb"), s("res")
        s_div, s_hi, s_lo = s("div"), s("hi"), s("lo")
        s_mm = s("mm")
        s_y0, s_y = s("y0"), s("y")
        s_yst = s("yst")
        s_st, s_ag, s_var, s_rstd = s("st"), s("ag"), s("var"), s("rstd")
        s_xn, s_tr, s_thi, s_tlo = s("xn"), s("tr"), s("thi"), s("tlo")
        s_qsq, s_norm, s_top = s("qsq"), s("norm"), s("top")
        s_z, s_qhi, s_qlo, s_qst = s("z"), s("qhi"), s("qlo"), s("qst")
        s_s, s_relu, s_g, s_f, s_fb, s_fin, s_fst = s("s"), s("relu"), s("g"), s("f"), s("fb"), s("fin"), [s("fst0"), s("fst1")]
        block = ctx.enter_context(nc.Block())


        @block.sync
        def _(sp):
            sp.nop().then_inc(s_yst, 16)
            sp.nop().then_inc(s_qst, 64)
            for i in range(2):
                sp.nop().then_inc(s_fst[i], 16)

            def load_o(n, b, half, par):
                sp.dma_start(o_raw[par][:], attn_dram[b].rearrange("c q t -> q c t")[:, :, half * HALF:(half + 1) * HALF])\
                    .then_inc(s_o[par], 16)

            def load_rest(n, b, half):
                for h in range(HP):
                    sp.dma_start(r_bc[h * W:(h + 1) * W],
                                 rsum_dram[b].rearrange("c h t -> h c t")[h][:, half * HALF:(half + 1) * HALF]
                                 .unsqueeze(0).to_broadcast([W, C, HALF])).then_inc(s_rb, 16)

            sp.dma_start(den[:], sum_dram.rearrange("b c h t -> (b c h t)").rearrange("(p v) -> p v", p=P))\
                .then_inc(s_den, 16)
            load_o(0, 0, 0, 0)
            for i in range(NW):
                if i:
                    sp.wait_ge(s_wlo, i)
                sp.dma_start(w_raw[:], w_dram.rearrange("(n c q) e -> n q c e", q=P, c=DC)[i]).then_inc(s_w, 16)
            if bias is not None:
                sp.dma_start(bias_bc[:], bias.partition_broadcast(P)).then_inc(s_bias, 16)
            if query is not None:
                sp.wait_ge(s_wlo, NW)
                sp.dma_start(w_raw[:], xwqT.rearrange("(c q) e -> q c e", q=P)).then_inc(s_w, 16)
            else:
                for i in range(2):
                    sp.dma_start(wi_raw[:, :, i * M:(i + 1) * M], win.rearrange("(c q) m -> q c m", q=P))\
                        .then_inc(s_small, 16)
                    rows = slice(i * M, (i + 1) * M)
                    for k, a in enumerate((w1, b1, w2)):
                        sp.dma_start(small[rows, k * HH:(k + 1) * HH], a[:, i * HH:(i + 1) * HH]).then_inc(s_small, 16)
                    sp.dma_start(bin_sb[rows, :], bin_.unsqueeze(1)).then_inc(s_small, 16)
                    sp.dma_start(wo2[rows, :], wout).then_inc(s_small, 16)
                sp.wait_ge(s_b2z, 1)
                sp.dma_start(b2_sb[0:M, :], b2.unsqueeze(1)).then_inc(s_small, 16)
                sp.dma_start(bout_bc[:], bout.partition_broadcast(P)).then_inc(s_small, 16)
            sp.wait_ge(s_rden, 1)
            sp.dma_start(rsum_dram.rearrange("b c h t -> (b c h t)").rearrange("(p v) -> p v", p=P), rden[:])\
                .then_inc(s_rst, 16)
            sp.wait_ge(s_rst, 16)
            load_rest(0, 0, 0)
            sp.dma_start(res[:], res_dram[0].rearrange("(c t q) d -> c q t d", q=P, t=TC)[0]).then_inc(s_res, 16)
            for b in range(B):
                for half in range(CH):
                    n = CH * b + half
                    nb, nh = (b, 1) if half == 0 else ((b + 1) % B, 0)
                    load_o(n + 1, nb, nh, 1 - half)
                    sp.wait_ge(s_div, n + 1)
                    load_rest(n + 1, nb, nh)
                    sp.wait_ge(s_y, TC * n + TC)
                    sp.dma_start(res[:], res_dram[nb].rearrange("(c t q) d -> c q t d", q=P, t=TC)[nh]).then_inc(s_res, 16)
                    if keep_dram is not None:
                        sp.dma_start(keep_dram[b].rearrange("(c t q) d -> c q t d", q=P, t=TC)[half], y[:])\
                            .then_inc(s_yst, 16)
                    if query is not None:
                        sp.wait_ge(s_qlo, GROUPS * n + 2 + GROUPS)
                        for i, part in enumerate((q_hi, q_lo)):
                            for g in range(GROUPS):
                                sp.dma_start(q2_dram.rearrange("(b g) h s q t -> b g h s q t", g=GROUPS)
                                             [b, g, :, i, :, half * HALF:(half + 1) * HALF], words(part[:, g, :]))\
                                    .then_inc(s_qst, 8 * 2)
                    else:
                        for t in range(TC):
                            sp.wait_ge(s_fin, TC * n + t + 1)
                            sp.dma_start(out[b].rearrange("(c t q) d -> c t q d", q=P, t=TC)[half, t], fin[:, t % 2, :])\
                                .then_inc(s_fst[t % 2], 16)
            for par in range(2):
                sp.wait_ge(s_o[par], 16 * (B + 1 - par))
            sp.wait_ge(s_rb, 16 * HP * (B * CH + 1))
            sp.wait_ge(s_res, 16 * (B * CH + 1))
            if keep_dram is not None:
                sp.wait_ge(s_yst, 16 + 16 * B * CH)
            if query is not None:
                sp.wait_ge(s_qst, 64 + 16 * 2 * GROUPS * B * CH)
            else:
                for i in range(2):
                    sp.wait_ge(s_fst[i], 16 + 8 * TC * B * CH)

        @block.gpsimd
        def _(pool):
            pool.memset(mhalf[:], -0.5).then_inc(s_b2z, 1) if ffn is None else pool.memset(b2_sb[:], 0.0).then_inc(s_b2z, 1)
            if ffn is not None:
                pool.memset(mhalf[:], -0.5).then_inc(s_b2z, 1)
            pool.wait_ge(s_b2z, 1 if ffn is None else 2)
            with pool.Fori(0, B * CH) as n:
                pool.wait_ge(s_var, n + 1)
                pool.tensor_tensor(rstd[:], var[:], mhalf[:], ALU.pow).then_inc(s_rstd, 1)

        @block.vector
        def _(dve):
            dve.nop().then_inc(s_lo, 1)
            dve.nop().then_inc(s_tlo, 2)
            dve.nop().then_inc(s_qlo, 2)
            dve.nop().then_inc(s_g, 1)
            dve.wait_ge(s_den, 16)
            dve.reciprocal(rden[:], den[:]).then_inc(s_rden, 1)
            for i in range(NW):
                dve.wait_ge(s_whi, i + 1)
                part = slice(i * DC, (i + 1) * DC)
                dve.tensor_tensor(w_lo[:, part], w_raw[:], w_hi[:, part].bitcast(F32), ALU.subtract).then_inc(s_wlo, 1)
            dve.wait_ge(s_whi, NW + 1)
            if query is not None:
                dve.tensor_tensor(wq_lo[:], w_raw[:], wq_hi[:].bitcast(F32), ALU.subtract).then_inc(s_wlo, 1)
            else:
                dve.tensor_tensor(wi_lo[:], wi_raw[:], wi_hi[:].bitcast(F32), ALU.subtract).then_inc(s_wlo, 1)

            with dve.Fori(0, B) as b:
                for half in range(CH):
                    n = CH * b + half
                    dve.wait_ge(s_o[half], 16 * b + 16)
                    dve.wait_ge(s_rb, 16 * HP * (n + 1))
                    dve.tensor_tensor(o_raw[half][:], o_raw[half][:], r_bc[:], ALU.mult).then_inc(s_div, 1)
                    dve.wait_ge(s_hi, n + 1)
                    dve.tensor_tensor(o_lo[:], o_raw[half][:], o_hi[:].bitcast(F32), ALU.subtract).then_inc(s_lo, 1)
                    dve.wait_ge(s_res, 16 * (n + 1))
                    if keep_dram is not None:
                        dve.wait_ge(s_yst, 16 * (n + 1))
                    if bias is not None:
                        dve.wait_ge(s_bias, 16)
                    for t in range(TC):
                        dve.wait_ge(s_mm, TC * n + t + 1)
                        if bias is not None:
                            dve.tensor_tensor(y[:, t, :], o_ps[t][:], bias_bc[:], ALU.add).then_inc(s_y0, 1)
                            dve.wait_ge(s_y0, TC * n + t + 1)
                            dve.tensor_tensor(y[:, t, :], y[:, t, :], res[:, t, :], ALU.add).then_inc(s_y, 1)
                        else:
                            dve.tensor_tensor(y[:, t, :], o_ps[t][:], res[:, t, :], ALU.add).then_inc(s_y, 1)
                        dve.wait_ge(s_y, TC * n + t + 1)
                        dve.bn_stats(stats[:, t, :], y[:, t, :]).then_inc(s_st, 1)
                        dve.wait_ge(s_den, 16)
                        dve.wait_ge(s_st, TC * n + t + 1)
                        dve.bn_aggr(mv[:, t, :], stats[:, t, :]).then_inc(s_ag, 1)
                    dve.wait_ge(s_ag, TC * n + TC)
                    dve.tensor_scalar(var[:], mv[:, :, 1], LN_EPS, None, ALU.add).then_inc(s_var, 1)
                    dve.wait_ge(s_rstd, n + 1)
                    for t in range(TC + 1):
                        if t < TC:
                            if t >= 2:
                                dve.wait_ge(s_tr, TC * n + t - 1)
                            dve.tensor_scalar(xn[:, t % 2, :], y[:, t, :], mv[:, t, 0:1], rstd[:, t:t + 1],
                                              ALU.subtract, ALU.mult).then_inc(s_xn, 1)
                        if t >= 1:
                            dve.wait_ge(s_thi, TC * n + t)
                            cols = slice((t - 1) * P, t * P)
                            dve.tensor_tensor(xT_lo[:, :, cols], t_ps[(t - 1) % 2][:].rearrange("p (c t) -> p c t", c=DC),
                                              xT_hi[:, :, cols].bitcast(F32), ALU.subtract).then_inc(s_tlo, 1)
                    if query is not None:
                        for g in range(GROUPS):
                            dve.wait_ge(s_qhi, GROUPS * n + g + 1)
                            dve.tensor_tensor(q_lo[:, g, :], z_ps[g % 2][:], q_hi[:, g, :].bitcast(F32),
                                              ALU.subtract).then_inc(s_qlo, 1)
                        for g in range(GROUPS):
                            dve.wait_ge(s_norm, GROUPS * n + g + 1)
                            dve.tensor_reduce(norm2_q[:, bass.ds(b, 1), half, g], t_ps[g % 2][:], AX_X, ALU.max)\
                                .then_inc(s_top, 1)
                    else:
                        dve.wait_ge(s_small, 16 * 14)
                        dve.wait_ge(s_z, n + 1)
                        dve.tensor_scalar(s_sb[:], z_ps[0][:], bin_sb[:, 0:1], None, ALU.add).then_inc(s_s, 1)
                        dve.wait_ge(s_f, TC * n + 1)
                        for j in range(HH):
                            dve.wait_ge(s_relu, HH * n + j + 1)
                            if j == 0:
                                dve.tensor_scalar(g_sb[:], relu[:, 0, :], small[:, 2 * HH:2 * HH + 1], b2_sb[:, 0:1],
                                                  ALU.mult, ALU.add).then_inc(s_g, 1)
                            else:
                                dve.wait_ge(s_g, HH * n + j + 1)
                                dve.scalar_tensor_tensor(out=g_sb[:], in0=relu[:, j % 2, :],
                                                         scalar=small[:, 2 * HH + j:2 * HH + j + 1], in1=g_sb[:],
                                                         op0=ALU.mult, op1=ALU.add).then_inc(s_g, 1)
                        for t in range(TC):
                            dve.wait_ge(s_f, TC * n + t + 2)
                            dve.wait_ge(s_fst[t % 2], 8 * TC * n + 16 * (t // 2 + 1))
                            dve.tensor_tensor(fin[:, t % 2, :], z_ps[t % 2][:], bout_bc[:], ALU.add).then_inc(s_fb, 1)
                            dve.wait_ge(s_fb, TC * n + t + 1)
                            dve.tensor_tensor(fin[:, t % 2, :], fin[:, t % 2, :], y[:, t, :], ALU.add).then_inc(s_fin, 1)

        @block.scalar
        def _(act):
            for i in range(NW):
                act.wait_ge(s_w, 16 * (i + 1))
                act.activation(w_hi[:, i * DC:(i + 1) * DC], w_raw[:], ACT.Copy).then_inc(s_whi, 1)
            if query is not None:
                act.wait_ge(s_w, 16 * (NW + 1))
                act.activation(wq_hi[:], w_raw[:], ACT.Copy).then_inc(s_whi, 1)
            else:
                act.wait_ge(s_small, 16 * 14)
                act.activation(wi_hi[:], wi_raw[:], ACT.Copy).then_inc(s_whi, 1)
            with act.Fori(0, B) as b:
                for half in range(CH):
                    n = CH * b + half
                    act.wait_ge(s_div, n + 1)
                    act.activation(o_hi[:], o_raw[half][:], ACT.Copy).then_inc(s_hi, 1)
                    for t in range(TC):
                        act.wait_ge(s_tr, TC * n + t + 1)
                        act.activation(xT_hi[:, :, t * P:(t + 1) * P],
                                       t_ps[t % 2][:].rearrange("p (c t) -> p c t", c=DC), ACT.Copy).then_inc(s_thi, 1)
                    if query is not None:
                        act.wait_ge(s_qst, 128 * n + 64)
                        for g in range(GROUPS):
                            act.wait_ge(s_z, GROUPS * n + g + 1)
                            act.activation(q_hi[:, g, :], z_ps[g % 2][:], ACT.Copy).then_inc(s_qhi, 1)
                            act.wait_ge(s_qhi, GROUPS * n + g + 1)
                            act.activation(q_sq[:, g, :], words(q_hi[:, g, :]), ACT.Square).then_inc(s_qsq, 1)
                    else:
                        act.wait_ge(s_s, n + 1)
                        for j in range(HH):
                            act.wait_ge(s_g, HH * n + j)
                            act.activation(relu[:, j % 2, :], s_sb[:], ACT.Relu, bias=small[:, HH + j:HH + j + 1],
                                           scale=small[:, j:j + 1]).then_inc(s_relu, 1)

        @block.tensor
        def _(pe):
            pe.nop().then_inc(s_f, 1)
            pe.nop().then_inc(s_qsq, GROUPS)
            pe.nop().then_inc(s_top, 2)

            def norm(n, g):
                pe.wait_ge(s_qsq, GROUPS * n + g + 1 + GROUPS)
                pe.wait_ge(s_top, GROUPS * n + g + 1)
                pe.matmul(t_ps[g % 2][:], ones_block[:], q_sq[:, g, :], start=True, stop=True).then_inc(s_norm, 1)

            pe.wait_ge(s_whi, NW + 1)
            pe.wait_ge(s_wlo, NW + 1)
            with pe.Fori(0, B) as b:
                for half in range(CH):
                    n = CH * b + half
                    pe.wait_ge(s_hi, n + 1)
                    pe.wait_ge(s_lo, n + 2)
                    for t in range(TC):
                        tok = slice(t * P, (t + 1) * P)
                        for c in range(C):
                            pe.matmul(o_ps[t][:], o_hi[:, c, tok], w_hi[:, c, :], start=(c == 0), stop=False)
                            pe.matmul(o_ps[t][:], o_hi[:, c, tok], w_lo[:, c, :], start=False, stop=False)
                            last = pe.matmul(o_ps[t][:], o_lo[:, c, tok], w_hi[:, c, :], start=False, stop=(c == C - 1))
                        last.then_inc(s_mm, 1)
                    for t in range(TC):
                        pe.wait_ge(s_xn, TC * n + t + 1)
                        pe.wait_ge(s_tlo, TC * n + t + 1)
                        for c in range(DC):
                            last = pe.transpose(t_ps[t % 2][:, c * P:(c + 1) * P], xn[:, t % 2, c * P:(c + 1) * P], ident[:])
                        last.then_inc(s_tr, 1)
                    pe.wait_ge(s_tlo, TC * n + TC + 2)
                    if query is not None:
                        for g in range(GROUPS):
                            pe.wait_ge(s_qlo, GROUPS * n + g + 1)
                            pe.wait_ge(s_qsq, GROUPS * n + g - 1 + GROUPS)
                            e = slice(g * P, (g + 1) * P)
                            for c in range(DC):
                                pe.matmul(z_ps[g % 2][:], wq_hi[:, c, e], xT_hi[:, c, :], start=(c == 0), stop=False)
                                pe.matmul(z_ps[g % 2][:], wq_hi[:, c, e], xT_lo[:, c, :], start=False, stop=False)
                                last = pe.matmul(z_ps[g % 2][:], wq_lo[:, c, e], xT_hi[:, c, :], start=False,
                                                 stop=(c == DC - 1))
                            last.then_inc(s_z, 1)
                            if g >= 1:
                                norm(n, g - 1)
                        norm(n, GROUPS - 1)
                    else:
                        for c in range(DC):
                            pe.matmul(z_ps[0][:], wi_hi[:, c, :], xT_hi[:, c, :], start=(c == 0), stop=False)
                            pe.matmul(z_ps[0][:], wi_hi[:, c, :], xT_lo[:, c, :], start=False, stop=False)
                            last = pe.matmul(z_ps[0][:], wi_lo[:, c, :], xT_hi[:, c, :], start=False, stop=(c == DC - 1))
                        last.then_inc(s_z, 1)
                        pe.wait_ge(s_g, HH * n + HH + 1)
                        for t in range(TC):
                            if t >= 2:
                                pe.wait_ge(s_fb, TC * n + t - 1)
                            pe.matmul(z_ps[t % 2][:], g_sb[:, t * P:(t + 1) * P], wo2[:], start=True, stop=True)\
                                .then_inc(s_f, 1)


def kernel(**inputs):
    import numpy as np
    import concourse.bacc as bacc
    from concourse.bass_utils import run_bass_kernel_spmd

    a = {k: np.asarray(v) for k, v in inputs.items()}

    def t(name):
        return a[name].T

    wqkv = np.stack([t("L0_attn_Wq").reshape(D, PAIRS, P), t("L0_attn_Wk").reshape(D, PAIRS, P),
                     t("L0_attn_Wv").reshape(D, PAIRS, P)], axis=2)
    arrays = {
        "x": a["x"],
        "ctxT": a["ctx_1024"].reshape(B, L // HALF, HALF, D).transpose(0, 1, 3, 2),
        "mask": a["mask_BxSxS2_if1"].transpose(0, 2, 1),
        "wqkv": wqkv.transpose(1, 0, 2, 3).reshape(PAIRS, D, 3 * P),
        "woT": t("L0_attn_Wo"),
        "bo": a["L0_attn_bo"],
        "qk_scale": np.stack([a["L0_attn_q_scale"].reshape(PAIRS, P), a["L0_attn_k_scale"].reshape(PAIRS, P)], axis=2),
        "xwqT": t("L0_xattn_w_q"),
        "xwkvT": np.stack([t("L0_xattn_w_k"), t("L0_xattn_w_v")]),
        "xwoT": t("L0_xattn_w_o"),
        "win": a["L0_ffn_Win"], "bin_": a["L0_ffn_bin_"], "w1": a["L0_ffn_W1"], "b1": a["L0_ffn_b1"],
        "w2": a["L0_ffn_W2"], "b2": a["L0_ffn_b2"], "wout": a["L0_ffn_Wout"], "bout": a["L0_ffn_bout"],
    }
    nc = bacc.Bacc("TRN2", target_bir_lowering=False, num_devices=1)
    args = {}
    for name, value in arrays.items():
        arrays[name] = np.ascontiguousarray(value)
        args[name] = nc.dram_tensor(name, value.shape, mybir.dt.from_np(value.dtype), kind="ExternalInput").ap()
    args["out"] = nc.dram_tensor("out", (B, N, D), F32, kind="ExternalOutput").ap()
    decoder_layer(nc, **args)
    return run_bass_kernel_spmd(nc, [arrays], core_ids=[0]).results[0]["out"]
```

```python
from contextlib import ExitStack

import concourse.bass as bass
from concourse import mybir

P = 128
B, N, D = 2, 1024, 512
L = 2048
H, DH = 16, 64
DK = 32
INNER = H * DH
T = B * N
M, HID = 64, 16
LN_EPS = 1e-5
NORM_EPS = 1e-12
CONSTS = 5 + 4
SUMS = B * H * N // P
SAFE = 60.0

DC = D // P
EC = INNER // P
PAIRS = H // 2
GROUPS = H // 4
TT = N // P
JT = L // P
HALF = 512
NH = N // HALF

ALU = mybir.AluOpType
ACT = mybir.ActivationFunctionType
F32 = mybir.dt.float32
F32R = mybir.dt.float32r
AX_X = mybir.AxisListType.X


def words(ap):
    return ap.bitcast(F32)


def by_partition(sums):
    return sums.rearrange("b c h t -> (b c h t)").rearrange("(p v) -> p v", p=P)


def decoder_layer(nc, x, ctxT, mask, wqkv, wo_xwqT, bo, qk_scale, xwkvT, xwoT,
                  win, bin_, w1, b1, w2, b2, wout, bout, out):
    top = ExitStack()
    with top:
        def sem(name):
            return top.enter_context(nc.semaphore(name))

        def scratch(name, shape, dt=F32):
            return nc.dram_tensor(name, shape, dt, kind="Internal").ap()

        attnT_dram = scratch("attnT_dram", (B, PAIRS, P, N))
        sum1_dram = scratch("sum1_dram", (B, PAIRS, 2, N))
        rsum1_dram = scratch("rsum1_dram", (B, PAIRS, 2, N))
        x1_dram = scratch("x1_dram", (B, N, D))
        q2_dram = scratch("q2_dram", (B * GROUPS, 4, 2, DK, N))
        k2_dram = scratch("k2_dram", (B * GROUPS, 4, 2, DK, L))
        v2_dram = scratch("v2_dram", (B * GROUPS, P, JT, P))
        attn2T_dram = scratch("attn2T_dram", (B, GROUPS, P, N))
        sum2_dram = scratch("sum2_dram", (B, GROUPS, 4, N))
        rsum2_dram = scratch("rsum2_dram", (B, GROUPS, 4, N))

        ident = top.enter_context(nc.sbuf_tensor("ident", [P, P], F32))
        ones = top.enter_context(nc.sbuf_tensor("ones", [P, 32], F32))
        ones_block = top.enter_context(nc.sbuf_tensor("ones_block", [P, P], F32R))
        norm2_k = top.enter_context(nc.sbuf_tensor("norm2_k", [P, B, L // HALF, GROUPS], F32))
        norm2_q = top.enter_context(nc.sbuf_tensor("norm2_q", [P, B, NH, GROUPS], F32))
        mask_min = top.enter_context(nc.sbuf_tensor("mask_min", [P, 4, B * L // HALF], F32))
        flags = top.enter_context(nc.sbuf_tensor("flags", [P, 2], mybir.dt.int32))
        flag = [flags[0:1, i:i + 1] for i in range(2)]
        s_const = sem("s_const")

        self_sems = []

        def self_sem(name):
            self_sems.append(nc.alloc_semaphore(name=name))
            return self_sems[-1]

        self_attention(nc, self_sem, x, wqkv, qk_scale, attnT_dram, sum1_dram, ident, ones, ones_block, s_const,
                       scratch, flags, flag[0])
        nc.clear_and_free_semaphores(self_sems)
        nc.all_engine_barrier()
        def parts(stack, name, chunks):
            return [stack.enter_context(nc.sbuf_tensor(f"{name}_{k}", [P, chunks, D], F32R)) for k in ("hi", "lo")]

        xwo = parts(top, "xwo", DC)
        with ExitStack() as weights:
            wo_xwq = parts(weights, "wo_xwq", EC + DC)
            context_projections(nc, sem, ctxT, mask, xwkvT, k2_dram, v2_dram, ones_block, norm2_k, mask_min,
                                sum1_dram, rsum1_dram, wo_xwqT, wo_xwq)
            output_projection(nc, sem, "b", attnT_dram, None, rsum1_dram, [w[:, 0:EC, :] for w in wo_xwq], bo, x, x1_dram,
                              ident, query=([w[:, EC:, :] for w in wo_xwq], q2_dram, ones_block, norm2_q, xwoT, xwo))
        cross_attention(nc, sem, q2_dram, k2_dram, v2_dram, attn2T_dram, sum2_dram, ones)
        cross_flag(nc, sem, norm2_q, norm2_k, mask_min, flags)
        stacked = [slice(i * 2 * DK, (i + 1) * 2 * DK) for i in range(2)]
        exact_attention(
            nc, sem, "exact_x_", flag[1], GROUPS, 4, P, DK, JT, DK ** -0.5,
            lambda b, g, h, f, t: [(t[rows, :], q2_dram.rearrange("(b g) h s q t -> b g h (s q) t", g=GROUPS)
                                    [b, g, h, :, f * HALF:(f + 1) * HALF]) for rows in stacked],
            lambda b, g, h, j, t: [(t[64 * i + 32 * c:64 * i + 32 * c + 32, :],
                                    k2_dram.rearrange("(b g) h s q t -> b g h s q t", g=GROUPS)
                                    [b, g, h, i, :, bass.ds(j * P, P)]) for i in range(2) for c in range(2)],
            lambda b, g, h, j: v2_dram.rearrange("(b g) q j e -> b g j q e", g=GROUPS)[b, g, j, :, h * DK:(h + 1) * DK],
            mask,
            lambda b, g, h, f: attn2T_dram[b, g, h * DK:(h + 1) * DK, f * HALF:(f + 1) * HALF],
            lambda b, g, h, f: sum2_dram[b, g, h:h + 1, f * HALF:(f + 1) * HALF], ones)
        output_projection(nc, sem, "e", attn2T_dram, sum2_dram, rsum2_dram, xwo, None,
                          x1_dram, None, ident, ffn=(win, bin_, w1, b1, w2, b2, wout, bout, out))


def self_attention(nc, sem, x, wqkv, qk_scale, attnT_dram, sum1_dram, ident, ones, ones_block, s_const,
                   scratch, flags, flag):
    with ExitStack() as outer:
        def sbo(name, shape, dt=F32):
            return outer.enter_context(nc.sbuf_tensor(name, shape, dt))

        xnT_hi = sbo("xnT_hi", [P, DC, T], F32R)
        xnT_lo = sbo("xnT_lo", [P, DC, T], F32R)

        with ExitStack() as ctx:
            tiles = T // P
            xt = ctx.enter_context(nc.sbuf_tensor("ln_x", [P, tiles, D], F32))
            xn = ctx.enter_context(nc.sbuf_tensor("ln_xn", [P, 2, D], F32))
            stats = ctx.enter_context(nc.sbuf_tensor("ln_stats", [P, tiles, 6], F32))
            mv = ctx.enter_context(nc.sbuf_tensor("ln_mv", [P, tiles, 2], F32))
            var = ctx.enter_context(nc.sbuf_tensor("ln_var", [P, tiles], F32))
            rstd = ctx.enter_context(nc.sbuf_tensor("ln_rstd", [P, tiles], F32))
            mhalf = ctx.enter_context(nc.sbuf_tensor("ln_mhalf", [P, tiles], F32))
            blocks = ctx.enter_context(nc.sbuf_tensor("ln_blocks", [P, P], F32))
            both_scales = ctx.enter_context(nc.sbuf_tensor("ln_scales", [P, PAIRS, 2], F32))
            prod = ctx.enter_context(nc.sbuf_tensor("ln_prod", [P, PAIRS], F32))
            prod2 = ctx.enter_context(nc.sbuf_tensor("ln_prod2", [P, PAIRS], F32))
            peak = ctx.enter_context(nc.sbuf_tensor("ln_peak", [P, 2], F32))
            tp = ctx.enter_context(nc.psum_tensor("ln_tp", [P, 2, HALF], F32))
            s_scales, s_prod, s_peak, s_flag = sem("ln_scales"), sem("ln_prod"), sem("ln_peak"), sem("ln_flag")
            s_x = [sem(f"ln_x{i}") for i in range(4)]
            s_stat, s_aggr, s_var, s_rstd = sem("ln_stat"), sem("ln_aggr"), sem("ln_var"), sem("ln_rstd")
            s_xn, s_tr, s_hi, s_lo = sem("ln_xn"), sem("ln_tr"), sem("ln_hi"), sem("ln_lo")
            block = ctx.enter_context(nc.Block())

            @block.sync
            def _(sp):
                for i in range(4):
                    sp.dma_start(xt[:, 4 * i:4 * i + 4, :],
                                 x.rearrange("b (n p) d -> p (b n) d", p=P)[:, 4 * i:4 * i + 4, :]).then_inc(s_x[i], 16)
                sp.dma_start(both_scales[:], qk_scale.rearrange("p q s -> q p s")).then_inc(s_scales, 16)

            @block.gpsimd
            def _(pool):
                pool.memset(ident[:], 0.0).then_inc(s_const, 1)
                pool.memset(ones[:], 1.0).then_inc(s_const, 1)
                pool.memset(mhalf[:], -0.5).then_inc(s_const, 1)
                pool.memset(blocks[:], 0.0).then_inc(s_const, 1)
                pool.wait_ge(s_const, 4)
                pool.affine_select(out=ident[:], in_=ident[:], compare_op=ALU.not_equal, fill=1.0, base=0,
                                   pattern=[[-1, P]], channel_multiplier=1).then_inc(s_const, 1)
                for h in range(4):
                    pool.wait_ge(s_const, 5 + h)
                    pool.memset(blocks[32 * h:32 * h + 32, 32 * h:32 * h + 32], 1.0).then_inc(s_const, 1)
                pool.wait_ge(s_const, CONSTS)
                for i in range(4):
                    pool.wait_ge(s_var, i + 1)
                    pool.tensor_tensor(rstd[:, 4 * i:4 * i + 4], var[:, 4 * i:4 * i + 4], mhalf[:, 0:4],
                                       ALU.pow).then_inc(s_rstd, 1)
                pool.wait_ge(s_rstd, 4)
                pool.wait_ge(s_prod, 3)
                pool.partition_all_reduce(peak[:, 1:2], peak[:, 0:1], P, bass.bass_isa.ReduceOp.max).then_inc(s_peak, 1)

            @block.vector
            def _(dve):
                def low(n):
                    dve.wait_ge(s_hi, n + 1)
                    dve.tensor_tensor(xnT_lo[:, :, n * P:(n + 1) * P],
                                      tp[:, n % 2, :].rearrange("p (c t) -> p c t", c=DC),
                                      xnT_hi[:, :, n * P:(n + 1) * P].bitcast(F32), ALU.subtract).then_inc(s_lo, 1)

                def statistics(i):
                    dve.wait_ge(s_x[i], 16)
                    for n in range(4 * i, 4 * i + 4):
                        dve.bn_stats(stats[:, n, :], xt[:, n, :]).then_inc(s_stat, 1)
                        dve.wait_ge(s_stat, n + 1)
                        dve.bn_aggr(mv[:, n, :], stats[:, n, :]).then_inc(s_aggr, 1)
                    dve.wait_ge(s_aggr, 4 * i + 4)
                    dve.tensor_scalar(var[:, 4 * i:4 * i + 4], mv[:, 4 * i:4 * i + 4, 1], LN_EPS, None,
                                      ALU.add).then_inc(s_var, 1)

                statistics(0)
                for i in range(4):
                    if i < 3:
                        statistics(i + 1)
                    dve.wait_ge(s_rstd, i + 1)
                    for n in range(4 * i, 4 * i + 4):
                        if n >= 2:
                            dve.wait_ge(s_tr, n - 1)
                        dve.tensor_scalar(xn[:, n % 2, :], xt[:, n, :], mv[:, n, 0:1], rstd[:, n:n + 1],
                                          ALU.subtract, ALU.mult).then_inc(s_xn, 1)
                        if n >= 1:
                            low(n - 1)
                low(tiles - 1)
                dve.wait_ge(s_scales, 16)
                dve.tensor_tensor(prod[:], both_scales[:, :, 0], both_scales[:, :, 1], ALU.mult).then_inc(s_prod, 1)
                dve.wait_ge(s_prod, 1)
                dve.tensor_tensor(prod2[:], prod[:], prod[:], ALU.mult).then_inc(s_prod, 1)
                dve.wait_ge(s_prod, 2)
                dve.tensor_reduce(peak[:, 0:1], prod2[:], AX_X, ALU.max).then_inc(s_prod, 1)
                dve.wait_ge(s_peak, 1)
                dve.tensor_scalar(flags[:, 0:1], peak[:, 1:2], (SAFE * DH ** 0.5) ** 2, None, ALU.is_gt).then_inc(s_flag, 1)
                dve.wait_ge(s_flag, 1)

            @block.tensor
            def _(pe):
                pe.wait_ge(s_const, CONSTS)
                for n in range(tiles):
                    pe.wait_ge(s_xn, n + 1)
                    if n >= 2:
                        pe.wait_ge(s_lo, n - 1)
                    for c in range(DC):
                        last = pe.transpose(tp[:, n % 2, c * P:(c + 1) * P], xn[:, n % 2, c * P:(c + 1) * P], ident[:])
                    last.then_inc(s_tr, 1)

            @block.scalar
            def _(act):
                act.wait_ge(s_const, CONSTS)
                act.activation(ones_block[:], blocks[:], ACT.Copy)
                for n in range(tiles):
                    act.wait_ge(s_tr, n + 1)
                    act.activation(xnT_hi[:, :, n * P:(n + 1) * P],
                                   tp[:, n % 2, :].rearrange("p (c t) -> p c t", c=DC), ACT.Copy).then_inc(s_hi, 1)

        with ExitStack() as inner:
            def sb(name, shape, dt=F32):
                return inner.enter_context(nc.sbuf_tensor(name, shape, dt))

            W3 = 3 * P
            w_raw = sb("w_raw", [P, DC, W3])
            w_hi = sb("w_hi", [P, DC, W3], F32R)
            w_lo = sb("w_lo", [P, DC, W3], F32R)
            scales_raw = sb("scales_raw", [P, 2])
            scales = sb("scales", [P, 2])
            qkv = [sb(f"qkv{i}", [P, TT, W3]) for i in range(2)]
            sq = sb("sq", [P, 2, 2, 2 * P])
            ss = sb("ss", [P, 2, 8])
            nrm = sb("nrm", [P, 2, 8])
            nmax = sb("nmax", [P, 2, 8])
            rn = sb("rn", [P, 2, 8])
            half8 = sb("half8", [P, 8])
            q_st = [[sb(f"q_st{i}{h}", [P, N], F32R) for h in range(2)] for i in range(2)]
            kh_st = [[sb(f"kh_st{i}{h}", [P, N], F32R) for h in range(2)] for i in range(2)]
            kl_st = [[sb(f"kl_st{i}{h}", [P, N], F32R) for h in range(2)] for i in range(2)]
            probs = [[sb(f"probs{i}{h}", [P, N]) for h in range(2)] for i in range(2)]
            psum_acc = [[sb(f"pacc{i}{h}", [P, N]) for h in range(2)] for i in range(2)]
            o_sb = sb("o_sb", [P, N])
            den_sb = sb("den_sb", [P, HALF])

            sc_ps = [inner.enter_context(nc.psum_tensor(f"sc_ps{h}", [P, N], F32)) for h in range(2)]
            o_ps = inner.enter_context(nc.psum_tensor("o_ps", [P, N], F32))
            m_ps = [inner.enter_context(nc.psum_tensor(f"m_ps{i}", [P, HALF], F32)) for i in range(2)]

            s_half = sem("a_half")
            s_wraw = sem("a_wraw")
            s_whi = sem("a_whi")
            s_wlo = sem("a_wlo")
            s_proj = sem("a_proj")
            s_qkv = sem("a_qkv")
            s_ss = sem("a_ss")
            s_nrm = sem("a_nrm")
            s_rn = sem("a_rn")
            s_unit = sem("a_unit")
            s_tr = sem("a_tr")
            s_hi = sem("a_hi")
            s_lo = sem("a_lo")
            s_dup = sem("a_dup")
            s_sc = sem("a_sc")
            s_pr = sem("a_pr")
            s_pv = sem("a_pv")
            s_acc = sem("a_acc")
            s_den = sem("a_den")
            s_dsb = sem("a_dsb")
            s_osb = sem("a_osb")
            s_ost = sem("a_ost")
            s_dst = sem("a_dst")
            block = inner.enter_context(nc.Block())


            @block.sync
            def _(sp):
                def load_weights(p):
                    sp.dma_start(w_raw[:], wqkv[p].rearrange("(c q) e -> q c e", q=P)).then_inc(s_wraw, 16)
                    sp.dma_start(scales_raw[:], qk_scale[p]).then_inc(s_wraw, 16)

                def duplicate(v, par, k):
                    cols = slice(k * HALF, (k + 1) * HALF)
                    sp.wait_ge(s_hi, 8 * v + 4 * k + 4)
                    sp.wait_ge(s_lo, 8 * v + 4 * k + 4)
                    for st in (kh_st, kl_st):
                        sp.dma_start(words(st[par][0][64:128, cols]), words(st[par][0][0:64, cols])).then_inc(s_dup, 16)
                        sp.dma_start(words(st[par][1][0:64, cols]), words(st[par][1][64:128, cols])).then_inc(s_dup, 16)

                def store(u, p, b):
                    sp.wait_ge(s_osb, u + 1)
                    sp.dma_start(attnT_dram[b, p],
                                 o_sb[:]).then_inc(s_ost, 16)
                    sp.wait_ge(s_dsb, u + 1)
                    for h in range(2):
                        for f in range(NH):
                            r = 32 * (2 * f + h)
                            sp.dma_start(sum1_dram[b, p, h:h + 1, f * HALF:(f + 1) * HALF],
                                         den_sb[r:r + 1, :]).then_inc(s_dst, 16)

                def body(p, first, last):
                    u = 2 * p
                    duplicate(u + 1, 1, 0)
                    duplicate(u + 1, 1, 1)
                    if not last:
                        sp.wait_ge(s_whi, p + 2)
                        sp.wait_ge(s_wlo, p + 2)
                    store(u, p, 0)
                    if not last:
                        load_next(p)
                        duplicate(u + 2, 0, 0)
                        duplicate(u + 2, 0, 1)
                    store(u + 1, p, 1)

                def load_next(p):
                    load_weights((p + 2) % PAIRS)

                load_weights(0)
                sp.wait_ge(s_whi, 1)
                sp.wait_ge(s_wlo, 1)
                load_weights(1)
                duplicate(0, 0, 0)
                duplicate(0, 0, 1)
                body(0, True, False)
                with sp.Fori(1, PAIRS - 1) as p:
                    body(p, False, False)
                body(PAIRS - 1, False, True)
                sp.wait_ge(s_ost, 16 * 2 * PAIRS)
                sp.wait_ge(s_dst, 64 * 2 * PAIRS)
                sp.wait_ge(s_wraw, 32 * (PAIRS + 1))

            @block.gpsimd
            def _(pool):
                pool.memset(half8[:], 0.5).then_inc(s_half, 1)
                pool.wait_ge(s_half, 1)

                def root(v, k):
                    pool.wait_ge(s_ss, 4 * v + k + 1)
                    pool.tensor_tensor(nrm[:, k % 2, :], ss[:, k % 2, :], half8[:], ALU.pow).then_inc(s_nrm, 1)

                with pool.Fori(0, 2 * PAIRS) as v:
                    for k in range(4):
                        root(v, k)

            @block.tensor
            def _(pe):
                def project(v, par, p, b, t, first=False):
                    m = m_ps[t % 2]
                    if t in (0, 1):
                        if t == 0:
                            pe.wait_ge(s_whi, p + 1)
                            pe.wait_ge(s_wlo, p + 1)
                        if not first:
                            pe.wait_ge(s_lo, 8 * v)
                    elif t in (2, 3):
                        pe.wait_ge(s_qkv, 8 * v + t - 1)
                        if t == 2 and not (isinstance(v, int) and v < 2):
                            pe.wait_ge(s_dsb, v - 1)
                    elif t in (4, 5):
                        pe.wait_ge(s_qkv, 8 * v + t - 1)
                    else:
                        pe.wait_ge(s_lo, 8 * v + 4)
                    tok = slice(b * N + t * P, b * N + (t + 1) * P)
                    for c in range(DC):
                        pe.matmul(m[:, 0:W3], xnT_hi[:, c, tok], w_hi[:, c, :], start=(c == 0), stop=False)
                        pe.matmul(m[:, 0:W3], xnT_hi[:, c, tok], w_lo[:, c, :], start=False, stop=False)
                        last = pe.matmul(m[:, 0:W3], xnT_lo[:, c, tok], w_hi[:, c, :], start=False, stop=(c == DC - 1))
                    last.then_inc(s_proj, 1)

                def turn(v, par, k):
                    pe.wait_ge(s_unit, 4 * v + 2 * k + 2)
                    pe.wait_ge(s_qkv, 8 * v + (6 if k == 0 else 8))
                    for i in range(2):
                        for t in range(4):
                            last = pe.transpose(m_ps[i][:, t * P:(t + 1) * P],
                                                qkv[par][:, 4 * k + t, i * P:(i + 1) * P], ident[:])
                        last.then_inc(s_tr, 1)

                def scores(u, par, j, first=False):
                    if j == 0:
                        pe.wait_ge(s_hi, 8 * u + 8)
                        pe.wait_ge(s_lo, 8 * u + 8)
                        pe.wait_ge(s_dup, 128 * u + 128)
                    for h in range(2):
                        if not (first and j == 0):
                            pe.wait_ge(s_pr, 16 * u + 2 * j + h - 1)
                        keys = slice(j * P, (j + 1) * P)
                        for st, k_st in enumerate((kh_st, kl_st)):
                            for f in range(NH):
                                q = slice(f * HALF, (f + 1) * HALF)
                                last = pe.matmul(sc_ps[h][:, q], k_st[par][h][:, keys], q_st[par][h][:, q],
                                                 start=(st == 0), stop=(st == 1))
                        last.then_inc(s_sc, 1)

                def values(u, par, j, first=False):
                    pe.wait_ge(s_pr, 16 * u + 2 * j + 2)
                    if j == 0 and not first:
                        pe.wait_ge(s_osb, u)
                    for f in range(NH):
                        q = slice(f * HALF, (f + 1) * HALF)
                        for h in range(2):
                            last = pe.matmul(o_ps[64 * h:64 * h + 64, q],
                                             qkv[par][:, j, 2 * P + 64 * h:2 * P + 64 * h + 64], probs[j % 2][h][:, q],
                                             start=(j == 0), stop=(j == TT - 1), skip_group_check=True)
                    last.then_inc(s_pv, 1)

                def sums(u, par):
                    pe.wait_ge(s_acc, 14 * (u + 1))
                    if isinstance(u, int) and u >= 2 * PAIRS - 2:
                        pe.wait_ge(s_lo, 8 * 2 * PAIRS)
                    else:
                        pe.wait_ge(s_qkv, 8 * (u + 2) + 1)
                    for f in range(NH):
                        for h in range(2):
                            r = 32 * (2 * f + h)
                            last = pe.matmul(m_ps[0][r:r + 32, :], ones[:, 0:32],
                                             psum_acc[par][h][:, f * HALF:(f + 1) * HALF],
                                             start=True, stop=True, skip_group_check=True)
                    last.then_inc(s_den, 1)

                def body(p, first, last):
                    for b in range(2):
                        u = 2 * p + b
                        nxt = not (last and b == 1)
                        pn, bn = (p, 1) if b == 0 else (p + 1, 0)
                        for j in range(1, TT):
                            scores(u, b, j)
                            values(u, b, j - 1, first and b == 0)
                            if nxt:
                                if j in (1, 2):
                                    project(u + 1, 1 - b, pn, bn, 2 * j)
                                    project(u + 1, 1 - b, pn, bn, 2 * j + 1)
                                if j == 3:
                                    turn(u + 1, 1 - b, 0)
                                    project(u + 1, 1 - b, pn, bn, 6)
                                    project(u + 1, 1 - b, pn, bn, 7)
                                if j == 5:
                                    turn(u + 1, 1 - b, 1)
                        if nxt:
                            scores(u + 1, 1 - b, 0)
                        values(u, b, TT - 1)
                        if not last:
                            project(u + 2, b, p + 1, b, 0)
                            project(u + 2, b, p + 1, b, 1)
                        sums(u, b)

                for t in range(6):
                    project(0, 0, 0, 0, t, first=True)
                turn(0, 0, 0)
                project(0, 0, 0, 0, 6)
                project(0, 0, 0, 0, 7)
                turn(0, 0, 1)
                project(1, 1, 0, 1, 0)
                project(1, 1, 0, 1, 1)
                scores(0, 0, 0, first=True)
                body(0, True, False)
                with pe.Fori(1, PAIRS - 1) as p:
                    body(p, False, False)
                body(PAIRS - 1, False, True)

            @block.scalar
            def _(act):
                def split_weights(p):
                    act.wait_ge(s_wraw, 32 * (p + 1))
                    act.activation(scales[:], scales_raw[:], ACT.Copy)
                    act.activation(w_hi[:], w_raw[:], ACT.Copy).then_inc(s_whi, 1)

                def keep(v, par, t, first=False):
                    act.wait_ge(s_proj, 8 * v + t + 1)
                    k = t // 2
                    if not (first and k < 2):
                        act.wait_ge(s_ss, 4 * v + k - 1)
                    act.activation(sq[:, k % 2, t % 2, :], m_ps[t % 2][:, 0:2 * P], ACT.Square)
                    act.activation(qkv[par][:, t, :], m_ps[t % 2][:, 0:W3], ACT.Copy).then_inc(s_qkv, 1)

                def high(v, par, p, k):
                    cols = slice(k * HALF, (k + 1) * HALF)
                    for i, st in enumerate((q_st, kh_st)):
                        act.wait_ge(s_tr, 4 * v + 2 * k + i + 1)
                        for h in range(2):
                            rows = slice(64 * h, 64 * h + 64)
                            act.activation(st[par][h][rows, cols], m_ps[i][rows, :], ACT.Copy,
                                           scale=scales[rows, i:i + 1]).then_inc(s_hi, 1)

                def exps(u, par, j, first=False):
                    for h in range(2):
                        act.wait_ge(s_sc, 16 * u + 2 * j + h + 1)
                        if not (first and j < 2):
                            act.wait_ge(s_pv, 8 * u + j - 1)
                            act.wait_ge(s_acc, 14 * u + {0: -4, 1: -2, 2: 0, 3: 0}.get(j, 2 * (j - 3)) + h + 1)
                        act.activation(probs[j % 2][h][:], sc_ps[h][:], ACT.Exp, scale=DH ** -0.5).then_inc(s_pr, 1)

                def collect(u, par, first=False):
                    act.wait_ge(s_pv, 8 * u + 8)
                    if not first:
                        act.wait_ge(s_ost, 16 * u)
                    act.activation(o_sb[:], o_ps[:], ACT.Copy).then_inc(s_osb, 1)

                def collect_sums(u, first=False):
                    act.wait_ge(s_den, u + 1)
                    if not first:
                        act.wait_ge(s_dst, 64 * u)
                    act.activation(den_sb[:], m_ps[0][:], ACT.Copy).then_inc(s_dsb, 1)

                def body(p, first, last):
                    for b in range(2):
                        u = 2 * p + b
                        f0 = first and b == 0
                        nxt = not (last and b == 1)
                        pn = p if b == 0 else p + 1
                        for j in range(1, TT):
                            exps(u, b, j, f0)
                            if nxt:
                                if j in (1, 2):
                                    keep(u + 1, 1 - b, 2 * j)
                                    keep(u + 1, 1 - b, 2 * j + 1)
                                if j == 3:
                                    high(u + 1, 1 - b, pn, 0)
                                    keep(u + 1, 1 - b, 6)
                                    keep(u + 1, 1 - b, 7)
                                if j == 5:
                                    high(u + 1, 1 - b, pn, 1)
                                if j == 6 and b == 0 and not last:
                                    act.wait_ge(s_proj, 8 * (u + 2))
                                    act.wait_ge(s_lo, 8 * (u + 2))
                                    split_weights(p + 1)
                        if nxt:
                            exps(u + 1, 1 - b, 0)
                        collect(u, b, f0)
                        if not last:
                            keep(u + 2, b, 0)
                            keep(u + 2, b, 1)
                        collect_sums(u, f0)

                split_weights(0)
                for t in range(6):
                    keep(0, 0, t, first=True)
                high(0, 0, 0, 0)
                keep(0, 0, 6)
                keep(0, 0, 7)
                high(0, 0, 0, 1)
                keep(1, 1, 0)
                keep(1, 1, 1)
                exps(0, 0, 0, first=True)
                body(0, True, False)
                with act.Fori(1, PAIRS - 1) as p:
                    body(p, False, False)
                body(PAIRS - 1, False, True)

            @block.vector
            def _(dve):
                def split_weights(p):
                    dve.wait_ge(s_whi, p + 1)
                    dve.tensor_tensor(w_lo[:], w_raw[:], w_hi[:].bitcast(F32), ALU.subtract).then_inc(s_wlo, 1)

                def squares(v, k, first=False):
                    dve.wait_ge(s_qkv, 8 * v + 2 * k + 2)
                    if not (first and k < 2):
                        dve.wait_ge(s_nrm, 4 * v + k - 1)
                    dve.tensor_reduce(ss[:, k % 2, :], sq[:, k % 2, :, :].rearrange("p t (h d) -> p (t h) d", d=DH),
                                      AX_X, ALU.add).then_inc(s_ss, 1)

                def normalise(v, par, k):
                    dve.wait_ge(s_nrm, 4 * v + k + 1)
                    dve.tensor_scalar(nmax[:, k % 2, :], nrm[:, k % 2, :], NORM_EPS, None, ALU.max).then_inc(s_rn, 1)
                    dve.wait_ge(s_rn, 8 * v + 2 * k + 1)
                    dve.reciprocal(rn[:, k % 2, :], nmax[:, k % 2, :]).then_inc(s_rn, 1)
                    dve.wait_ge(s_rn, 8 * v + 2 * k + 2)
                    for t in range(2):
                        qk = qkv[par][:, 2 * k + t, 0:2 * P].rearrange("p (h d) -> p h d", d=DH)
                        last = dve.tensor_tensor(qk, qk,
                                                 rn[:, k % 2, 4 * t:4 * t + 4].unsqueeze(2).to_broadcast([P, 4, DH]),
                                                 ALU.mult)
                    last.then_inc(s_unit, 1)

                def low(v, par, p, k):
                    cols = slice(k * HALF, (k + 1) * HALF)
                    for i, (st, dst) in enumerate(((q_st, q_st), (kh_st, kl_st))):
                        for h in range(2):
                            rows = slice(64 * h, 64 * h + 64)
                            to = slice(64 - 64 * h, 128 - 64 * h) if i == 0 else rows
                            dve.wait_ge(s_hi, 8 * v + 4 * k + 2 * i + h + 1)
                            dve.scalar_tensor_tensor(out=dst[par][h][to, cols], in0=m_ps[i][rows, :],
                                                     scalar=scales[rows, i:i + 1],
                                                     in1=st[par][h][rows, cols].bitcast(F32),
                                                     op0=ALU.mult, op1=ALU.subtract).then_inc(s_lo, 1)

                def add(u, par, j, first=False):
                    for h in range(2):
                        dve.wait_ge(s_pr, 16 * u + 2 * j + h + 1)
                        acc = psum_acc[par][h]
                        if j == 1:
                            if not first:
                                dve.wait_ge(s_den, u - 1)
                            dve.tensor_tensor(acc[:], probs[0][h][:], probs[1][h][:], ALU.add).then_inc(s_acc, 1)
                        else:
                            dve.wait_ge(s_acc, 14 * u + 2 * (j - 2) + h + 1)
                            dve.tensor_tensor(acc[:], acc[:], probs[j % 2][h][:], ALU.add).then_inc(s_acc, 1)

                def body(p, first, last):
                    for b in range(2):
                        u = 2 * p + b
                        nxt = not (last and b == 1)
                        pn = p if b == 0 else p + 1
                        for j in range(1, TT):
                            add(u, b, j, first)
                            if nxt:
                                if j == 1:
                                    normalise(u + 1, 1 - b, 0)
                                    squares(u + 1, 1)
                                if j == 2:
                                    normalise(u + 1, 1 - b, 1)
                                    squares(u + 1, 2)
                                if j == 3:
                                    low(u + 1, 1 - b, pn, 0)
                                    normalise(u + 1, 1 - b, 2)
                                    squares(u + 1, 3)
                                if j == 4:
                                    normalise(u + 1, 1 - b, 3)
                                if j == 5:
                                    low(u + 1, 1 - b, pn, 1)
                                if j == 6 and b == 0 and not last:
                                    split_weights(p + 1)
                        if not last:
                            squares(u + 2, 0)

                split_weights(0)
                squares(0, 0, first=True)
                squares(0, 1, first=True)
                normalise(0, 0, 0)
                normalise(0, 0, 1)
                squares(0, 2, first=True)
                normalise(0, 0, 2)
                low(0, 0, 0, 0)
                squares(0, 3, first=True)
                normalise(0, 0, 3)
                low(0, 0, 0, 1)
                squares(1, 0)
                body(0, True, False)
                with dve.Fori(1, PAIRS - 1) as p:
                    body(p, False, False)
                body(PAIRS - 1, False, True)

        gq_dram = scratch("gq_dram", (B, PAIRS, P, N))
        gk_dram = scratch("gk_dram", (B, PAIRS, P, N))
        gv_dram = scratch("gv_dram", (B, PAIRS, N, P))
        exact_inputs(nc, sem, xnT_hi, xnT_lo, wqkv, qk_scale, gq_dram, gk_dram, gv_dram, ident, flag)
        exact_attention(
            nc, sem, "exact_s_", flag, PAIRS, 2, DH, DH, TT, DH ** -0.5,
            lambda b, g, h, f, t: [(t[:], gq_dram[b, g, h * DH:(h + 1) * DH, f * HALF:(f + 1) * HALF])],
            lambda b, g, h, j, t: [(t[:], gk_dram[b, g, h * DH:(h + 1) * DH, bass.ds(j * P, P)])],
            lambda b, g, h, j: gv_dram[b, g, bass.ds(j * P, P), h * DH:(h + 1) * DH],
            None,
            lambda b, g, h, f: attnT_dram[b, g, h * DH:(h + 1) * DH, f * HALF:(f + 1) * HALF],
            lambda b, g, h, f: sum1_dram[b, g, h:h + 1, f * HALF:(f + 1) * HALF], ones)


def exact_inputs(nc, sem, xnT_hi, xnT_lo, wqkv, qk_scale, gq_dram, gk_dram, gv_dram, ident, flag):
    with ExitStack() as ctx:
        def sb(name, shape, dt=F32):
            return ctx.enter_context(nc.sbuf_tensor("gi_" + name, shape, dt))

        W3 = 3 * P
        w_raw = sb("wraw", [P, DC, W3])
        w_hi = sb("whi", [P, DC, W3], F32R)
        w_lo = sb("wlo", [P, DC, W3], F32R)
        scales = sb("scales", [P, 2])
        x_hi = sb("xhi", [P, DC, P], F32R)
        x_lo = sb("xlo", [P, DC, P], F32R)
        qkv = sb("qkv", [P, W3])
        sq = sb("sq", [P, 2 * P])
        ss, nrm, nmax, rn, half4 = (sb(k, [P, 4]) for k in ("ss", "nrm", "nmax", "rn", "half4"))
        qkT = sb("qkT", [P, 2 * P])
        m_ps = ctx.enter_context(nc.psum_tensor("gi_m", [P, HALF], F32))
        t_ps = ctx.enter_context(nc.psum_tensor("gi_t", [P, HALF], F32))
        s_w, s_whi, s_wlo, s_half = sem("gi_w"), sem("gi_whi"), sem("gi_wlo"), sem("gi_half")
        s_cur, s_mm, s_qkv, s_ss, s_nrm = sem("gi_cur"), sem("gi_mm"), sem("gi_qkv"), sem("gi_ss"), sem("gi_nrm")
        s_rn, s_unit, s_tr, s_out, s_st = sem("gi_rn"), sem("gi_unit"), sem("gi_tr"), sem("gi_out"), sem("gi_st")
        block = ctx.enter_context(nc.Block())


        @block.sync
        def _(sp):
            taken = sp.value_load(flag, min_val=0, max_val=1)
            with sp.If(taken > 0):
                sp.nop().then_inc(s_st, 48)
                with sp.Fori(0, PAIRS) as p:
                    sp.wait_ge(s_st, 48 * B * TT * p + 48)
                    sp.dma_start(w_raw[:], wqkv[p].rearrange("(c q) e -> q c e", q=P)).then_inc(s_w, 16)
                    sp.dma_start(scales[:], qk_scale[p]).then_inc(s_w, 16)
                    for b in range(B):
                        with sp.Fori(0, TT) as t:
                            sp.wait_ge(s_out, 2 * (B * TT * p + TT * b + t) + 2)
                            sp.dma_start(gq_dram[b, p, :, bass.ds(t * P, P)], qkT[:, 0:P]).then_inc(s_st, 16)
                            sp.dma_start(gk_dram[b, p, :, bass.ds(t * P, P)], qkT[:, P:2 * P]).then_inc(s_st, 16)
                            sp.dma_start(gv_dram[b, p, bass.ds(t * P, P), :], qkv[:, 2 * P:]).then_inc(s_st, 16)
                sp.wait_ge(s_st, 48 * B * TT * PAIRS + 48)

        @block.scalar
        def _(act):
            taken = act.value_load(flag, min_val=0, max_val=1)
            with act.If(taken > 0):
                with act.Fori(0, PAIRS) as p:
                    act.wait_ge(s_w, 32 * p + 32)
                    act.activation(w_hi[:], w_raw[:], ACT.Copy).then_inc(s_whi, 1)
                    for b in range(B):
                        with act.Fori(0, TT) as t:
                            s = B * TT * p + TT * b + t
                            act.wait_ge(s_st, 48 * s + 48)
                            act.activation(x_hi[:], words(xnT_hi[:, :, bass.ds(t * P + b * N, P)]), ACT.Copy)
                            act.activation(x_lo[:], words(xnT_lo[:, :, bass.ds(t * P + b * N, P)]), ACT.Copy)\
                                .then_inc(s_cur, 1)
                            act.wait_ge(s_mm, s + 1)
                            act.activation(qkv[:], m_ps[:, 0:W3], ACT.Copy)
                            act.activation(sq[:], m_ps[:, 0:2 * P], ACT.Square).then_inc(s_qkv, 1)
                            act.wait_ge(s_tr, s + 1)
                            for i in range(2):
                                act.activation(qkT[:, i * P:(i + 1) * P], t_ps[:, i * P:(i + 1) * P], ACT.Copy,
                                               scale=scales[:, i:i + 1]).then_inc(s_out, 1)

        @block.gpsimd
        def _(pool):
            taken = pool.value_load(flag, min_val=0, max_val=1)
            with pool.If(taken > 0):
                pool.memset(half4[:], 0.5).then_inc(s_half, 1)
                pool.wait_ge(s_half, 1)
                with pool.Fori(0, PAIRS * B * TT) as s:
                    pool.wait_ge(s_ss, s + 1)
                    pool.tensor_tensor(nrm[:], ss[:], half4[:], ALU.pow).then_inc(s_nrm, 1)

        @block.vector
        def _(dve):
            taken = dve.value_load(flag, min_val=0, max_val=1)
            with dve.If(taken > 0):
                with dve.Fori(0, PAIRS) as p:
                    dve.wait_ge(s_whi, p + 1)
                    dve.tensor_tensor(w_lo[:], w_raw[:], w_hi[:].bitcast(F32), ALU.subtract).then_inc(s_wlo, 1)
                    with dve.Fori(0, B * TT) as t:
                        s = B * TT * p + t
                        dve.wait_ge(s_qkv, s + 1)
                        dve.tensor_reduce(ss[:], sq[:].rearrange("p (h d) -> p h d", d=DH), AX_X, ALU.add)\
                            .then_inc(s_ss, 1)
                        dve.wait_ge(s_nrm, s + 1)
                        dve.tensor_scalar(nmax[:], nrm[:], NORM_EPS, None, ALU.max).then_inc(s_rn, 1)
                        dve.wait_ge(s_rn, 2 * s + 1)
                        dve.reciprocal(rn[:], nmax[:]).then_inc(s_rn, 1)
                        dve.wait_ge(s_rn, 2 * s + 2)
                        qk = qkv[:, 0:2 * P].rearrange("p (h d) -> p h d", d=DH)
                        dve.tensor_tensor(qk, qk, rn[:].unsqueeze(2).to_broadcast([P, 4, DH]), ALU.mult)\
                            .then_inc(s_unit, 1)

        @block.tensor
        def _(pe):
            taken = pe.value_load(flag, min_val=0, max_val=1)
            with pe.If(taken > 0):
                with pe.Fori(0, PAIRS) as p:
                    with pe.Fori(0, B * TT) as t:
                        s = B * TT * p + t
                        pe.wait_ge(s_wlo, p + 1)
                        pe.wait_ge(s_cur, s + 1)
                        for c in range(DC):
                            pe.matmul(m_ps[:, 0:W3], x_hi[:, c, :], w_hi[:, c, :], start=(c == 0), stop=False)
                            pe.matmul(m_ps[:, 0:W3], x_hi[:, c, :], w_lo[:, c, :], start=False, stop=False)
                            last = pe.matmul(m_ps[:, 0:W3], x_lo[:, c, :], w_hi[:, c, :], start=False, stop=(c == DC - 1))
                        last.then_inc(s_mm, 1)
                        pe.wait_ge(s_unit, s + 1)
                        for i in range(2):
                            last = pe.transpose(t_ps[:, i * P:(i + 1) * P], qkv[:, i * P:(i + 1) * P], ident[:])
                        last.then_inc(s_tr, 1)


def exact_attention(nc, sem, tag, flag, G, HG, K, W, KT, scale, load_q, load_k, load_v, mask, store_o, store_sums, ones):
    with ExitStack() as ctx:
        def sb(name, shape, dt=F32):
            return ctx.enter_context(nc.sbuf_tensor(tag + name, shape, dt))

        q_sb = sb("q", [K, HALF])
        k_sb = sb("k", [K, P])
        v_sb = sb("v", [P, W])
        mask_sb = sb("mask", [P, HALF], mybir.dt.int32)
        keep = sb("keep", [P, HALF])
        penalty = sb("penalty", [P, HALF])
        logits = sb("logits", [P, HALF])
        kept = sb("kept", [P, HALF])
        final = sb("final", [P, HALF])
        top = sb("top", [P, HALF])
        top_bc = sb("topbc", [P, HALF])
        below = sb("below", [P, HALF])
        probs = sb("probs", [P, HALF])
        zero = sb("zero", [P, HALF])
        o_sb = sb("o", [W, HALF])
        den_sb = sb("den", [32, HALF])
        sc_ps = ctx.enter_context(nc.psum_tensor(tag + "sc_ps", [P, HALF], F32))
        o_ps = ctx.enter_context(nc.psum_tensor(tag + "o_ps", [P, HALF], F32))
        den_ps = ctx.enter_context(nc.psum_tensor(tag + "den_ps", [P, HALF], F32))

        def s(name):
            return sem(tag + name)

        s_q, s_in1, s_in2 = s("q"), s("in1"), s("in2")
        s_sc, s_v, s_max, s_mbc = s("sc"), s("v"), s("max"), s("mbc")
        s_below, s_p, s_pv, s_osb, s_st, s_top, s_zero = s("below"), s("p"), s("pv"), s("osb"), s("st"), s("top"), s("zero")
        block = ctx.enter_context(nc.Block())
        NV = 1 if mask is None else 5
        Q1 = 16 * len(load_q(0, 0, 0, 0, q_sb))
        N1 = 16 * (len(load_k(0, 0, 0, 0, k_sb)) + (0 if mask is None else 1))
        N2 = N1 + 16
        UNITS = B * G * HG * NH

        def unit(b, g, h, f):
            return NH * HG * (G * b + g) + NH * h + f

        def over_units(eng, work):
            for b in range(B):
                with eng.Fori(0, G) as g:
                    for h in range(HG):
                        for f in range(NH):
                            work(b, g, h, f, unit(b, g, h, f))

        @block.sync
        def _(sp):
            taken = sp.value_load(flag, min_val=0, max_val=1)
            with sp.If(taken > 0):
                sp.nop().then_inc(s_max, 1)
                sp.nop().then_inc(s_pv, 1)
                sp.nop().then_inc(s_st, 32)

                def work(b, g, h, f, c):
                    sp.wait_ge(s_pv, KT * c + 1)
                    for ap, src in load_q(b, g, h, f, q_sb):
                        sp.dma_start(ap, src).then_inc(s_q, 16)
                    with sp.Fori(0, KT) as j:
                        sp.wait_ge(s_max, KT * c + j + 1)
                        if mask is not None:
                            sp.dma_start(mask_sb[:], mask[b, bass.ds(j * P, P), f * HALF:(f + 1) * HALF]).then_inc(s_in1, 16)
                        for ap, src in load_k(b, g, h, j, k_sb):
                            sp.dma_start(ap, src).then_inc(s_in1, 16)
                    with sp.Fori(0, KT) as j:
                        sp.wait_ge(s_max, KT * c + KT + 1)
                        sp.wait_ge(s_pv, KT * c + j + 1)
                        if mask is not None:
                            sp.dma_start(mask_sb[:], mask[b, bass.ds(j * P, P), f * HALF:(f + 1) * HALF]).then_inc(s_in2, 16)
                        for ap, src in load_k(b, g, h, j, k_sb):
                            sp.dma_start(ap, src).then_inc(s_in2, 16)
                        sp.dma_start(v_sb[:], load_v(b, g, h, j)).then_inc(s_in2, 16)
                    sp.wait_ge(s_osb, 2 * c + 2 + 1)
                    sp.dma_start(store_o(b, g, h, f), o_sb[:]).then_inc(s_st, 16)
                    sp.dma_start(store_sums(b, g, h, f), den_sb[0:1, :]).then_inc(s_st, 16)

                over_units(sp, work)
                sp.wait_ge(s_st, 32 * UNITS + 32)

        @block.tensor
        def _(pe):
            taken = pe.value_load(flag, min_val=0, max_val=1)
            with pe.If(taken > 0):
                pe.wait_ge(s_zero, 1)

                def work(b, g, h, f, c):
                    pe.wait_ge(s_q, Q1 * c + Q1)
                    pe.wait_ge(s_osb, 2 * c + 1)
                    pe.matmul(o_ps[0:W, :], zero[:, 0:W], zero[:], start=True, stop=False, skip_group_check=True)
                    pe.matmul(den_ps[0:32, :], zero[:, 0:32], zero[:], start=True, stop=False, skip_group_check=True)
                    with pe.Fori(0, KT) as j:
                        pe.wait_ge(s_in1, N1 * (KT * c + j) + N1)
                        pe.matmul(sc_ps[:], k_sb[:], q_sb[:], start=True, stop=True).then_inc(s_sc, 1)
                    with pe.Fori(0, KT) as j:
                        pe.wait_ge(s_in2, N2 * (KT * c + j) + N2)
                        pe.matmul(sc_ps[:], k_sb[:], q_sb[:], start=True, stop=True).then_inc(s_sc, 1)
                        pe.wait_ge(s_p, KT * c + j + 1)
                        pe.matmul(o_ps[0:W, :], v_sb[:], probs[:], start=False, stop=False, skip_group_check=True)
                        pe.matmul(den_ps[0:32, :], ones[:, 0:32], probs[:], start=False, stop=False,
                                  skip_group_check=True).then_inc(s_pv, 1)

                over_units(pe, work)

        @block.vector
        def _(dve):
            taken = dve.value_load(flag, min_val=0, max_val=1)
            with dve.If(taken > 0):

                def masked(step):
                    dve.wait_ge(s_sc, step + 1)
                    dve.tensor_scalar(logits[:], sc_ps[:], scale, None, ALU.mult).then_inc(s_v, 1)
                    if mask is None:
                        dve.wait_ge(s_v, step + 1)
                        return logits
                    dve.tensor_scalar(keep[:], mask_sb[:], 0.0, None, ALU.not_equal).then_inc(s_v, 1)
                    dve.wait_ge(s_v, NV * step + 2)
                    dve.tensor_scalar(penalty[:], keep[:], 1.0, 1e9, ALU.subtract, ALU.mult).then_inc(s_v, 1)
                    dve.tensor_tensor(kept[:], logits[:], keep[:], ALU.mult).then_inc(s_v, 1)
                    dve.wait_ge(s_v, NV * step + 4)
                    dve.tensor_tensor(final[:], kept[:], penalty[:], ALU.add).then_inc(s_v, 1)
                    dve.wait_ge(s_v, NV * step + 5)
                    return final

                def work(b, g, h, f, c):
                    dve.wait_ge(s_zero, 1)
                    dve.wait_ge(s_mbc, c + 1)
                    dve.tensor_scalar(top[:], zero[:], -3e38, None, ALU.add).then_inc(s_top, 1)
                    with dve.Fori(0, KT) as j:
                        tile = masked(2 * KT * c + j)
                        dve.wait_ge(s_top, c + 1)
                        dve.tensor_tensor(top[:], top[:], tile[:], ALU.max).then_inc(s_max, 1)
                        dve.wait_ge(s_max, KT * c + j + 2)
                    with dve.Fori(0, KT) as j:
                        tile = masked(2 * KT * c + KT + j)
                        dve.wait_ge(s_mbc, c + 2)
                        dve.tensor_tensor(below[:], tile[:], top_bc[:], ALU.subtract).then_inc(s_below, 1)

                over_units(dve, work)

        @block.gpsimd
        def _(pool):
            taken = pool.value_load(flag, min_val=0, max_val=1)
            with pool.If(taken > 0):
                pool.memset(zero[:], 0.0).then_inc(s_zero, 1)
                pool.nop().then_inc(s_mbc, 1)
                for c in range(UNITS):
                    pool.wait_ge(s_max, KT * c + KT + 1)
                    pool.partition_all_reduce(top_bc[:], top[:], P, bass.bass_isa.ReduceOp.max).then_inc(s_mbc, 1)

        @block.scalar
        def _(act):
            taken = act.value_load(flag, min_val=0, max_val=1)
            with act.If(taken > 0):
                act.nop().then_inc(s_osb, 1)

                def work(b, g, h, f, c):
                    with act.Fori(0, KT) as j:
                        act.wait_ge(s_below, KT * c + j + 1)
                        act.activation(probs[:], below[:], ACT.Exp).then_inc(s_p, 1)
                    act.wait_ge(s_pv, KT * c + KT + 1)
                    act.wait_ge(s_st, 32 * c + 32)
                    act.activation(o_sb[:], o_ps[0:W, :], ACT.Copy).then_inc(s_osb, 1)
                    act.activation(den_sb[:], den_ps[0:32, :], ACT.Copy).then_inc(s_osb, 1)

                over_units(act, work)


def cross_flag(nc, sem, norm2_q, norm2_k, mask_min, flags):
    with ExitStack() as ctx:
        def sb(name, shape):
            return ctx.enter_context(nc.sbuf_tensor("f_" + name, shape, F32))

        top_q, top_k, prod = (sb(k, [P, B, GROUPS]) for k in ("top_q", "top_k", "prod"))
        low = sb("low", [P, 1])
        worst = sb("worst", [P, 2])
        worst_all = sb("worst_all", [P, 2])
        over = sb("over", [P, 2])
        s_red, s_worst, s_all, s_over, s_flag = sem("f_red"), sem("f_worst"), sem("f_all"), sem("f_over"), sem("f_flag")
        block = ctx.enter_context(nc.Block())

        @block.vector
        def _(dve):
            dve.tensor_reduce(top_q[:], norm2_q[:].rearrange("p b c g -> p b g c"), AX_X, ALU.max).then_inc(s_red, 1)
            dve.tensor_reduce(top_k[:], norm2_k[:].rearrange("p b c g -> p b g c"), AX_X, ALU.max).then_inc(s_red, 1)
            dve.tensor_reduce(low[:], mask_min[:].rearrange("p i n -> p (i n)"), AX_X, ALU.min).then_inc(s_red, 1)
            dve.wait_ge(s_red, 3)
            dve.tensor_tensor(prod[:], top_q[:], top_k[:], ALU.mult).then_inc(s_red, 1)
            dve.tensor_scalar(worst[:, 1:2], low[:], 0.5, None, ALU.is_lt).then_inc(s_worst, 1)
            dve.wait_ge(s_red, 4)
            dve.tensor_reduce(worst[:, 0:1], prod[:].rearrange("p b g -> p (b g)"), AX_X, ALU.max).then_inc(s_worst, 1)
            dve.wait_ge(s_all, 1)
            dve.tensor_scalar(over[:, 0:1], worst_all[:, 0:1], (SAFE * DK ** 0.5) ** 2, None, ALU.is_gt).then_inc(s_over, 1)
            dve.wait_ge(s_over, 1)
            dve.tensor_tensor(over[:, 1:2], over[:, 0:1], worst_all[:, 1:2], ALU.add).then_inc(s_over, 1)
            dve.wait_ge(s_over, 2)
            dve.tensor_scalar(flags[:, 1:2], over[:, 1:2], 0.5, None, ALU.is_gt).then_inc(s_flag, 1)
            dve.wait_ge(s_flag, 1)

        @block.gpsimd
        def _(pool):
            pool.wait_ge(s_worst, 2)
            pool.partition_all_reduce(worst_all[:], worst[:], P, bass.bass_isa.ReduceOp.max).then_inc(s_all, 1)


def context_projections(nc, sem, ctxT, mask, xwkvT, k2_dram, v2_dram, ones_block, norm2_k, mask_min,
                        sum_dram, rsum_dram, ahead_dram, ahead):
    CH = L // HALF
    with ExitStack() as ctx:
        def sb(name, shape, dt=F32):
            return ctx.enter_context(nc.sbuf_tensor(name, shape, dt))

        w_raw = sb("c_wraw", [P, 2, DC, D])
        w_hi = sb("c_whi", [P, 2, DC, D], F32R)
        w_lo = sb("c_wlo", [P, 2, DC, D], F32R)
        c_raw = [sb(f"c_raw{i}", [P, DC, HALF]) for i in range(2)]
        c_hi = [sb(f"c_hi{i}", [P, DC, HALF], F32R) for i in range(2)]
        c_lo = [sb(f"c_lo{i}", [P, DC, HALF], F32R) for i in range(2)]
        k_hi = sb("c_khi", [P, GROUPS, HALF], F32R)
        k_lo = sb("c_klo", [P, GROUPS, HALF], F32R)
        v_sb = sb("c_v", [P, 4, D])
        k_sq = sb("c_ksq", [P, 2, HALF], F32R)
        CHUNKS = B * CH
        MP = mask_min.shape[1]
        mask_rows = mask.rearrange("b l t -> (b l t)").rearrange("(n i p v) -> i n p v", n=CHUNKS, i=MP, p=P)
        mask_sb = [sb(f"c_mask{i}", [P, B * L * N // (MP * CHUNKS * P)], mybir.dt.int32) for i in range(2)]
        den = sb("c_den", [P, SUMS])
        rden = sb("c_rden", [P, SUMS])
        SHARE = (EC + DC) // CH
        ahead_raw = sb("c_ahead", [P, SHARE, D])
        ahead_rows = ahead_dram.rearrange("(n c q) e -> n q c e", q=P, c=SHARE)
        ps = [ctx.enter_context(nc.psum_tensor(f"c_ps{i}", [P, HALF], F32)) for i in range(8)]

        s_w = [sem(f"c_w{i}") for i in range(2)]
        s_whi, s_wlo = sem("c_whi"), sem("c_wlo")
        s_raw = [sem(f"c_raw{i}") for i in range(2)]
        s_hi, s_lo = sem("c_hi"), sem("c_lo")
        s_mm = sem("c_mm")
        s_khi, s_klo, s_v = sem("c_khi"), sem("c_klo"), sem("c_v")
        s_kst, s_vst = sem("c_kst"), sem("c_vst")
        s_ksq = sem("c_ksq")
        s_norm, s_top = sem("c_norm"), sem("c_top")
        s_mask = [sem(f"c_mask{i}") for i in range(2)]
        s_min = sem("c_min")
        s_den, s_rden, s_rst = sem("c_den"), sem("c_rden"), sem("c_rst")
        s_ahead, s_ahi, s_alo = sem("c_ahead"), sem("c_ahi"), sem("c_alo")
        block = ctx.enter_context(nc.Block())


        @block.sync
        def _(sp):
            sp.nop().then_inc(s_kst, 128)
            sp.nop().then_inc(s_vst, 64)
            for i in range(2):
                sp.dma_start(w_raw[:, i], xwkvT[i].rearrange("(c q) e -> q c e", q=P)).then_inc(s_w[i], 16)
                sp.dma_start(c_raw[i][:], ctxT[i, 0].rearrange("(c q) t -> q c t", q=P)).then_inc(s_raw[i], 16)
            for i in range(2):
                sp.dma_start(mask_sb[i][:], mask_rows[i, 0]).then_inc(s_mask[i], 16)
            sp.dma_start(den[:], by_partition(sum_dram)).then_inc(s_den, 16)
            sp.wait_ge(s_rden, 1)
            sp.dma_start(by_partition(rsum_dram), rden[:]).then_inc(s_rst, 16)
            with sp.Fori(0, CH) as jc:
                for b in range(B):
                    n = B * jc + b
                    sp.wait_ge(s_hi, n + 1)
                    sp.wait_ge(s_lo, n + 1)
                    sp.dma_start(c_raw[b][:], ctxT[b, (jc + 1) % CH].rearrange("(c q) t -> q c t", q=P))\
                        .then_inc(s_raw[b], 16)
                    if b == 0:
                        sp.wait_ge(s_alo, jc + 1)
                        sp.dma_start(ahead_raw[:], ahead_rows[jc]).then_inc(s_ahead, 16)
                    sp.wait_ge(s_klo, GROUPS * n + GROUPS)
                    for g in range(GROUPS):
                        for i, part in enumerate((k_hi, k_lo)):
                            sp.dma_start(k2_dram[GROUPS * b + g, :, i, :, bass.ds(jc * HALF, HALF)],
                                         words(part[:, g, :])).then_inc(s_kst, 16)
                    for i in range(MP):
                        sp.wait_ge(s_min, MP * n + i + 1)
                        at = B * jc + b if i + 2 < MP else B * jc + 1 if b == 0 else B * ((jc + 1) % CH)
                        sp.dma_start(mask_sb[i % 2][:], mask_rows[(i + 2) % MP, at]).then_inc(s_mask[i % 2], 16)
                    sp.wait_ge(s_v, 4 * n + 8)
                    for t in range(4):
                        sp.dma_start(v2_dram[GROUPS * b:GROUPS * (b + 1)].rearrange("g q t e -> t q g e")[4 * jc + t],
                                     v_sb[:, t, :].rearrange("p (g e) -> p g e", e=P)).then_inc(s_vst, 16)
            sp.wait_ge(s_kst, 128 + 128 * B * CH)
            sp.wait_ge(s_vst, 64 + 64 * B * CH)
            for b in range(B):
                sp.wait_ge(s_raw[b], 16 * (CH + 1))
            for i in range(2):
                sp.wait_ge(s_mask[i], 16 * (MP // 2 * CHUNKS + 1))
            sp.wait_ge(s_rst, 16)

        @block.scalar
        def _(act):
            act.nop().then_inc(s_v, 4)
            act.nop().then_inc(s_top, GROUPS)
            act.nop().then_inc(s_norm, GROUPS)
            for i in range(2):
                act.wait_ge(s_w[i], 16)
                act.activation(w_hi[:, i], w_raw[:, i], ACT.Copy).then_inc(s_whi, 1)
                if i == 0:
                    act.wait_ge(s_raw[0], 16)
                    act.activation(c_hi[0][:], c_raw[0][:], ACT.Copy).then_inc(s_hi, 1)
            with act.Fori(0, CH) as jc:
                for b in range(B):
                    n = B * jc + b
                    act.wait_ge(s_raw[1 - b], 16 * jc + 16 + 16 * b)
                    act.wait_ge(s_mm, 8 * n + 16)
                    act.activation(c_hi[1 - b][:], c_raw[1 - b][:], ACT.Copy).then_inc(s_hi, 1)
                    act.wait_ge(s_kst, 128 * n + 128)
                    for g in range(GROUPS):
                        act.wait_ge(s_mm, 8 * n + g + 17)
                        act.activation(k_hi[:, g, :], ps[g][:], ACT.Copy).then_inc(s_khi, 1)
                    for g in range(GROUPS):
                        act.wait_ge(s_norm, GROUPS * n + g - 1 + GROUPS)
                        act.wait_ge(s_khi, GROUPS * n + g + 1)
                        act.activation(k_sq[:, g % 2, :], words(k_hi[:, g, :]), ACT.Square).then_inc(s_ksq, 1)
                    act.wait_ge(s_vst, 64 * n + 64)
                    for t in range(4):
                        act.wait_ge(s_mm, 8 * n + 4 + t + 17)
                        act.activation(v_sb[:, t, :], ps[4 + t][:], ACT.Copy).then_inc(s_v, 1)
                    if b == 0:
                        act.wait_ge(s_ahead, 16 * jc + 16)
                        act.activation(ahead[0][:, bass.ds(SHARE * jc, SHARE), :], ahead_raw[:], ACT.Copy).then_inc(s_ahi, 1)

        @block.vector
        def _(dve):
            dve.nop().then_inc(s_alo, 1)
            for i in range(2):
                dve.wait_ge(s_whi, i + 1)
                dve.tensor_tensor(w_lo[:, i], w_raw[:, i], w_hi[:, i].bitcast(F32), ALU.subtract).then_inc(s_wlo, 1)
                if i == 0:
                    dve.wait_ge(s_hi, 1)
                    dve.tensor_tensor(c_lo[0][:], c_raw[0][:], c_hi[0][:].bitcast(F32), ALU.subtract).then_inc(s_lo, 1)
            dve.wait_ge(s_den, 16)
            dve.reciprocal(rden[:], den[:]).then_inc(s_rden, 1)
            with dve.Fori(0, CH) as jc:
                for b in range(B):
                    n = B * jc + b
                    dve.wait_ge(s_hi, n + 2)
                    dve.tensor_tensor(c_lo[1 - b][:], c_raw[1 - b][:], c_hi[1 - b][:].bitcast(F32),
                                      ALU.subtract).then_inc(s_lo, 1)
                    dve.wait_ge(s_kst, 128 * n + 128)
                    for g in range(GROUPS):
                        dve.wait_ge(s_khi, GROUPS * n + g + 1)
                        dve.tensor_tensor(k_lo[:, g, :], ps[g][:], k_hi[:, g, :].bitcast(F32),
                                          ALU.subtract).then_inc(s_klo, 1)
                    for i in range(MP):
                        dve.wait_ge(s_mask[i % 2], 8 * MP * n + 16 * (i // 2) + 16)
                        dve.tensor_reduce(mask_min[:, i, bass.ds(n, 1)], mask_sb[i % 2][:].bitcast(mybir.dt.uint32), AX_X,
                                          ALU.min).then_inc(s_min, 1)
                    for g in range(GROUPS):
                        dve.wait_ge(s_norm, GROUPS * n + g + 1 + GROUPS)
                        dve.tensor_reduce(norm2_k[:, b, bass.ds(jc, 1), g], ps[g][:], AX_X, ALU.max).then_inc(s_top, 1)
                    if b == 0:
                        dve.wait_ge(s_ahi, jc + 1)
                        dve.tensor_tensor(ahead[1][:, bass.ds(SHARE * jc, SHARE), :], ahead_raw[:],
                                          words(ahead[0][:, bass.ds(SHARE * jc, SHARE), :]), ALU.subtract).then_inc(s_alo, 1)

        @block.tensor
        def _(pe):
            pe.nop().then_inc(s_mm, 16)
            pe.wait_ge(s_whi, 1)
            pe.wait_ge(s_wlo, 1)
            with pe.Fori(0, CH) as jc:
                for b in range(B):
                    n = B * jc + b
                    pe.wait_ge(s_hi, n + 1)
                    pe.wait_ge(s_lo, n + 1)
                    for g in range(GROUPS):
                        pe.wait_ge(s_top, GROUPS * n + g + 1)
                        e = slice(g * P, (g + 1) * P)
                        for c in range(DC):
                            pe.matmul(ps[g][:], w_hi[:, 0, c, e], c_hi[b][:, c, :], start=(c == 0), stop=False)
                            pe.matmul(ps[g][:], w_hi[:, 0, c, e], c_lo[b][:, c, :], start=False, stop=False)
                            last = pe.matmul(ps[g][:], w_lo[:, 0, c, e], c_hi[b][:, c, :], start=False, stop=(c == DC - 1))
                        last.then_inc(s_mm, 1)
                    pe.wait_ge(s_wlo, 2)
                    for t in range(4):
                        pe.wait_ge(s_v, 4 * n + t + 1)
                        tok = slice(t * P, (t + 1) * P)
                        for c in range(DC):
                            pe.matmul(ps[4 + t][:], c_hi[b][:, c, tok], w_hi[:, 1, c, :], start=(c == 0), stop=False)
                            pe.matmul(ps[4 + t][:], c_hi[b][:, c, tok], w_lo[:, 1, c, :], start=False, stop=False)
                            last = pe.matmul(ps[4 + t][:], c_lo[b][:, c, tok], w_hi[:, 1, c, :], start=False,
                                             stop=(c == DC - 1))
                        last.then_inc(s_mm, 1)
                        if t == 1:
                            pe.wait_ge(s_klo, GROUPS * n + GROUPS)
                            for g in range(GROUPS):
                                pe.wait_ge(s_ksq, GROUPS * n + g + 1)
                                pe.matmul(ps[g][:], ones_block[:], k_sq[:, g % 2, :], start=True, stop=True).then_inc(s_norm, 1)


def cross_attention(nc, sem, q2_dram, k2_dram, v2_dram, attn2T_dram, sum2_dram, ones):
    with ExitStack() as ctx:
        def sb(name, shape, dt=F32):
            return ctx.enter_context(nc.sbuf_tensor(name, shape, dt))

        k_st = [[sb(f"d_k{i}{h}", [P, L], F32R) for h in range(4)] for i in range(2)]
        q_st = [[sb(f"d_q{i}{h}", [P, N], F32R) for h in range(4)] for i in range(2)]
        v_sb = [sb(f"d_v{i}", [P, JT, P]) for i in range(2)]
        NP = 4
        probs = [sb(f"d_p{i}", [P, 4 * HALF]) for i in range(NP)]
        acc = [sb(f"d_acc{f}", [P, 4 * HALF]) for f in range(NH)]
        o_sb = [sb(f"d_o{f}", [P, HALF]) for f in range(NH)]
        den_sb = [sb(f"d_den{f}", [P, HALF]) for f in range(NH)]
        sc_ps = [ctx.enter_context(nc.psum_tensor(f"d_sc{i}", [P, 2 * HALF], F32)) for i in range(2)]
        o_ps = [ctx.enter_context(nc.psum_tensor(f"d_ops{f}", [P, HALF], F32)) for f in range(NH)]
        den_ps = [ctx.enter_context(nc.psum_tensor(f"d_dps{f}", [P, HALF], F32)) for f in range(NH)]

        s_in = [[sem(f"d_in{i}{k}") for k in range(3)] for i in range(2)]
        s_sc, s_pr, s_pv = sem("d_sc"), sem("d_pr"), sem("d_pv")
        s_acc, s_den = sem("d_acc"), sem("d_den")
        s_osb, s_dsb = sem("d_osb"), sem("d_dsb")
        s_ost, s_dst = ([sem(f"d_{k}{f}") for f in range(NH)] for k in ("ost", "dst"))
        block = ctx.enter_context(nc.Block())

        ITS, STEPS = B * GROUPS, NH * JT
        LOADS = 16 * 2 * 3
        ADDS = 2 * (JT - 1)

        def head_on_pe(j):
            return j % 4 if j >= 2 else None

        def added(it, f, j, pair):
            return 2 * NP + NH * ADDS * it + ADDS * f + 2 * (max(j, 1) - 1) + pair + 1

        @block.sync
        def _(sp):
            for f in range(NH):
                sp.nop().then_inc(s_ost[f], 16)
                sp.nop().then_inc(s_dst[f], 16)

            def load(it, par):
                for h in range(4):
                    for i in range(2):
                        sp.dma_start(words(k_st[par][h][64 * i:64 * i + 64, :]),
                                     k2_dram[it, h, i].unsqueeze(0).to_broadcast([2, DK, L])).then_inc(s_in[par][h // 2], 16)
                    sp.dma_start(words(q_st[par][h][:]), q2_dram[it, h].rearrange("s q t -> (s q) t").unsqueeze(0)
                                 .to_broadcast([2, 2 * DK, N])).then_inc(s_in[par][h // 2], 16)
                sp.dma_start(v_sb[par][:], v2_dram[it]).then_inc(s_in[par][2], 16)

            def store(it, f):
                sp.wait_ge(s_osb, NH * it + f + 3)
                sp.dma_start(attn2T_dram.rearrange("b g q t -> (b g) q t")[it, :, f * HALF:(f + 1) * HALF],
                             o_sb[f][:]).then_inc(s_ost[f], 16)
                sp.wait_ge(s_dsb, NH * it + f + 3)
                sp.dma_start(sum2_dram.rearrange("b g h t -> (b g) h t")[it, :, f * HALF:(f + 1) * HALF],
                             den_sb[f][0:P:32, :]).then_inc(s_dst[f], 16)

            def body(i, last):
                for par in range(2):
                    it = 2 * i + par
                    store(it, 0)
                    store(it, 1)
                    if not last:
                        load(it + 2, par)

            load(0, 0)
            load(1, 1)
            with sp.Fori(0, ITS // 2 - 1) as i:
                body(i, False)
            body(ITS // 2 - 1, True)
            for f in range(NH):
                sp.wait_ge(s_ost[f], 16 + 16 * ITS)
                sp.wait_ge(s_dst[f], 16 + 16 * ITS)

        @block.tensor
        def _(pe):
            pe.nop().then_inc(s_pv, NP)

            def scores(it, par, s, nth=None, first=False):
                f, j = divmod(s, JT)
                for pair in range(2):
                    if s == 0:
                        pe.wait_ge(s_in[par][pair], LOADS * nth)
                    if not first:
                        pe.wait_ge(s_pr, 2 * STEPS * it + 2 * s + pair - 1)
                    for h in range(2):
                        last = pe.matmul(sc_ps[pair][:, h * HALF:(h + 1) * HALF],
                                         k_st[par][2 * pair + h][:, j * P:(j + 1) * P],
                                         q_st[par][2 * pair + h][:, f * HALF:(f + 1) * HALF], start=True, stop=True)
                    last.then_inc(s_sc, 1)

            def values(it, par, s, nth):
                f, j = divmod(s, JT)
                if s == 0:
                    pe.wait_ge(s_in[par][2], 16 * nth)
                pe.wait_ge(s_pr, 2 * STEPS * it + 2 * s + 2)
                if j == 0:
                    pe.wait_ge(s_osb, NH * it + f + 1)
                for h in range(4):
                    last = pe.matmul(o_ps[f][32 * h:32 * h + 32, :], v_sb[par][:, j, 32 * h:32 * h + 32],
                                     probs[s % NP][:, h * HALF:(h + 1) * HALF],
                                     start=(j == 0), stop=(j == JT - 1), skip_group_check=True)
                h = head_on_pe(j)
                if h is not None:
                    if j == 2:
                        pe.wait_ge(s_dsb, NH * it + f + 1)
                    last = pe.matmul(den_ps[f][32 * h:32 * h + 32, :], ones[:], probs[s % NP][:, h * HALF:(h + 1) * HALF],
                                     start=(j < 6), stop=False, skip_group_check=True)
                last.then_inc(s_pv, 1)

            def sums(it, f):
                pe.wait_ge(s_acc, added(it, f, JT - 1, 1))
                for h in range(4):
                    last = pe.matmul(den_ps[f][32 * h:32 * h + 32, :], ones[:], acc[f][:, h * HALF:(h + 1) * HALF],
                                     start=False, stop=True, skip_group_check=True)
                last.then_inc(s_den, 1)

            def body(i, last):
                for par in range(2):
                    it = 2 * i + par
                    for s in range(1, STEPS):
                        scores(it, par, s)
                        values(it, par, s - 1, i + 1)
                        if s == JT + 1:
                            sums(it, 0)
                    if not (last and par == 1):
                        scores(it + 1, 1 - par, 0, nth=i + 1 + par)
                    values(it, par, STEPS - 1, i + 1)
                    sums(it, 1)

            scores(0, 0, 0, nth=1, first=True)
            with pe.Fori(0, ITS // 2 - 1) as i:
                body(i, False)
            body(ITS // 2 - 1, True)

        @block.scalar
        def _(act):
            act.nop().then_inc(s_osb, 2)
            act.nop().then_inc(s_dsb, 2)

            def exps(it, s):
                f, j = divmod(s, JT)
                for pair in range(2):
                    act.wait_ge(s_sc, 2 * STEPS * it + 2 * s + pair + 1)
                    act.wait_ge(s_pv, STEPS * it + s + 1)
                    if s >= NP:
                        act.wait_ge(s_acc, added(it, *divmod(s - NP, JT), pair))
                    else:
                        act.wait_ge(s_acc, added(it - 1, NH - 1, JT + s - NP, pair))
                    act.activation(probs[s % NP][:, pair * 2 * HALF:(pair + 1) * 2 * HALF], sc_ps[pair][:],
                                   ACT.Exp, scale=DK ** -0.5).then_inc(s_pr, 1)

            def collect(it, f):
                act.wait_ge(s_pv, STEPS * it + JT * (f + 1) + NP)
                act.wait_ge(s_ost[f], 16 * (it + 1))
                act.activation(o_sb[f][:], o_ps[f][:], ACT.Copy).then_inc(s_osb, 1)

            def collect_sums(it, f):
                act.wait_ge(s_den, NH * it + f + 1)
                act.wait_ge(s_dst[f], 16 * (it + 1))
                act.activation(den_sb[f][:], den_ps[f][:], ACT.Copy).then_inc(s_dsb, 1)

            def body(i, last):
                for par in range(2):
                    it = 2 * i + par
                    for s in range(1, STEPS):
                        exps(it, s)
                        if s == JT:
                            collect(it, 0)
                        if s == JT + 1:
                            collect_sums(it, 0)
                    if not (last and par == 1):
                        exps(it + 1, 0)
                    collect(it, 1)
                    collect_sums(it, 1)

            exps(0, 0)
            with act.Fori(0, ITS // 2 - 1) as i:
                body(i, False)
            body(ITS // 2 - 1, True)

        @block.vector
        def _(dve):
            dve.nop().then_inc(s_acc, 2 * NP)

            def add(it, f, j):
                s = JT * f + j
                for pair in range(2):
                    heads = [h for h in (2 * pair, 2 * pair + 1) if h != head_on_pe(j)]
                    cols = slice(heads[0] * HALF, (heads[-1] + 1) * HALF)
                    dve.wait_ge(s_pr, 2 * STEPS * it + 2 * s + pair + 1)
                    if j == 1:
                        dve.wait_ge(s_dsb, NH * it + f + 1)
                        dve.tensor_tensor(acc[f][:, cols], probs[(s - 1) % NP][:, cols], probs[s % NP][:, cols],
                                          ALU.add).then_inc(s_acc, 1)
                    else:
                        dve.wait_ge(s_acc, added(it, f, j - 1, pair))
                        dve.tensor_tensor(acc[f][:, cols], acc[f][:, cols], probs[s % NP][:, cols],
                                          ALU.add).then_inc(s_acc, 1)

            with dve.Fori(0, ITS) as it:
                for f in range(NH):
                    for j in range(1, JT):
                        add(it, f, j)


def output_projection(nc, sem, tag, attn_dram, sum_dram, rsum_dram, w, bias, res_dram, keep_dram, ident, query=None, ffn=None):
    C, HP = rsum_dram.shape[1], rsum_dram.shape[2]
    W = P // HP
    CH = N // HALF
    CHUNKS = B * CH
    TC = HALF // P
    NY = 1 if ffn is None else 3
    with ExitStack() as ctx:
        def sb(name, shape, dt=F32):
            return ctx.enter_context(nc.sbuf_tensor(tag + name, shape, dt))

        w_hi, w_lo = w
        o_raw = sb("oraw", [P, C, HALF])
        r_bc = sb("rbc", [P, C, HALF])
        o_hi = sb("ohi", [P, C, HALF], F32R)
        o_lo = sb("olo", [P, C, HALF], F32R)
        res = sb("res", [P, TC, D])
        y = sb("y", [P, NY, TC, D])
        xn = sb("xn", [P, TC, D])
        stats = sb("stats", [P, TC, 6])
        mv = sb("mv", [P, TC, 2])
        var = sb("var", [P, TC])
        rstd = sb("rstd", [P, TC])
        mhalf = sb("mhalf", [P, TC])
        xT_hi = sb("xThi", [P, DC, HALF], F32R)
        xT_lo = sb("xTlo", [P, DC, HALF], F32R)
        o_ps = [ctx.enter_context(nc.psum_tensor(f"{tag}o_ps{i}", [P, HALF], F32)) for i in range(TC)]
        t_ps = [ctx.enter_context(nc.psum_tensor(f"{tag}t_ps{i}", [P, HALF], F32)) for i in range(2)]
        z_ps = [ctx.enter_context(nc.psum_tensor(f"{tag}z_ps{i}", [P, HALF], F32)) for i in range(2)]
        if sum_dram is not None:
            den = sb("den", [P, SUMS])
            rden = sb("rden", [P, SUMS])
        if bias is not None:
            bias_bc = sb("bias", [P, D])
        if query is not None:
            (wq_hi, wq_lo), q2_dram, ones_block, norm2_q, ahead_dram, ahead = query
            ahead_raw = sb("ahead", [P, DC, D])
            q_hi = sb("qhi", [P, GROUPS, HALF], F32R)
            q_lo = sb("qlo", [P, GROUPS, HALF], F32R)
            q_sq = sb("qsq", [P, 2, HALF], F32R)
        else:
            win, bin_, w1, b1, w2, b2, wout, bout, out = ffn
            HH = HID // 2
            wi_raw = sb("wiraw", [P, DC, P])
            wi_hi = sb("wihi", [P, DC, P], F32R)
            wi_lo = sb("wilo", [P, DC, P], F32R)
            small = sb("small", [P, 3 * HH])
            bin_sb = sb("binsb", [P, 1])
            b2_sb = sb("b2sb", [P, 1])
            wo2 = sb("wo2", [P, D])
            bout_bc = sb("bout", [P, D])
            s_sb = sb("ssb", [P, HALF])
            relu = sb("relu", [P, 2, HALF])
            g_sb = sb("gsb", [P, 2, HALF])
            fin = sb("fin", [P, 2, D])

        def s(name):
            return sem(tag + "_" + name)

        s_den, s_rden, s_rst = s("den"), s("rden"), s("rst")
        s_bias, s_mhalf = s("bias"), s("mhalf")
        s_o = [s(f"o{i}") for i in range(2)]
        s_rb = [s(f"rb{i}") for i in range(2)]
        s_res = s("res")
        s_resb = s("resb")
        s_div, s_hi, s_lo = s("div"), s("hi"), s("lo")
        s_mm = s("mm")
        s_y, s_yst = s("y"), s("yst")
        s_st, s_ag, s_var, s_rstd = s("st"), s("ag"), s("var"), s("rstd")
        s_xn, s_tr, s_thi, s_tlo = s("xn"), s("tr"), s("thi"), s("tlo")
        s_z = s("z")
        if query is not None:
            s_qhi, s_qlo, s_qst = s("qhi"), s("qlo"), s("qst")
            s_ahead, s_ahi = s("ahead"), s("ahi")
            s_qsq, s_norm, s_top = s("qsq"), s("norm"), s("top")
        else:
            s_small, s_wi, s_b2z = s("small"), s("wi"), s("b2z")
            s_s, s_relu, s_g = s("s"), s("relu"), s("g")
            s_f, s_yb, s_fin, s_fst = s("f"), s("yb"), s("fin"), [s("fst0"), s("fst1")]
            SMALL = 16 * (2 * 6 + 2)
        block = ctx.enter_context(nc.Block())

        def part(k):
            return slice(k * HALF // 2, (k + 1) * HALF // 2)

        def tokens(dram, n):
            return dram[n // CH].rearrange("(c t q) d -> c q t d", q=P, t=TC)[n % CH]

        @block.sync
        def _(sp):
            def load_sums(n, k):
                for h in range(HP):
                    sp.dma_start(r_bc[h * W:(h + 1) * W, :, part(k)],
                                 rsum_dram[n // CH].rearrange("c h t -> h c t")[h]
                                 .rearrange("c (n t) -> c n t", n=2 * CH)[:, n % CH * 2 + k, :]
                                 .unsqueeze(0).to_broadcast([W, C, HALF // 2])).then_inc(s_rb[k], 16)

            def load_outputs(n, k):
                sp.dma_start(o_raw[:, :, part(k)], attn_dram[n // CH].rearrange("c q t -> q c t")
                             .rearrange("q c (n t) -> q c n t", n=2 * CH)[:, :, n % CH * 2 + k, :]).then_inc(s_o[k], 16)

            def store_queries(n):
                sp.wait_ge(s_qlo, GROUPS * (n + 1))
                for i, part in enumerate((q_hi, q_lo)):
                    for g in range(GROUPS):
                        sp.dma_start(q2_dram.rearrange("(b g) h s q t -> b g h s q t", g=GROUPS)
                                     [n // CH, g, :, i, :, n % CH * HALF:(n % CH + 1) * HALF],
                                     words(part[:, g, :])).then_inc(s_qst, 16)

            def store_result(n):
                for t in range(TC):
                    sp.wait_ge(s_fin, TC * n + t + 1)
                    sp.dma_start(tokens(out, n)[:, t, :], fin[:, t % 2, :]).then_inc(s_fst[t % 2], 16)

            if sum_dram is not None:
                sp.dma_start(den[:], by_partition(sum_dram)).then_inc(s_den, 16)
            load_outputs(0, 0)
            if sum_dram is not None:
                sp.wait_ge(s_rden, 1)
                sp.dma_start(by_partition(rsum_dram), rden[:]).then_inc(s_rst, 16)
                load_outputs(0, 1)
                sp.dma_start(res[:], tokens(res_dram, 0)).then_inc(s_res, 16)
                sp.wait_ge(s_rst, 16)
                load_sums(0, 0)
                load_sums(0, 1)
            else:
                load_sums(0, 0)
                load_outputs(0, 1)
                load_sums(0, 1)
                sp.dma_start(res[:], tokens(res_dram, 0)).then_inc(s_res, 16)
            if bias is not None:
                sp.dma_start(bias_bc[:], bias.partition_broadcast(P)).then_inc(s_bias, 16)
            if query is not None:
                sp.dma_start(ahead_raw[:], ahead_dram.rearrange("(c q) e -> q c e", q=P)).then_inc(s_ahead, 16)
            if ffn is not None:
                for i in range(2):
                    sp.dma_start(wi_raw[:, :, i * M:(i + 1) * M], win.rearrange("(c q) m -> q c m", q=P))\
                        .then_inc(s_small, 16)
                    rows = slice(i * M, (i + 1) * M)
                    for k, a in enumerate((w1, b1, w2)):
                        sp.dma_start(small[rows, k * HH:(k + 1) * HH], a[:, i * HH:(i + 1) * HH]).then_inc(s_small, 16)
                    sp.dma_start(bin_sb[rows, :], bin_.unsqueeze(1)).then_inc(s_small, 16)
                    sp.dma_start(wo2[rows, :], wout).then_inc(s_small, 16)
                sp.wait_ge(s_b2z, 1)
                sp.dma_start(b2_sb[0:M, :], b2.unsqueeze(1)).then_inc(s_small, 16)
                sp.dma_start(bout_bc[:], bout.partition_broadcast(P)).then_inc(s_small, 16)
            for n in range(CHUNKS + 2):
                if n + 1 < CHUNKS:
                    for k in range(2):
                        sp.wait_ge(s_div, 2 * n + k + 1)
                        load_sums(n + 1, k)
                        sp.wait_ge(s_lo, 2 * n + k + 1)
                        load_outputs(n + 1, k)
                if n < CHUNKS:
                    sp.wait_ge(s_y, TC * (n + 1))
                    if n + 1 < CHUNKS:
                        sp.dma_start(res[:], tokens(res_dram, n + 1)).then_inc(s_res, 16)
                    if keep_dram is not None:
                        sp.dma_start(tokens(keep_dram, n), y[:, 0]).then_inc(s_yst, 16)
                if query is not None and 1 <= n <= CHUNKS:
                    store_queries(n - 1)
                if ffn is not None and n >= 2:
                    store_result(n - 2)
            if keep_dram is not None:
                sp.wait_ge(s_yst, 16 * CHUNKS)
            if query is not None:
                sp.wait_ge(s_qst, 16 * 2 * GROUPS * CHUNKS)
            else:
                for i in range(2):
                    sp.wait_ge(s_fst[i], 8 * TC * CHUNKS)

        @block.gpsimd
        def _(pool):
            pool.memset(mhalf[:], -0.5).then_inc(s_mhalf, 1)
            pool.wait_ge(s_mhalf, 1)
            if ffn is not None:
                pool.memset(b2_sb[:], 0.0).then_inc(s_b2z, 1)
                pool.wait_ge(s_b2z, 1)
            for n in range(CHUNKS):
                if bias is not None:
                    pool.wait_ge(s_bias, 16)
                    pool.wait_ge(s_res, 16 * (n + 1))
                    pool.tensor_tensor(res[:], res[:], bias_bc[:].unsqueeze(1).to_broadcast([P, TC, D]), ALU.add)\
                        .then_inc(s_resb, 1)
                    pool.wait_ge(s_resb, n + 1)
                pool.wait_ge(s_var, n + 1)
                pool.tensor_tensor(rstd[:], var[:], mhalf[:], ALU.pow).then_inc(s_rstd, 1)
                if ffn is not None:
                    pool.wait_ge(s_small, SMALL)
                    pool.wait_ge(s_rstd, n + 1)
                    pool.wait_ge(s_xn, TC * (n + 1))
                    pool.tensor_tensor(y[:, n % NY], y[:, n % NY], bout_bc[:].unsqueeze(1).to_broadcast([P, TC, D]),
                                       ALU.add).then_inc(s_yb, 1)
                    pool.wait_ge(s_yb, n + 1)

        @block.vector
        def _(dve):
            def divide(n, k):
                dve.wait_ge(s_o[k], 16 * (n + 1))
                dve.wait_ge(s_rb[k], 16 * HP * (n + 1))
                dve.tensor_tensor(o_raw[:, :, part(k)], o_raw[:, :, part(k)], r_bc[:, :, part(k)], ALU.mult)\
                    .then_inc(s_div, 1)

            def low(n, k):
                dve.wait_ge(s_hi, 2 * n + k + 1)
                dve.tensor_tensor(o_lo[:, :, part(k)], o_raw[:, :, part(k)], words(o_hi[:, :, part(k)]), ALU.subtract)\
                    .then_inc(s_lo, 1)

            def residual(n, t):
                if t == 0:
                    if bias is not None:
                        dve.wait_ge(s_resb, n + 1)
                    else:
                        dve.wait_ge(s_res, 16 * (n + 1))
                    if keep_dram is not None and n >= 1:
                        dve.wait_ge(s_yst, 16 * n)
                    if n >= 1:
                        dve.wait_ge(s_xn, TC * n)
                    if ffn is not None and n >= NY:
                        dve.wait_ge(s_fin, TC * (n - NY + 1))
                dve.wait_ge(s_mm, TC * n + t + 1)
                dve.tensor_tensor(y[:, n % NY, t, :], o_ps[t][:], res[:, t, :], ALU.add).then_inc(s_y, 1)
                dve.wait_ge(s_y, TC * n + t + 1)
                dve.bn_stats(stats[:, t, :], y[:, n % NY, t, :]).then_inc(s_st, 1)
                dve.wait_ge(s_st, TC * n + t + 1)
                dve.bn_aggr(mv[:, t, :], stats[:, t, :]).then_inc(s_ag, 1)

            def variance(n):
                dve.wait_ge(s_ag, TC * (n + 1))
                dve.tensor_scalar(var[:], mv[:, :, 1], LN_EPS, None, ALU.add).then_inc(s_var, 1)

            def normalise(n):
                dve.wait_ge(s_rstd, n + 1)
                if n >= 1:
                    dve.wait_ge(s_tr, TC * n)
                for t in range(TC):
                    dve.tensor_scalar(xn[:, t, :], y[:, n % NY, t, :], mv[:, t, 0:1], rstd[:, t:t + 1],
                                      ALU.subtract, ALU.mult).then_inc(s_xn, 1)

            def low_transposed(n):
                for t in range(TC):
                    dve.wait_ge(s_thi, TC * n + t + 1)
                    cols = slice(t * P, (t + 1) * P)
                    dve.tensor_tensor(xT_lo[:, :, cols], t_ps[t % 2][:].rearrange("p (c t) -> p c t", c=DC),
                                      xT_hi[:, :, cols].bitcast(F32), ALU.subtract).then_inc(s_tlo, 1)

            def low_queries(n, g):
                if g == 0 and n >= 1:
                    dve.wait_ge(s_qst, 16 * 2 * GROUPS * n)
                dve.wait_ge(s_qhi, GROUPS * n + g + 1)
                dve.tensor_tensor(q_lo[:, g, :], z_ps[g % 2][:], q_hi[:, g, :].bitcast(F32),
                                  ALU.subtract).then_inc(s_qlo, 1)

            def top_norm(n, g):
                dve.wait_ge(s_norm, GROUPS * n + g + 1)
                dve.tensor_reduce(norm2_q[:, n // CH, n % CH, g:g + 1], t_ps[g % 2][:], AX_X, ALU.max).then_inc(s_top, 1)

            def units_in(n):
                dve.wait_ge(s_small, SMALL)
                dve.wait_ge(s_z, n + 1)
                if n >= 1:
                    dve.wait_ge(s_relu, HH * n)
                dve.tensor_scalar(s_sb[:], z_ps[0][:], bin_sb[:, 0:1], None, ALU.add).then_inc(s_s, 1)

            def units_out(n):
                if n >= 2:
                    dve.wait_ge(s_f, TC * (n - 1))
                g = g_sb[:, n % 2, :]
                for j in range(HH):
                    dve.wait_ge(s_relu, HH * n + j + 1)
                    if j == 0:
                        dve.tensor_scalar(g, relu[:, 0, :], small[:, 2 * HH:2 * HH + 1], b2_sb[:, 0:1],
                                          ALU.mult, ALU.add).then_inc(s_g, 1)
                    else:
                        dve.wait_ge(s_g, HH * n + j)
                        dve.scalar_tensor_tensor(out=g, in0=relu[:, j % 2, :],
                                                 scalar=small[:, 2 * HH + j:2 * HH + j + 1], in1=g,
                                                 op0=ALU.mult, op1=ALU.add).then_inc(s_g, 1)

            def result(n):
                dve.wait_ge(s_yb, n + 1)
                for t in range(TC):
                    dve.wait_ge(s_f, TC * n + t + 1)
                    stores = n * TC // 2 + t // 2
                    if stores:
                        dve.wait_ge(s_fst[t % 2], 16 * stores)
                    dve.tensor_tensor(fin[:, t % 2, :], z_ps[(t + 1) % 2][:], y[:, n % NY, t, :], ALU.add)\
                        .then_inc(s_fin, 1)

            if sum_dram is not None:
                dve.wait_ge(s_den, 16)
                dve.reciprocal(rden[:], den[:]).then_inc(s_rden, 1)
            divide(0, 0)
            divide(0, 1)
            low(0, 0)
            low(0, 1)
            if query is not None:
                dve.wait_ge(s_ahi, 1)
                dve.tensor_tensor(ahead[1][:], ahead_raw[:], words(ahead[0][:]), ALU.subtract)
            if ffn is not None:
                dve.wait_ge(s_wi, 1)
                dve.tensor_tensor(wi_lo[:], wi_raw[:], wi_hi[:].bitcast(F32), ALU.subtract).then_inc(s_wi, 1)
            for n in range(CHUNKS + 2):
                if n < CHUNKS:
                    for t in range(TC):
                        if t >= 2 and n + 1 < CHUNKS:
                            divide(n + 1, t - 2)
                        residual(n, t)
                        if t == 0 and ffn is None and n >= 2:
                            top_norm(n - 2, 2)
                            top_norm(n - 2, 3)
                    variance(n)
                elif ffn is None:
                    for g in range(2, GROUPS):
                        top_norm(n - 2, g)
                if 1 <= n <= CHUNKS:
                    low_transposed(n - 1)
                    if ffn is None:
                        low_queries(n - 1, 0)
                    else:
                        units_in(n - 1)
                if n + 1 < CHUNKS:
                    low(n + 1, 0)
                    low(n + 1, 1)
                if 1 <= n <= CHUNKS:
                    if ffn is None:
                        for g in range(1, GROUPS):
                            low_queries(n - 1, g)
                    else:
                        units_out(n - 1)
                if n < CHUNKS:
                    normalise(n)
                if ffn is None and 1 <= n <= CHUNKS:
                    for g in range(2):
                        top_norm(n - 1, g)
                if ffn is not None and n >= 2:
                    result(n - 2)

        @block.scalar
        def _(act):
            def high(n):
                for k in range(2):
                    act.wait_ge(s_div, 2 * n + k + 1)
                    if n >= 1:
                        act.wait_ge(s_mm, TC * n)
                    act.activation(o_hi[:, :, part(k)], o_raw[:, :, part(k)], ACT.Copy).then_inc(s_hi, 1)

            def high_transposed(n):
                for t in range(TC):
                    act.wait_ge(s_tr, TC * n + t + 1)
                    act.activation(xT_hi[:, :, t * P:(t + 1) * P],
                                   t_ps[t % 2][:].rearrange("p (c t) -> p c t", c=DC), ACT.Copy).then_inc(s_thi, 1)

            def high_queries(n):
                if n >= 1:
                    act.wait_ge(s_qst, 16 * 2 * GROUPS * n)
                for g in range(GROUPS):
                    act.wait_ge(s_z, GROUPS * n + g + 1)
                    act.activation(q_hi[:, g, :], z_ps[g % 2][:], ACT.Copy).then_inc(s_qhi, 1)
                    act.wait_ge(s_qhi, GROUPS * n + g + 1)
                    if GROUPS * n + g >= 2:
                        act.wait_ge(s_norm, GROUPS * n + g - 1)
                    act.activation(q_sq[:, g % 2, :], words(q_hi[:, g, :]), ACT.Square).then_inc(s_qsq, 1)

            def relus(n):
                act.wait_ge(s_s, n + 1)
                for j in range(HH):
                    if HH * n + j >= 2:
                        act.wait_ge(s_g, HH * n + j - 1)
                    act.activation(relu[:, j % 2, :], s_sb[:], ACT.Relu, bias=small[:, HH + j:HH + j + 1],
                                   scale=small[:, j:j + 1]).then_inc(s_relu, 1)

            high(0)
            if query is not None:
                act.wait_ge(s_ahead, 16)
                act.activation(ahead[0][:], ahead_raw[:], ACT.Copy).then_inc(s_ahi, 1)
            if ffn is not None:
                act.wait_ge(s_small, SMALL)
                act.activation(wi_hi[:], wi_raw[:], ACT.Copy).then_inc(s_wi, 1)
            for n in range(CHUNKS + 1):
                if n >= 1:
                    high_transposed(n - 1)
                if n + 1 < CHUNKS:
                    high(n + 1)
                if n >= 1:
                    if ffn is None:
                        high_queries(n - 1)
                    else:
                        relus(n - 1)

        @block.tensor
        def _(pe):
            def project(n):
                for t in range(TC):
                    if t % 2 == 0:
                        pe.wait_ge(s_hi, 2 * n + t // 2 + 1)
                        pe.wait_ge(s_lo, 2 * n + t // 2 + 1)
                    if n >= 1:
                        pe.wait_ge(s_y, TC * (n - 1) + t + 1)
                    tok = slice(t * P, (t + 1) * P)
                    for c in range(C):
                        pe.matmul(o_ps[t][:], o_hi[:, c, tok], w_hi[:, c, :], start=(c == 0), stop=False)
                        pe.matmul(o_ps[t][:], o_hi[:, c, tok], w_lo[:, c, :], start=False, stop=False)
                        last = pe.matmul(o_ps[t][:], o_lo[:, c, tok], w_hi[:, c, :], start=False, stop=(c == C - 1))
                    last.then_inc(s_mm, 1)
                    if t == 0 and query is not None and n >= 2:
                        norm(n - 2, 2)
                        norm(n - 2, 3)

            def transpose(n):
                if query is not None and n >= 1:
                    pe.wait_ge(s_top, GROUPS * n)
                for t in range(TC):
                    pe.wait_ge(s_xn, TC * n + t + 1)
                    if TC * n + t >= 2:
                        pe.wait_ge(s_tlo, TC * n + t - 1)
                    for c in range(DC):
                        last = pe.transpose(t_ps[t % 2][:, c * P:(c + 1) * P], xn[:, t, c * P:(c + 1) * P], ident[:])
                    last.then_inc(s_tr, 1)
                pe.wait_ge(s_tlo, TC * (n + 1))

            def three(ps, a_hi, a_lo):
                for c in range(DC):
                    pe.matmul(ps, a_hi(c), xT_hi[:, c, :], start=(c == 0), stop=False)
                    pe.matmul(ps, a_hi(c), xT_lo[:, c, :], start=False, stop=False)
                    last = pe.matmul(ps, a_lo(c), xT_hi[:, c, :], start=False, stop=(c == DC - 1))
                last.then_inc(s_z, 1)

            def norm(n, g):
                pe.wait_ge(s_qsq, GROUPS * n + g + 1)
                if g >= 2:
                    pe.wait_ge(s_top, GROUPS * n + g - 1)
                pe.matmul(t_ps[g % 2][:], ones_block[:], q_sq[:, g % 2, :], start=True, stop=True).then_inc(s_norm, 1)

            def queries(n):
                for g in range(GROUPS):
                    if GROUPS * n + g >= 2:
                        pe.wait_ge(s_qlo, GROUPS * n + g - 1)
                    e = slice(g * P, (g + 1) * P)
                    three(z_ps[g % 2][:], lambda c: wq_hi[:, c, e], lambda c: wq_lo[:, c, e])
                    if g in (1, 2):
                        norm(n, g - 1)

            def units(n):
                if n == 0:
                    pe.wait_ge(s_wi, 2)
                if n >= 2:
                    pe.wait_ge(s_fin, TC * (n - 1))
                elif n == 1:
                    pe.wait_ge(s_s, 1)
                three(z_ps[0][:], lambda c: wi_hi[:, c, :], lambda c: wi_lo[:, c, :])

            def last_product(n):
                pe.wait_ge(s_g, HH * (n + 1))
                for t in range(TC):
                    if t == 1:
                        pe.wait_ge(s_s, min(n + 2, CHUNKS))
                    if TC * n + t >= 2:
                        pe.wait_ge(s_fin, TC * n + t - 1)
                    pe.matmul(z_ps[(t + 1) % 2][:], g_sb[:, n % 2, t * P:(t + 1) * P], wo2[:], start=True, stop=True)\
                        .then_inc(s_f, 1)

            for n in range(CHUNKS + 2):
                if n < CHUNKS:
                    project(n)
                elif query is not None:
                    for g in range(2, GROUPS):
                        norm(n - 2, g)
                if 1 <= n <= CHUNKS:
                    transpose(n - 1)
                    if ffn is None:
                        queries(n - 1)
                    else:
                        units(n - 1)
                if ffn is not None and n >= 2:
                    last_product(n - 2)


def kernel(**inputs):
    import numpy as np
    import concourse.bacc as bacc
    from concourse.bass_utils import run_bass_kernel_spmd

    a = {k: np.asarray(v) for k, v in inputs.items()}

    def t(name):
        return a[name].T

    wqkv = np.stack([t("L0_attn_Wq").reshape(D, PAIRS, P), t("L0_attn_Wk").reshape(D, PAIRS, P),
                     t("L0_attn_Wv").reshape(D, PAIRS, P)], axis=2)
    arrays = {
        "x": a["x"],
        "ctxT": a["ctx_1024"].reshape(B, L // HALF, HALF, D).transpose(0, 1, 3, 2),
        "mask": a["mask_BxSxS2_if1"].transpose(0, 2, 1),
        "wqkv": wqkv.transpose(1, 0, 2, 3).reshape(PAIRS, D, 3 * P),
        "wo_xwqT": np.concatenate([t("L0_attn_Wo"), t("L0_xattn_w_q")]),
        "bo": a["L0_attn_bo"],
        "qk_scale": np.stack([a["L0_attn_q_scale"].reshape(PAIRS, P), a["L0_attn_k_scale"].reshape(PAIRS, P)], axis=2),
        "xwkvT": np.stack([t("L0_xattn_w_k"), t("L0_xattn_w_v")]),
        "xwoT": t("L0_xattn_w_o"),
        "win": a["L0_ffn_Win"], "bin_": a["L0_ffn_bin_"], "w1": a["L0_ffn_W1"], "b1": a["L0_ffn_b1"],
        "w2": a["L0_ffn_W2"], "b2": a["L0_ffn_b2"], "wout": a["L0_ffn_Wout"], "bout": a["L0_ffn_bout"],
    }
    nc = bacc.Bacc("TRN2", target_bir_lowering=False, num_devices=1)
    args = {}
    for name, value in arrays.items():
        arrays[name] = np.ascontiguousarray(value)
        args[name] = nc.dram_tensor(name, value.shape, mybir.dt.from_np(value.dtype), kind="ExternalInput").ap()
    args["out"] = nc.dram_tensor("out", (B, N, D), F32, kind="ExternalOutput").ap()
    decoder_layer(nc, **args)
    return run_bass_kernel_spmd(nc, [arrays], core_ids=[0]).results[0]["out"]
```

```python
from contextlib import ExitStack

import concourse.bass as bass
from concourse import mybir

P = 128
B, N, D = 2, 1024, 512
L = 2048
H, DH = 16, 64
DK = 32
INNER = H * DH
T = B * N
M, HID = 64, 16
LN_EPS = 1e-5
NORM_EPS = 1e-12
CONSTS = 5 + 4
SUMS = B * H * N // P
SAFE = 60.0

DC = D // P
EC = INNER // P
PAIRS = H // 2
GROUPS = H // 4
TT = N // P
JT = L // P
HALF = 512
NH = N // HALF

ALU = mybir.AluOpType
ACT = mybir.ActivationFunctionType
F32 = mybir.dt.float32
F32R = mybir.dt.float32r
AX_X = mybir.AxisListType.X


def words(ap):
    return ap.bitcast(F32)


FFN_LOADS = 16 * (2 * 6 + 2)


def load_ffn_constants(sp, drams, tiles, s_loads, s_zero):
    win, bin_, w1, b1, w2, b2, wout, bout = drams
    wi_raw, small, bin_sb, b2_sb, wo2, bout_bc = tiles
    HH = HID // 2
    for i in range(2):
        rows = slice(i * M, (i + 1) * M)
        sp.dma_start(wi_raw[:, :, rows], win.rearrange("(c q) m -> q c m", q=P)).then_inc(s_loads, 16)
        for k, a in enumerate((w1, b1, w2)):
            sp.dma_start(small[rows, k * HH:(k + 1) * HH], a[:, i * HH:(i + 1) * HH]).then_inc(s_loads, 16)
        sp.dma_start(bin_sb[rows, :], bin_.unsqueeze(1)).then_inc(s_loads, 16)
        sp.dma_start(wo2[rows, :], wout).then_inc(s_loads, 16)
    sp.wait_ge(s_zero, 1)
    sp.dma_start(b2_sb[0:M, :], b2.unsqueeze(1)).then_inc(s_loads, 16)
    sp.dma_start(bout_bc[:], bout.partition_broadcast(P)).then_inc(s_loads, 16)


def by_partition(sums):
    return sums.rearrange("b c h t -> (b c h t)").rearrange("(p v) -> p v", p=P)


def decoder_layer(nc, x, ctxT, mask, wqkv, wo_xwqT, bo, qk_scale, xwkvT, xwoT,
                  win, bin_, w1, b1, w2, b2, wout, bout, out):
    top = ExitStack()
    with top:
        def sem(name):
            return top.enter_context(nc.semaphore(name))

        def scratch(name, shape, dt=F32):
            return nc.dram_tensor(name, shape, dt, kind="Internal").ap()

        attnT_dram = scratch("attnT_dram", (B, PAIRS, P, N))
        sum1_dram = scratch("sum1_dram", (B, PAIRS, 2, N))
        rsum1_dram = scratch("rsum1_dram", (B, PAIRS, 2, N))
        x1_dram = scratch("x1_dram", (B, N, D))
        q2_dram = scratch("q2_dram", (B * GROUPS, 4, 2, DK, N))
        k2_dram = scratch("k2_dram", (B * GROUPS, 4, 2, DK, L))
        v2_dram = scratch("v2_dram", (B * GROUPS, P, JT, P))
        attn2T_dram = scratch("attn2T_dram", (B, GROUPS, P, N))
        sum2_dram = scratch("sum2_dram", (B, GROUPS, 4, N))
        rsum2_dram = scratch("rsum2_dram", (B, GROUPS, 4, N))

        ident = top.enter_context(nc.sbuf_tensor("ident", [P, P], F32))
        ones = top.enter_context(nc.sbuf_tensor("ones", [P, 32], F32))
        ones_block = top.enter_context(nc.sbuf_tensor("ones_block", [P, P], F32R))
        norm2_k = top.enter_context(nc.sbuf_tensor("norm2_k", [P, B, L // HALF, GROUPS], F32))
        norm2_q = top.enter_context(nc.sbuf_tensor("norm2_q", [P, B, NH, GROUPS], F32))
        mask_min = top.enter_context(nc.sbuf_tensor("mask_min", [P, 4, B * L // HALF], F32))
        flags = top.enter_context(nc.sbuf_tensor("flags", [P, 2], mybir.dt.int32))
        flag = [flags[0:1, i:i + 1] for i in range(2)]
        s_const = sem("s_const")

        self_sems = []

        def self_sem(name):
            self_sems.append(nc.alloc_semaphore(name=name))
            return self_sems[-1]

        self_attention(nc, self_sem, x, wqkv, qk_scale, attnT_dram, sum1_dram, ident, ones, ones_block, s_const,
                       scratch, flags, flag[0])
        nc.clear_and_free_semaphores(self_sems)
        nc.all_engine_barrier()

        def parts(stack, name, chunks):
            return [stack.enter_context(nc.sbuf_tensor(f"{name}_{k}", [P, chunks, D], F32R)) for k in ("hi", "lo")]

        xwo = parts(top, "xwo", DC)
        with ExitStack() as weights:
            wo_xwq = parts(weights, "wo_xwq", EC + DC)
            context_projections(nc, sem, ctxT, mask, xwkvT, k2_dram, v2_dram, ones_block, norm2_k, mask_min,
                                sum1_dram, rsum1_dram, wo_xwqT, wo_xwq)
            output_projection(nc, sem, "b", attnT_dram, None, rsum1_dram, [w[:, 0:EC, :] for w in wo_xwq], bo, x, x1_dram,
                              ident, query=([w[:, EC:, :] for w in wo_xwq], q2_dram, ones_block, norm2_q, xwoT, xwo))
        ffn_tiles = [top.enter_context(nc.sbuf_tensor(name, shape, F32)) for name, shape in (
            ("ffn_win", [P, DC, P]), ("ffn_small", [P, 3 * HID // 2]), ("ffn_bin", [P, 1]), ("ffn_b2", [P, 1]),
            ("ffn_wout", [P, D]), ("ffn_bout", [P, D]))]
        s_ffn = sem("ffn_loads")
        cross_attention(nc, sem, q2_dram, k2_dram, v2_dram, attn2T_dram, sum2_dram, ones,
                        (norm2_q, norm2_k, mask_min, flags), (win, bin_, w1, b1, w2, b2, wout, bout), ffn_tiles, s_ffn)
        stacked = [slice(i * 2 * DK, (i + 1) * 2 * DK) for i in range(2)]
        exact_attention(
            nc, sem, "exact_x_", flag[1], GROUPS, 4, P, DK, JT, DK ** -0.5,
            lambda b, g, h, f, t: [(t[rows, :], q2_dram.rearrange("(b g) h s q t -> b g h (s q) t", g=GROUPS)
                                    [b, g, h, :, f * HALF:(f + 1) * HALF]) for rows in stacked],
            lambda b, g, h, j, t: [(t[64 * i + 32 * c:64 * i + 32 * c + 32, :],
                                    k2_dram.rearrange("(b g) h s q t -> b g h s q t", g=GROUPS)
                                    [b, g, h, i, :, bass.ds(j * P, P)]) for i in range(2) for c in range(2)],
            lambda b, g, h, j: v2_dram.rearrange("(b g) q j e -> b g j q e", g=GROUPS)[b, g, j, :, h * DK:(h + 1) * DK],
            mask,
            lambda b, g, h, f: attn2T_dram[b, g, h * DK:(h + 1) * DK, f * HALF:(f + 1) * HALF],
            lambda b, g, h, f: sum2_dram[b, g, h:h + 1, f * HALF:(f + 1) * HALF], ones)
        output_projection(nc, sem, "e", attn2T_dram, sum2_dram, rsum2_dram, xwo, None,
                          x1_dram, None, ident, ffn=(ffn_tiles, s_ffn, out))


def self_attention(nc, sem, x, wqkv, qk_scale, attnT_dram, sum1_dram, ident, ones, ones_block, s_const,
                   scratch, flags, flag):
    with ExitStack() as outer:
        def sbo(name, shape, dt=F32):
            return outer.enter_context(nc.sbuf_tensor(name, shape, dt))

        xnT_hi = sbo("xnT_hi", [P, DC, T], F32R)
        xnT_lo = sbo("xnT_lo", [P, DC, T], F32R)
        W3 = 3 * P
        w_raw = sbo("w_raw", [P, DC, W3])
        w_hi = sbo("w_hi", [P, DC, W3], F32R)
        w_lo = sbo("w_lo", [P, DC, W3], F32R)
        scales_raw = sbo("scales_raw", [P, 2])
        scales = sbo("scales", [P, 2])
        s_wraw = sem("a_wraw")
        s_whi = sem("a_whi")
        s_wlo = sem("a_wlo")

        def load_weights(sp, p):
            sp.dma_start(w_raw[:], wqkv[p].rearrange("(c q) e -> q c e", q=P)).then_inc(s_wraw, 16)
            sp.dma_start(scales_raw[:], qk_scale[p]).then_inc(s_wraw, 16)

        def split_weights_high(act, p):
            act.wait_ge(s_wraw, 32 * (p + 1))
            act.activation(scales[:], scales_raw[:], ACT.Copy)
            act.activation(w_hi[:], w_raw[:], ACT.Copy).then_inc(s_whi, 1)

        def split_weights_low(dve, p):
            dve.wait_ge(s_whi, p + 1)
            dve.tensor_tensor(w_lo[:], w_raw[:], w_hi[:].bitcast(F32), ALU.subtract).then_inc(s_wlo, 1)

        with ExitStack() as ctx:
            tiles = T // P
            NB = 4
            xt = ctx.enter_context(nc.sbuf_tensor("ln_x", [P, tiles, D], F32))
            xn = ctx.enter_context(nc.sbuf_tensor("ln_xn", [P, NB, D], F32))
            stats = ctx.enter_context(nc.sbuf_tensor("ln_stats", [P, tiles, 6], F32))
            mv = ctx.enter_context(nc.sbuf_tensor("ln_mv", [P, tiles, 2], F32))
            var = ctx.enter_context(nc.sbuf_tensor("ln_var", [P, tiles], F32))
            rstd = ctx.enter_context(nc.sbuf_tensor("ln_rstd", [P, tiles], F32))
            mhalf = ctx.enter_context(nc.sbuf_tensor("ln_mhalf", [P, tiles], F32))
            blocks = ctx.enter_context(nc.sbuf_tensor("ln_blocks", [P, P], F32))
            both_scales = ctx.enter_context(nc.sbuf_tensor("ln_scales", [P, PAIRS, 2], F32))
            prod = ctx.enter_context(nc.sbuf_tensor("ln_prod", [P, PAIRS], F32))
            prod2 = ctx.enter_context(nc.sbuf_tensor("ln_prod2", [P, PAIRS], F32))
            peak = ctx.enter_context(nc.sbuf_tensor("ln_peak", [P, 2], F32))
            tp = ctx.enter_context(nc.psum_tensor("ln_tp", [P, NB, HALF], F32))
            s_scales, s_prod, s_peak, s_flag = sem("ln_scales"), sem("ln_prod"), sem("ln_peak"), sem("ln_flag")
            s_x = [sem(f"ln_x{i}") for i in range(4)]
            s_stat, s_aggr, s_var, s_rstd = sem("ln_stat"), sem("ln_aggr"), sem("ln_var"), sem("ln_rstd")
            s_xn, s_tr, s_hi, s_lo = sem("ln_xn"), sem("ln_tr"), sem("ln_hi"), sem("ln_lo")
            block = ctx.enter_context(nc.Block())

            @block.sync
            def _(sp):
                for i in range(4):
                    sp.dma_start(xt[:, 4 * i:4 * i + 4, :],
                                 x.rearrange("b (n p) d -> p (b n) d", p=P)[:, 4 * i:4 * i + 4, :]).then_inc(s_x[i], 16)
                load_weights(sp, 0)
                sp.dma_start(both_scales[:], qk_scale.rearrange("p q s -> q p s")).then_inc(s_scales, 16)

            @block.gpsimd
            def _(pool):
                pool.memset(ident[:], 0.0).then_inc(s_const, 1)
                pool.memset(ones[:], 1.0).then_inc(s_const, 1)
                pool.memset(mhalf[:], -0.5).then_inc(s_const, 1)
                pool.memset(blocks[:], 0.0).then_inc(s_const, 1)
                pool.wait_ge(s_const, 4)
                pool.affine_select(out=ident[:], in_=ident[:], compare_op=ALU.not_equal, fill=1.0, base=0,
                                   pattern=[[-1, P]], channel_multiplier=1).then_inc(s_const, 1)
                for h in range(4):
                    pool.wait_ge(s_const, 5 + h)
                    pool.memset(blocks[32 * h:32 * h + 32, 32 * h:32 * h + 32], 1.0).then_inc(s_const, 1)
                pool.wait_ge(s_const, CONSTS)
                for i in range(4):
                    pool.wait_ge(s_var, i + 1)
                    pool.tensor_tensor(rstd[:, 4 * i:4 * i + 4], var[:, 4 * i:4 * i + 4], mhalf[:, 0:4],
                                       ALU.pow).then_inc(s_rstd, 1)
                pool.wait_ge(s_rstd, 4)
                pool.wait_ge(s_prod, 3)
                pool.partition_all_reduce(peak[:, 1:2], peak[:, 0:1], P, bass.bass_isa.ReduceOp.max).then_inc(s_peak, 1)

            @block.vector
            def _(dve):
                def low(n):
                    dve.wait_ge(s_hi, n + 1)
                    dve.tensor_tensor(xnT_lo[:, :, n * P:(n + 1) * P],
                                      tp[:, n % NB, :].rearrange("p (c t) -> p c t", c=DC),
                                      xnT_hi[:, :, n * P:(n + 1) * P].bitcast(F32), ALU.subtract).then_inc(s_lo, 1)

                def statistics(i):
                    dve.wait_ge(s_x[i], 16)
                    for n in range(4 * i, 4 * i + 4):
                        dve.bn_stats(stats[:, n, :], xt[:, n, :]).then_inc(s_stat, 1)
                    for n in range(4 * i, 4 * i + 4):
                        dve.wait_ge(s_stat, n + 1)
                        dve.bn_aggr(mv[:, n, :], stats[:, n, :]).then_inc(s_aggr, 1)
                    dve.wait_ge(s_aggr, 4 * i + 4)
                    dve.tensor_scalar(var[:, 4 * i:4 * i + 4], mv[:, 4 * i:4 * i + 4, 1], LN_EPS, None,
                                      ALU.add).then_inc(s_var, 1)

                statistics(0)
                for i in range(4):
                    if i < 3:
                        statistics(i + 1)
                    dve.wait_ge(s_rstd, i + 1)
                    for n in range(4 * i, 4 * i + 4):
                        if n >= NB:
                            dve.wait_ge(s_tr, n - NB + 1)
                        dve.tensor_scalar(xn[:, n % NB, :], xt[:, n, :], mv[:, n, 0:1], rstd[:, n:n + 1],
                                          ALU.subtract, ALU.mult).then_inc(s_xn, 1)
                        if n >= 2:
                            low(n - 2)
                split_weights_low(dve, 0)
                dve.wait_ge(s_scales, 16)
                dve.tensor_tensor(prod[:], both_scales[:, :, 0], both_scales[:, :, 1], ALU.mult).then_inc(s_prod, 1)
                dve.wait_ge(s_prod, 1)
                dve.tensor_tensor(prod2[:], prod[:], prod[:], ALU.mult).then_inc(s_prod, 1)
                dve.wait_ge(s_prod, 2)
                dve.tensor_reduce(peak[:, 0:1], prod2[:], AX_X, ALU.max).then_inc(s_prod, 1)
                dve.wait_ge(s_peak, 1)
                dve.tensor_scalar(flags[:, 0:1], peak[:, 1:2], (SAFE * DH ** 0.5) ** 2, None, ALU.is_gt).then_inc(s_flag, 1)
                low(tiles - 2)
                low(tiles - 1)
                dve.wait_ge(s_flag, 1)

            @block.tensor
            def _(pe):
                pe.wait_ge(s_const, CONSTS)
                for n in range(tiles):
                    pe.wait_ge(s_xn, n + 1)
                    if n >= NB:
                        pe.wait_ge(s_lo, n - NB + 1)
                    for c in range(DC):
                        last = pe.transpose(tp[:, n % NB, c * P:(c + 1) * P], xn[:, n % NB, c * P:(c + 1) * P], ident[:])
                    last.then_inc(s_tr, 1)

            @block.scalar
            def _(act):
                act.wait_ge(s_const, CONSTS)
                act.activation(ones_block[:], blocks[:], ACT.Copy)
                for n in range(tiles):
                    if n == 6:
                        split_weights_high(act, 0)
                    act.wait_ge(s_tr, n + 1)
                    act.activation(xnT_hi[:, :, n * P:(n + 1) * P],
                                   tp[:, n % NB, :].rearrange("p (c t) -> p c t", c=DC), ACT.Copy).then_inc(s_hi, 1)

        with ExitStack() as inner:
            def sb(name, shape, dt=F32):
                return inner.enter_context(nc.sbuf_tensor(name, shape, dt))

            qkv = [sb(f"qkv{i}", [P, TT, W3]) for i in range(2)]
            sq = sb("sq", [P, 2, 2, 2 * P])
            ss = sb("ss", [P, 2, 8])
            nrm = sb("nrm", [P, 2, 8])
            nmax = sb("nmax", [P, 2, 8])
            rn = sb("rn", [P, 2, 8])
            half8 = sb("half8", [P, 8])
            q_st = [[sb(f"q_st{i}{h}", [P, N], F32R) for h in range(2)] for i in range(2)]
            kh_st = [[sb(f"kh_st{i}{h}", [P, N], F32R) for h in range(2)] for i in range(2)]
            kl_st = [[sb(f"kl_st{i}{h}", [P, N], F32R) for h in range(2)] for i in range(2)]
            probs = [[sb(f"probs{i}{h}", [P, N]) for h in range(2)] for i in range(2)]
            psum_acc = [[sb(f"pacc{i}{h}", [P, N]) for h in range(2)] for i in range(2)]
            o_sb = sb("o_sb", [P, N])
            den_sb = sb("den_sb", [P, HALF])

            sc_ps = [inner.enter_context(nc.psum_tensor(f"sc_ps{h}", [P, N], F32)) for h in range(2)]
            o_ps = inner.enter_context(nc.psum_tensor("o_ps", [P, N], F32))
            m_ps = [inner.enter_context(nc.psum_tensor(f"m_ps{i}", [P, HALF], F32)) for i in range(2)]

            s_half = sem("a_half")
            s_proj = sem("a_proj")
            s_qkv = sem("a_qkv")
            s_ss = sem("a_ss")
            s_nrm = sem("a_nrm")
            s_rn = sem("a_rn")
            s_unit = sem("a_unit")
            s_tr = sem("a_tr")
            s_hi = sem("a_hi")
            s_lo = sem("a_lo")
            s_dup = sem("a_dup")
            s_sc = sem("a_sc")
            s_pr = sem("a_pr")
            s_pv = sem("a_pv")
            s_acc = sem("a_acc")
            s_den = sem("a_den")
            s_dsb = sem("a_dsb")
            s_osb = sem("a_osb")
            s_ost = sem("a_ost")
            s_dst = sem("a_dst")
            block = inner.enter_context(nc.Block())


            @block.sync
            def _(sp):
                def duplicate(v, par, k):
                    cols = slice(k * HALF, (k + 1) * HALF)
                    sp.wait_ge(s_hi, 8 * v + 4 * k + 4)
                    sp.wait_ge(s_lo, 8 * v + 4 * k + 4)
                    for st in (kh_st, kl_st):
                        sp.dma_start(words(st[par][0][64:128, cols]), words(st[par][0][0:64, cols])).then_inc(s_dup, 16)
                        sp.dma_start(words(st[par][1][0:64, cols]), words(st[par][1][64:128, cols])).then_inc(s_dup, 16)

                def store(u, p, b):
                    sp.wait_ge(s_osb, u + 1)
                    sp.dma_start(attnT_dram[b, p],
                                 o_sb[:]).then_inc(s_ost, 16)
                    sp.wait_ge(s_dsb, u + 1)
                    for h in range(2):
                        for f in range(NH):
                            r = 32 * (2 * f + h)
                            sp.dma_start(sum1_dram[b, p, h:h + 1, f * HALF:(f + 1) * HALF],
                                         den_sb[r:r + 1, :]).then_inc(s_dst, 16)

                def body(p, first, last):
                    u = 2 * p
                    duplicate(u + 1, 1, 0)
                    duplicate(u + 1, 1, 1)
                    if not last:
                        sp.wait_ge(s_whi, p + 2)
                        sp.wait_ge(s_wlo, p + 2)
                    store(u, p, 0)
                    if not last:
                        load_next(p)
                        duplicate(u + 2, 0, 0)
                        duplicate(u + 2, 0, 1)
                    store(u + 1, p, 1)

                def load_next(p):
                    load_weights(sp, (p + 2) % PAIRS)

                sp.wait_ge(s_whi, 1)
                sp.wait_ge(s_wlo, 1)
                load_weights(sp, 1)
                duplicate(0, 0, 0)
                duplicate(0, 0, 1)
                body(0, True, False)
                with sp.Fori(1, PAIRS - 1) as p:
                    body(p, False, False)
                body(PAIRS - 1, False, True)
                sp.wait_ge(s_ost, 16 * 2 * PAIRS)
                sp.wait_ge(s_dst, 64 * 2 * PAIRS)
                sp.wait_ge(s_wraw, 32 * (PAIRS + 1))

            @block.gpsimd
            def _(pool):
                pool.memset(half8[:], 0.5).then_inc(s_half, 1)
                pool.wait_ge(s_half, 1)

                def root(v, k):
                    pool.wait_ge(s_ss, 4 * v + k + 1)
                    pool.tensor_tensor(nrm[:, k % 2, :], ss[:, k % 2, :], half8[:], ALU.pow).then_inc(s_nrm, 1)

                with pool.Fori(0, 2 * PAIRS) as v:
                    for k in range(4):
                        root(v, k)

            @block.tensor
            def _(pe):
                def project(v, par, p, b, t, first=False):
                    m = m_ps[t % 2]
                    if t in (0, 1):
                        if t == 0:
                            pe.wait_ge(s_whi, p + 1)
                            pe.wait_ge(s_wlo, p + 1)
                        if not first:
                            pe.wait_ge(s_lo, 8 * v)
                    elif t in (2, 3):
                        pe.wait_ge(s_qkv, 8 * v + t - 1)
                        if t == 2 and not (isinstance(v, int) and v < 2):
                            pe.wait_ge(s_dsb, v - 1)
                    elif t in (4, 5):
                        pe.wait_ge(s_qkv, 8 * v + t - 1)
                    else:
                        pe.wait_ge(s_lo, 8 * v + 4)
                    tok = slice(b * N + t * P, b * N + (t + 1) * P)
                    for c in range(DC):
                        pe.matmul(m[:, 0:W3], xnT_hi[:, c, tok], w_hi[:, c, :], start=(c == 0), stop=False)
                        pe.matmul(m[:, 0:W3], xnT_hi[:, c, tok], w_lo[:, c, :], start=False, stop=False)
                        last = pe.matmul(m[:, 0:W3], xnT_lo[:, c, tok], w_hi[:, c, :], start=False, stop=(c == DC - 1))
                    last.then_inc(s_proj, 1)

                def turn(v, par, k):
                    pe.wait_ge(s_unit, 4 * v + 2 * k + 2)
                    pe.wait_ge(s_qkv, 8 * v + (6 if k == 0 else 8))
                    for i in range(2):
                        for t in range(4):
                            last = pe.transpose(m_ps[i][:, t * P:(t + 1) * P],
                                                qkv[par][:, 4 * k + t, i * P:(i + 1) * P], ident[:])
                        last.then_inc(s_tr, 1)

                def scores(u, par, j, first=False):
                    if j == 0:
                        pe.wait_ge(s_hi, 8 * u + 8)
                        pe.wait_ge(s_lo, 8 * u + 8)
                        pe.wait_ge(s_dup, 128 * u + 128)
                    for h in range(2):
                        if not (first and j == 0):
                            pe.wait_ge(s_pr, 16 * u + 2 * j + h - 1)
                        keys = slice(j * P, (j + 1) * P)
                        for st, k_st in enumerate((kh_st, kl_st)):
                            for f in range(NH):
                                q = slice(f * HALF, (f + 1) * HALF)
                                last = pe.matmul(sc_ps[h][:, q], k_st[par][h][:, keys], q_st[par][h][:, q],
                                                 start=(st == 0), stop=(st == 1))
                        last.then_inc(s_sc, 1)

                def values(u, par, j, first=False):
                    pe.wait_ge(s_pr, 16 * u + 2 * j + 2)
                    if j == 0 and not first:
                        pe.wait_ge(s_osb, u)
                    for f in range(NH):
                        q = slice(f * HALF, (f + 1) * HALF)
                        for h in range(2):
                            last = pe.matmul(o_ps[64 * h:64 * h + 64, q],
                                             qkv[par][:, j, 2 * P + 64 * h:2 * P + 64 * h + 64], probs[j % 2][h][:, q],
                                             start=(j == 0), stop=(j == TT - 1), skip_group_check=True)
                    last.then_inc(s_pv, 1)

                def sums(u, par):
                    pe.wait_ge(s_acc, 14 * (u + 1))
                    if isinstance(u, int) and u >= 2 * PAIRS - 2:
                        pe.wait_ge(s_lo, 8 * 2 * PAIRS)
                    else:
                        pe.wait_ge(s_qkv, 8 * (u + 2) + 1)
                    for f in range(NH):
                        for h in range(2):
                            r = 32 * (2 * f + h)
                            last = pe.matmul(m_ps[0][r:r + 32, :], ones[:, 0:32],
                                             psum_acc[par][h][:, f * HALF:(f + 1) * HALF],
                                             start=True, stop=True, skip_group_check=True)
                    last.then_inc(s_den, 1)

                def body(p, first, last):
                    for b in range(2):
                        u = 2 * p + b
                        nxt = not (last and b == 1)
                        pn, bn = (p, 1) if b == 0 else (p + 1, 0)
                        for j in range(1, TT):
                            scores(u, b, j)
                            if nxt and j == 4:
                                project(u + 1, 1 - b, pn, bn, 6)
                                project(u + 1, 1 - b, pn, bn, 7)
                            values(u, b, j - 1, first and b == 0)
                            if nxt:
                                if j in (1, 2):
                                    project(u + 1, 1 - b, pn, bn, 2 * j)
                                    project(u + 1, 1 - b, pn, bn, 2 * j + 1)
                                if j == 3:
                                    turn(u + 1, 1 - b, 0)
                                if j == 5:
                                    turn(u + 1, 1 - b, 1)
                        if nxt:
                            scores(u + 1, 1 - b, 0)
                        values(u, b, TT - 1)
                        if not last:
                            project(u + 2, b, p + 1, b, 0)
                            project(u + 2, b, p + 1, b, 1)
                        sums(u, b)

                for t in range(6):
                    project(0, 0, 0, 0, t, first=True)
                turn(0, 0, 0)
                project(0, 0, 0, 0, 6)
                project(0, 0, 0, 0, 7)
                turn(0, 0, 1)
                project(1, 1, 0, 1, 0)
                project(1, 1, 0, 1, 1)
                scores(0, 0, 0, first=True)
                body(0, True, False)
                with pe.Fori(1, PAIRS - 1) as p:
                    body(p, False, False)
                body(PAIRS - 1, False, True)

            @block.scalar
            def _(act):
                def keep(v, par, t, first=False):
                    act.wait_ge(s_proj, 8 * v + t + 1)
                    k = t // 2
                    if not (first and k < 2):
                        act.wait_ge(s_ss, 4 * v + k - 1)
                    act.activation(sq[:, k % 2, t % 2, :], m_ps[t % 2][:, 0:2 * P], ACT.Square)
                    act.activation(qkv[par][:, t, :], m_ps[t % 2][:, 0:W3], ACT.Copy).then_inc(s_qkv, 1)

                def high(v, par, p, k):
                    cols = slice(k * HALF, (k + 1) * HALF)
                    for i, st in enumerate((q_st, kh_st)):
                        act.wait_ge(s_tr, 4 * v + 2 * k + i + 1)
                        for h in range(2):
                            rows = slice(64 * h, 64 * h + 64)
                            act.activation(st[par][h][rows, cols], m_ps[i][rows, :], ACT.Copy,
                                           scale=scales[rows, i:i + 1]).then_inc(s_hi, 1)

                def exps(u, par, j, first=False):
                    for h in range(2):
                        act.wait_ge(s_sc, 16 * u + 2 * j + h + 1)
                        if not (first and j < 2):
                            act.wait_ge(s_pv, 8 * u + j - 1)
                            act.wait_ge(s_acc, 14 * u + {0: -4, 1: -2, 2: 0, 3: 0}.get(j, 2 * (j - 3)) + h + 1)
                        act.activation(probs[j % 2][h][:], sc_ps[h][:], ACT.Exp, scale=DH ** -0.5).then_inc(s_pr, 1)

                def collect(u, par, first=False):
                    act.wait_ge(s_pv, 8 * u + 8)
                    if not first:
                        act.wait_ge(s_ost, 16 * u)
                    act.activation(o_sb[:], o_ps[:], ACT.Copy).then_inc(s_osb, 1)

                def collect_sums(u, first=False):
                    act.wait_ge(s_den, u + 1)
                    if not first:
                        act.wait_ge(s_dst, 64 * u)
                    act.activation(den_sb[:], m_ps[0][:], ACT.Copy).then_inc(s_dsb, 1)

                def body(p, first, last):
                    for b in range(2):
                        u = 2 * p + b
                        f0 = first and b == 0
                        nxt = not (last and b == 1)
                        pn = p if b == 0 else p + 1
                        for j in range(1, TT):
                            exps(u, b, j, f0)
                            if nxt:
                                if j in (1, 2):
                                    keep(u + 1, 1 - b, 2 * j)
                                    keep(u + 1, 1 - b, 2 * j + 1)
                                if j == 3:
                                    high(u + 1, 1 - b, pn, 0)
                                if j == 4:
                                    keep(u + 1, 1 - b, 6)
                                    keep(u + 1, 1 - b, 7)
                                if j == 5:
                                    high(u + 1, 1 - b, pn, 1)
                                if j == 6 and b == 0 and not last:
                                    act.wait_ge(s_proj, 8 * (u + 2))
                                    act.wait_ge(s_lo, 8 * (u + 2))
                                    split_weights_high(act, p + 1)
                        if nxt:
                            exps(u + 1, 1 - b, 0)
                        collect(u, b, f0)
                        if not last:
                            keep(u + 2, b, 0)
                            keep(u + 2, b, 1)
                        collect_sums(u, f0)

                for t in range(6):
                    keep(0, 0, t, first=True)
                high(0, 0, 0, 0)
                keep(0, 0, 6)
                keep(0, 0, 7)
                high(0, 0, 0, 1)
                keep(1, 1, 0)
                keep(1, 1, 1)
                exps(0, 0, 0, first=True)
                body(0, True, False)
                with act.Fori(1, PAIRS - 1) as p:
                    body(p, False, False)
                body(PAIRS - 1, False, True)

            @block.vector
            def _(dve):
                def squares(v, k, first=False):
                    dve.wait_ge(s_qkv, 8 * v + 2 * k + 2)
                    if not (first and k < 2):
                        dve.wait_ge(s_nrm, 4 * v + k - 1)
                    dve.tensor_reduce(ss[:, k % 2, :], sq[:, k % 2, :, :].rearrange("p t (h d) -> p (t h) d", d=DH),
                                      AX_X, ALU.add).then_inc(s_ss, 1)

                def normalise(v, par, k):
                    dve.wait_ge(s_nrm, 4 * v + k + 1)
                    dve.tensor_scalar(nmax[:, k % 2, :], nrm[:, k % 2, :], NORM_EPS, None, ALU.max).then_inc(s_rn, 1)
                    dve.wait_ge(s_rn, 8 * v + 2 * k + 1)
                    dve.reciprocal(rn[:, k % 2, :], nmax[:, k % 2, :]).then_inc(s_rn, 1)
                    dve.wait_ge(s_rn, 8 * v + 2 * k + 2)
                    for t in range(2):
                        qk = qkv[par][:, 2 * k + t, 0:2 * P].rearrange("p (h d) -> p h d", d=DH)
                        last = dve.tensor_tensor(qk, qk,
                                                 rn[:, k % 2, 4 * t:4 * t + 4].unsqueeze(2).to_broadcast([P, 4, DH]),
                                                 ALU.mult)
                    last.then_inc(s_unit, 1)

                def low(v, par, p, k):
                    cols = slice(k * HALF, (k + 1) * HALF)
                    for i, (st, dst) in enumerate(((q_st, q_st), (kh_st, kl_st))):
                        for h in range(2):
                            rows = slice(64 * h, 64 * h + 64)
                            to = slice(64 - 64 * h, 128 - 64 * h) if i == 0 else rows
                            dve.wait_ge(s_hi, 8 * v + 4 * k + 2 * i + h + 1)
                            dve.scalar_tensor_tensor(out=dst[par][h][to, cols], in0=m_ps[i][rows, :],
                                                     scalar=scales[rows, i:i + 1],
                                                     in1=st[par][h][rows, cols].bitcast(F32),
                                                     op0=ALU.mult, op1=ALU.subtract).then_inc(s_lo, 1)

                def add(u, par, j, first=False):
                    for h in range(2):
                        dve.wait_ge(s_pr, 16 * u + 2 * j + h + 1)
                        acc = psum_acc[par][h]
                        if j == 1:
                            if not first:
                                dve.wait_ge(s_den, u - 1)
                            dve.tensor_tensor(acc[:], probs[0][h][:], probs[1][h][:], ALU.add).then_inc(s_acc, 1)
                        else:
                            dve.wait_ge(s_acc, 14 * u + 2 * (j - 2) + h + 1)
                            dve.tensor_tensor(acc[:], acc[:], probs[j % 2][h][:], ALU.add).then_inc(s_acc, 1)

                def body(p, first, last):
                    for b in range(2):
                        u = 2 * p + b
                        nxt = not (last and b == 1)
                        pn = p if b == 0 else p + 1
                        for j in range(1, TT):
                            if nxt and j == 5:
                                normalise(u + 1, 1 - b, 3)
                            add(u, b, j, first)
                            if nxt:
                                if j == 1:
                                    normalise(u + 1, 1 - b, 0)
                                    squares(u + 1, 1)
                                if j == 2:
                                    normalise(u + 1, 1 - b, 1)
                                    squares(u + 1, 2)
                                if j == 3:
                                    low(u + 1, 1 - b, pn, 0)
                                    normalise(u + 1, 1 - b, 2)
                                if j == 4:
                                    squares(u + 1, 3)
                                if j == 5:
                                    low(u + 1, 1 - b, pn, 1)
                                if j == 6 and b == 0 and not last:
                                    split_weights_low(dve, p + 1)
                        if not last:
                            squares(u + 2, 0)

                squares(0, 0, first=True)
                squares(0, 1, first=True)
                normalise(0, 0, 0)
                normalise(0, 0, 1)
                squares(0, 2, first=True)
                normalise(0, 0, 2)
                low(0, 0, 0, 0)
                squares(0, 3, first=True)
                normalise(0, 0, 3)
                low(0, 0, 0, 1)
                squares(1, 0)
                body(0, True, False)
                with dve.Fori(1, PAIRS - 1) as p:
                    body(p, False, False)
                body(PAIRS - 1, False, True)

        gq_dram = scratch("gq_dram", (B, PAIRS, P, N))
        gk_dram = scratch("gk_dram", (B, PAIRS, P, N))
        gv_dram = scratch("gv_dram", (B, PAIRS, N, P))
        exact_inputs(nc, sem, xnT_hi, xnT_lo, wqkv, qk_scale, gq_dram, gk_dram, gv_dram, ident, flag)
        exact_attention(
            nc, sem, "exact_s_", flag, PAIRS, 2, DH, DH, TT, DH ** -0.5,
            lambda b, g, h, f, t: [(t[:], gq_dram[b, g, h * DH:(h + 1) * DH, f * HALF:(f + 1) * HALF])],
            lambda b, g, h, j, t: [(t[:], gk_dram[b, g, h * DH:(h + 1) * DH, bass.ds(j * P, P)])],
            lambda b, g, h, j: gv_dram[b, g, bass.ds(j * P, P), h * DH:(h + 1) * DH],
            None,
            lambda b, g, h, f: attnT_dram[b, g, h * DH:(h + 1) * DH, f * HALF:(f + 1) * HALF],
            lambda b, g, h, f: sum1_dram[b, g, h:h + 1, f * HALF:(f + 1) * HALF], ones)


def exact_inputs(nc, sem, xnT_hi, xnT_lo, wqkv, qk_scale, gq_dram, gk_dram, gv_dram, ident, flag):
    with ExitStack() as ctx:
        def sb(name, shape, dt=F32):
            return ctx.enter_context(nc.sbuf_tensor("gi_" + name, shape, dt))

        W3 = 3 * P
        w_raw = sb("wraw", [P, DC, W3])
        w_hi = sb("whi", [P, DC, W3], F32R)
        w_lo = sb("wlo", [P, DC, W3], F32R)
        scales = sb("scales", [P, 2])
        x_hi = sb("xhi", [P, DC, P], F32R)
        x_lo = sb("xlo", [P, DC, P], F32R)
        qkv = sb("qkv", [P, W3])
        sq = sb("sq", [P, 2 * P])
        ss, nrm, nmax, rn, half4 = (sb(k, [P, 4]) for k in ("ss", "nrm", "nmax", "rn", "half4"))
        qkT = sb("qkT", [P, 2 * P])
        m_ps = ctx.enter_context(nc.psum_tensor("gi_m", [P, HALF], F32))
        t_ps = ctx.enter_context(nc.psum_tensor("gi_t", [P, HALF], F32))
        s_w, s_whi, s_wlo, s_half = sem("gi_w"), sem("gi_whi"), sem("gi_wlo"), sem("gi_half")
        s_cur, s_mm, s_qkv, s_ss, s_nrm = sem("gi_cur"), sem("gi_mm"), sem("gi_qkv"), sem("gi_ss"), sem("gi_nrm")
        s_rn, s_unit, s_tr, s_out, s_st = sem("gi_rn"), sem("gi_unit"), sem("gi_tr"), sem("gi_out"), sem("gi_st")
        block = ctx.enter_context(nc.Block())


        @block.sync
        def _(sp):
            taken = sp.value_load(flag, min_val=0, max_val=1)
            with sp.If(taken > 0):
                sp.nop().then_inc(s_st, 48)
                with sp.Fori(0, PAIRS) as p:
                    sp.wait_ge(s_st, 48 * B * TT * p + 48)
                    sp.dma_start(w_raw[:], wqkv[p].rearrange("(c q) e -> q c e", q=P)).then_inc(s_w, 16)
                    sp.dma_start(scales[:], qk_scale[p]).then_inc(s_w, 16)
                    for b in range(B):
                        with sp.Fori(0, TT) as t:
                            sp.wait_ge(s_out, 2 * (B * TT * p + TT * b + t) + 2)
                            sp.dma_start(gq_dram[b, p, :, bass.ds(t * P, P)], qkT[:, 0:P]).then_inc(s_st, 16)
                            sp.dma_start(gk_dram[b, p, :, bass.ds(t * P, P)], qkT[:, P:2 * P]).then_inc(s_st, 16)
                            sp.dma_start(gv_dram[b, p, bass.ds(t * P, P), :], qkv[:, 2 * P:]).then_inc(s_st, 16)
                sp.wait_ge(s_st, 48 * B * TT * PAIRS + 48)

        @block.scalar
        def _(act):
            taken = act.value_load(flag, min_val=0, max_val=1)
            with act.If(taken > 0):
                with act.Fori(0, PAIRS) as p:
                    act.wait_ge(s_w, 32 * p + 32)
                    act.activation(w_hi[:], w_raw[:], ACT.Copy).then_inc(s_whi, 1)
                    for b in range(B):
                        with act.Fori(0, TT) as t:
                            s = B * TT * p + TT * b + t
                            act.wait_ge(s_st, 48 * s + 48)
                            act.activation(x_hi[:], words(xnT_hi[:, :, bass.ds(t * P + b * N, P)]), ACT.Copy)
                            act.activation(x_lo[:], words(xnT_lo[:, :, bass.ds(t * P + b * N, P)]), ACT.Copy)\
                                .then_inc(s_cur, 1)
                            act.wait_ge(s_mm, s + 1)
                            act.activation(qkv[:], m_ps[:, 0:W3], ACT.Copy)
                            act.activation(sq[:], m_ps[:, 0:2 * P], ACT.Square).then_inc(s_qkv, 1)
                            act.wait_ge(s_tr, s + 1)
                            for i in range(2):
                                act.activation(qkT[:, i * P:(i + 1) * P], t_ps[:, i * P:(i + 1) * P], ACT.Copy,
                                               scale=scales[:, i:i + 1]).then_inc(s_out, 1)

        @block.gpsimd
        def _(pool):
            taken = pool.value_load(flag, min_val=0, max_val=1)
            with pool.If(taken > 0):
                pool.memset(half4[:], 0.5).then_inc(s_half, 1)
                pool.wait_ge(s_half, 1)
                with pool.Fori(0, PAIRS * B * TT) as s:
                    pool.wait_ge(s_ss, s + 1)
                    pool.tensor_tensor(nrm[:], ss[:], half4[:], ALU.pow).then_inc(s_nrm, 1)

        @block.vector
        def _(dve):
            taken = dve.value_load(flag, min_val=0, max_val=1)
            with dve.If(taken > 0):
                with dve.Fori(0, PAIRS) as p:
                    dve.wait_ge(s_whi, p + 1)
                    dve.tensor_tensor(w_lo[:], w_raw[:], w_hi[:].bitcast(F32), ALU.subtract).then_inc(s_wlo, 1)
                    with dve.Fori(0, B * TT) as t:
                        s = B * TT * p + t
                        dve.wait_ge(s_qkv, s + 1)
                        dve.tensor_reduce(ss[:], sq[:].rearrange("p (h d) -> p h d", d=DH), AX_X, ALU.add)\
                            .then_inc(s_ss, 1)
                        dve.wait_ge(s_nrm, s + 1)
                        dve.tensor_scalar(nmax[:], nrm[:], NORM_EPS, None, ALU.max).then_inc(s_rn, 1)
                        dve.wait_ge(s_rn, 2 * s + 1)
                        dve.reciprocal(rn[:], nmax[:]).then_inc(s_rn, 1)
                        dve.wait_ge(s_rn, 2 * s + 2)
                        qk = qkv[:, 0:2 * P].rearrange("p (h d) -> p h d", d=DH)
                        dve.tensor_tensor(qk, qk, rn[:].unsqueeze(2).to_broadcast([P, 4, DH]), ALU.mult)\
                            .then_inc(s_unit, 1)

        @block.tensor
        def _(pe):
            taken = pe.value_load(flag, min_val=0, max_val=1)
            with pe.If(taken > 0):
                with pe.Fori(0, PAIRS) as p:
                    with pe.Fori(0, B * TT) as t:
                        s = B * TT * p + t
                        pe.wait_ge(s_wlo, p + 1)
                        pe.wait_ge(s_cur, s + 1)
                        for c in range(DC):
                            pe.matmul(m_ps[:, 0:W3], x_hi[:, c, :], w_hi[:, c, :], start=(c == 0), stop=False)
                            pe.matmul(m_ps[:, 0:W3], x_hi[:, c, :], w_lo[:, c, :], start=False, stop=False)
                            last = pe.matmul(m_ps[:, 0:W3], x_lo[:, c, :], w_hi[:, c, :], start=False, stop=(c == DC - 1))
                        last.then_inc(s_mm, 1)
                        pe.wait_ge(s_unit, s + 1)
                        for i in range(2):
                            last = pe.transpose(t_ps[:, i * P:(i + 1) * P], qkv[:, i * P:(i + 1) * P], ident[:])
                        last.then_inc(s_tr, 1)


def exact_attention(nc, sem, tag, flag, G, HG, K, W, KT, scale, load_q, load_k, load_v, mask, store_o, store_sums, ones):
    with ExitStack() as ctx:
        def sb(name, shape, dt=F32):
            return ctx.enter_context(nc.sbuf_tensor(tag + name, shape, dt))

        q_sb = sb("q", [K, HALF])
        k_sb = sb("k", [K, P])
        v_sb = sb("v", [P, W])
        mask_sb = sb("mask", [P, HALF], mybir.dt.int32)
        keep = sb("keep", [P, HALF])
        penalty = sb("penalty", [P, HALF])
        logits = sb("logits", [P, HALF])
        kept = sb("kept", [P, HALF])
        final = sb("final", [P, HALF])
        top = sb("top", [P, HALF])
        top_bc = sb("topbc", [P, HALF])
        below = sb("below", [P, HALF])
        probs = sb("probs", [P, HALF])
        zero = sb("zero", [P, HALF])
        o_sb = sb("o", [W, HALF])
        den_sb = sb("den", [32, HALF])
        sc_ps = ctx.enter_context(nc.psum_tensor(tag + "sc_ps", [P, HALF], F32))
        o_ps = ctx.enter_context(nc.psum_tensor(tag + "o_ps", [P, HALF], F32))
        den_ps = ctx.enter_context(nc.psum_tensor(tag + "den_ps", [P, HALF], F32))

        def s(name):
            return sem(tag + name)

        s_q, s_in1, s_in2 = s("q"), s("in1"), s("in2")
        s_sc, s_v, s_max, s_mbc = s("sc"), s("v"), s("max"), s("mbc")
        s_below, s_p, s_pv, s_osb, s_st, s_top, s_zero = s("below"), s("p"), s("pv"), s("osb"), s("st"), s("top"), s("zero")
        block = ctx.enter_context(nc.Block())
        NV = 1 if mask is None else 5
        Q1 = 16 * len(load_q(0, 0, 0, 0, q_sb))
        N1 = 16 * (len(load_k(0, 0, 0, 0, k_sb)) + (0 if mask is None else 1))
        N2 = N1 + 16
        UNITS = B * G * HG * NH

        def unit(b, g, h, f):
            return NH * HG * (G * b + g) + NH * h + f

        def over_units(eng, work):
            for b in range(B):
                with eng.Fori(0, G) as g:
                    for h in range(HG):
                        for f in range(NH):
                            work(b, g, h, f, unit(b, g, h, f))

        @block.sync
        def _(sp):
            taken = sp.value_load(flag, min_val=0, max_val=1)
            with sp.If(taken > 0):
                sp.nop().then_inc(s_max, 1)
                sp.nop().then_inc(s_pv, 1)
                sp.nop().then_inc(s_st, 32)

                def work(b, g, h, f, c):
                    sp.wait_ge(s_pv, KT * c + 1)
                    for ap, src in load_q(b, g, h, f, q_sb):
                        sp.dma_start(ap, src).then_inc(s_q, 16)
                    with sp.Fori(0, KT) as j:
                        sp.wait_ge(s_max, KT * c + j + 1)
                        if mask is not None:
                            sp.dma_start(mask_sb[:], mask[b, bass.ds(j * P, P), f * HALF:(f + 1) * HALF]).then_inc(s_in1, 16)
                        for ap, src in load_k(b, g, h, j, k_sb):
                            sp.dma_start(ap, src).then_inc(s_in1, 16)
                    with sp.Fori(0, KT) as j:
                        sp.wait_ge(s_max, KT * c + KT + 1)
                        sp.wait_ge(s_pv, KT * c + j + 1)
                        if mask is not None:
                            sp.dma_start(mask_sb[:], mask[b, bass.ds(j * P, P), f * HALF:(f + 1) * HALF]).then_inc(s_in2, 16)
                        for ap, src in load_k(b, g, h, j, k_sb):
                            sp.dma_start(ap, src).then_inc(s_in2, 16)
                        sp.dma_start(v_sb[:], load_v(b, g, h, j)).then_inc(s_in2, 16)
                    sp.wait_ge(s_osb, 2 * c + 2 + 1)
                    sp.dma_start(store_o(b, g, h, f), o_sb[:]).then_inc(s_st, 16)
                    sp.dma_start(store_sums(b, g, h, f), den_sb[0:1, :]).then_inc(s_st, 16)

                over_units(sp, work)
                sp.wait_ge(s_st, 32 * UNITS + 32)

        @block.tensor
        def _(pe):
            taken = pe.value_load(flag, min_val=0, max_val=1)
            with pe.If(taken > 0):
                pe.wait_ge(s_zero, 1)

                def work(b, g, h, f, c):
                    pe.wait_ge(s_q, Q1 * c + Q1)
                    pe.wait_ge(s_osb, 2 * c + 1)
                    pe.matmul(o_ps[0:W, :], zero[:, 0:W], zero[:], start=True, stop=False, skip_group_check=True)
                    pe.matmul(den_ps[0:32, :], zero[:, 0:32], zero[:], start=True, stop=False, skip_group_check=True)
                    with pe.Fori(0, KT) as j:
                        pe.wait_ge(s_in1, N1 * (KT * c + j) + N1)
                        pe.matmul(sc_ps[:], k_sb[:], q_sb[:], start=True, stop=True).then_inc(s_sc, 1)
                    with pe.Fori(0, KT) as j:
                        pe.wait_ge(s_in2, N2 * (KT * c + j) + N2)
                        pe.matmul(sc_ps[:], k_sb[:], q_sb[:], start=True, stop=True).then_inc(s_sc, 1)
                        pe.wait_ge(s_p, KT * c + j + 1)
                        pe.matmul(o_ps[0:W, :], v_sb[:], probs[:], start=False, stop=False, skip_group_check=True)
                        pe.matmul(den_ps[0:32, :], ones[:, 0:32], probs[:], start=False, stop=False,
                                  skip_group_check=True).then_inc(s_pv, 1)

                over_units(pe, work)

        @block.vector
        def _(dve):
            taken = dve.value_load(flag, min_val=0, max_val=1)
            with dve.If(taken > 0):

                def masked(step):
                    dve.wait_ge(s_sc, step + 1)
                    dve.tensor_scalar(logits[:], sc_ps[:], scale, None, ALU.mult).then_inc(s_v, 1)
                    if mask is None:
                        dve.wait_ge(s_v, step + 1)
                        return logits
                    dve.tensor_scalar(keep[:], mask_sb[:], 0.0, None, ALU.not_equal).then_inc(s_v, 1)
                    dve.wait_ge(s_v, NV * step + 2)
                    dve.tensor_scalar(penalty[:], keep[:], 1.0, 1e9, ALU.subtract, ALU.mult).then_inc(s_v, 1)
                    dve.tensor_tensor(kept[:], logits[:], keep[:], ALU.mult).then_inc(s_v, 1)
                    dve.wait_ge(s_v, NV * step + 4)
                    dve.tensor_tensor(final[:], kept[:], penalty[:], ALU.add).then_inc(s_v, 1)
                    dve.wait_ge(s_v, NV * step + 5)
                    return final

                def work(b, g, h, f, c):
                    dve.wait_ge(s_zero, 1)
                    dve.wait_ge(s_mbc, c + 1)
                    dve.tensor_scalar(top[:], zero[:], -3e38, None, ALU.add).then_inc(s_top, 1)
                    with dve.Fori(0, KT) as j:
                        tile = masked(2 * KT * c + j)
                        dve.wait_ge(s_top, c + 1)
                        dve.tensor_tensor(top[:], top[:], tile[:], ALU.max).then_inc(s_max, 1)
                        dve.wait_ge(s_max, KT * c + j + 2)
                    with dve.Fori(0, KT) as j:
                        tile = masked(2 * KT * c + KT + j)
                        dve.wait_ge(s_mbc, c + 2)
                        dve.tensor_tensor(below[:], tile[:], top_bc[:], ALU.subtract).then_inc(s_below, 1)

                over_units(dve, work)

        @block.gpsimd
        def _(pool):
            taken = pool.value_load(flag, min_val=0, max_val=1)
            with pool.If(taken > 0):
                pool.memset(zero[:], 0.0).then_inc(s_zero, 1)
                pool.nop().then_inc(s_mbc, 1)
                for c in range(UNITS):
                    pool.wait_ge(s_max, KT * c + KT + 1)
                    pool.partition_all_reduce(top_bc[:], top[:], P, bass.bass_isa.ReduceOp.max).then_inc(s_mbc, 1)

        @block.scalar
        def _(act):
            taken = act.value_load(flag, min_val=0, max_val=1)
            with act.If(taken > 0):
                act.nop().then_inc(s_osb, 1)

                def work(b, g, h, f, c):
                    with act.Fori(0, KT) as j:
                        act.wait_ge(s_below, KT * c + j + 1)
                        act.activation(probs[:], below[:], ACT.Exp).then_inc(s_p, 1)
                    act.wait_ge(s_pv, KT * c + KT + 1)
                    act.wait_ge(s_st, 32 * c + 32)
                    act.activation(o_sb[:], o_ps[0:W, :], ACT.Copy).then_inc(s_osb, 1)
                    act.activation(den_sb[:], den_ps[0:32, :], ACT.Copy).then_inc(s_osb, 1)

                over_units(act, work)


def cross_flag(nc, ctx, sem, flag_data):
    norm2_q, norm2_k, mask_min, flags = flag_data

    def sb(name, shape):
        return ctx.enter_context(nc.sbuf_tensor("f_" + name, shape, F32))

    top_q, top_k, prod = (sb(k, [P, B, GROUPS]) for k in ("top_q", "top_k", "prod"))
    low = sb("low", [P, 1])
    worst = sb("worst", [P, 2])
    worst_all = sb("worst_all", [P, 2])
    over = sb("over", [P, 2])
    s_red, s_worst, s_all, s_over, s_flag = sem("f_red"), sem("f_worst"), sem("f_all"), sem("f_over"), sem("f_flag")

    def vector(dve):
        dve.tensor_reduce(top_q[:], norm2_q[:].rearrange("p b c g -> p b g c"), AX_X, ALU.max).then_inc(s_red, 1)
        dve.tensor_reduce(top_k[:], norm2_k[:].rearrange("p b c g -> p b g c"), AX_X, ALU.max).then_inc(s_red, 1)
        dve.tensor_reduce(low[:], mask_min[:].rearrange("p i n -> p (i n)"), AX_X, ALU.min).then_inc(s_red, 1)
        dve.wait_ge(s_red, 3)
        dve.tensor_tensor(prod[:], top_q[:], top_k[:], ALU.mult).then_inc(s_red, 1)
        dve.tensor_scalar(worst[:, 1:2], low[:], 0.5, None, ALU.is_lt).then_inc(s_worst, 1)
        dve.wait_ge(s_red, 4)
        dve.tensor_reduce(worst[:, 0:1], prod[:].rearrange("p b g -> p (b g)"), AX_X, ALU.max).then_inc(s_worst, 1)
        dve.wait_ge(s_all, 1)
        dve.tensor_scalar(over[:, 0:1], worst_all[:, 0:1], (SAFE * DK ** 0.5) ** 2, None, ALU.is_gt).then_inc(s_over, 1)
        dve.wait_ge(s_over, 1)
        dve.tensor_tensor(over[:, 1:2], over[:, 0:1], worst_all[:, 1:2], ALU.add).then_inc(s_over, 1)
        dve.wait_ge(s_over, 2)
        dve.tensor_scalar(flags[:, 1:2], over[:, 1:2], 0.5, None, ALU.is_gt).then_inc(s_flag, 1)

    def gpsimd(pool):
        pool.wait_ge(s_worst, 2)
        pool.partition_all_reduce(worst_all[:], worst[:], P, bass.bass_isa.ReduceOp.max).then_inc(s_all, 1)

    return vector, gpsimd, s_flag


def context_projections(nc, sem, ctxT, mask, xwkvT, k2_dram, v2_dram, ones_block, norm2_k, mask_min,
                        sum_dram, rsum_dram, ahead_dram, ahead):
    CH = L // HALF
    with ExitStack() as ctx:
        def sb(name, shape, dt=F32):
            return ctx.enter_context(nc.sbuf_tensor(name, shape, dt))

        w_raw = sb("c_wraw", [P, 2, DC, D])
        w_hi = sb("c_whi", [P, 2, DC, D], F32R)
        w_lo = sb("c_wlo", [P, 2, DC, D], F32R)
        c_raw = [sb(f"c_raw{i}", [P, DC, HALF]) for i in range(2)]
        c_hi = [sb(f"c_hi{i}", [P, DC, HALF], F32R) for i in range(2)]
        c_lo = [sb(f"c_lo{i}", [P, DC, HALF], F32R) for i in range(2)]
        k_hi = sb("c_khi", [P, GROUPS, HALF], F32R)
        k_lo = sb("c_klo", [P, GROUPS, HALF], F32R)
        v_sb = sb("c_v", [P, 4, D])
        k_sq = sb("c_ksq", [P, 2, HALF], F32R)
        CHUNKS = B * CH
        MP = mask_min.shape[1]
        mask_rows = mask.rearrange("b l t -> (b l t)").rearrange("(n i p v) -> i n p v", n=CHUNKS, i=MP, p=P)
        mask_sb = [sb(f"c_mask{i}", [P, B * L * N // (MP * CHUNKS * P)], mybir.dt.int32) for i in range(2)]
        den = sb("c_den", [P, SUMS])
        rden = sb("c_rden", [P, SUMS])
        SHARE = (EC + DC) // CH
        ahead_raw = sb("c_ahead", [P, SHARE, D])
        ahead_rows = ahead_dram.rearrange("(n c q) e -> n q c e", q=P, c=SHARE)
        ps = [ctx.enter_context(nc.psum_tensor(f"c_ps{i}", [P, HALF], F32)) for i in range(8)]

        s_w = [sem(f"c_w{i}") for i in range(2)]
        s_whi, s_wlo = sem("c_whi"), sem("c_wlo")
        s_raw = [sem(f"c_raw{i}") for i in range(2)]
        s_hi, s_lo = sem("c_hi"), sem("c_lo")
        s_mm = sem("c_mm")
        s_khi, s_klo, s_v = sem("c_khi"), sem("c_klo"), sem("c_v")
        s_kst, s_vst = sem("c_kst"), sem("c_vst")
        s_ksq = sem("c_ksq")
        s_norm, s_top = sem("c_norm"), sem("c_top")
        s_mask = [sem(f"c_mask{i}") for i in range(2)]
        s_min = sem("c_min")
        s_den, s_rden, s_rst = sem("c_den"), sem("c_rden"), sem("c_rst")
        s_ahead, s_ahi, s_alo = sem("c_ahead"), sem("c_ahi"), sem("c_alo")
        block = ctx.enter_context(nc.Block())


        @block.sync
        def _(sp):
            def load_mask(jc, b, n, i):
                sp.wait_ge(s_min, MP * n + i + 1)
                at = B * jc + b if i + 2 < MP else B * jc + 1 if b == 0 else B * ((jc + 1) % CH)
                sp.dma_start(mask_sb[i % 2][:], mask_rows[(i + 2) % MP, at]).then_inc(s_mask[i % 2], 16)

            sp.nop().then_inc(s_kst, 128)
            sp.nop().then_inc(s_vst, 64)
            for i in range(2):
                sp.dma_start(w_raw[:, i], xwkvT[i].rearrange("(c q) e -> q c e", q=P)).then_inc(s_w[i], 16)
                sp.dma_start(c_raw[i][:], ctxT[i, 0].rearrange("(c q) t -> q c t", q=P)).then_inc(s_raw[i], 16)
            for i in range(2):
                sp.dma_start(mask_sb[i][:], mask_rows[i, 0]).then_inc(s_mask[i], 16)
            sp.dma_start(den[:], by_partition(sum_dram)).then_inc(s_den, 16)
            sp.wait_ge(s_rden, 1)
            sp.dma_start(by_partition(rsum_dram), rden[:]).then_inc(s_rst, 16)
            with sp.Fori(0, CH) as jc:
                for b in range(B):
                    n = B * jc + b
                    sp.wait_ge(s_hi, n + 1)
                    sp.wait_ge(s_lo, n + 1)
                    sp.dma_start(c_raw[b][:], ctxT[b, (jc + 1) % CH].rearrange("(c q) t -> q c t", q=P))\
                        .then_inc(s_raw[b], 16)
                    load_mask(jc, b, n, 0)
                    load_mask(jc, b, n, 1)
                    if b == 0:
                        sp.wait_ge(s_alo, jc + 1)
                        sp.dma_start(ahead_raw[:], ahead_rows[jc]).then_inc(s_ahead, 16)
                    sp.wait_ge(s_klo, GROUPS * n + GROUPS)
                    for g in range(GROUPS):
                        for i, part in enumerate((k_hi, k_lo)):
                            sp.dma_start(k2_dram[GROUPS * b + g, :, i, :, bass.ds(jc * HALF, HALF)],
                                         words(part[:, g, :])).then_inc(s_kst, 16)
                    load_mask(jc, b, n, 2)
                    load_mask(jc, b, n, 3)
                    sp.wait_ge(s_v, 4 * n + 8)
                    for t in range(4):
                        sp.dma_start(v2_dram[GROUPS * b:GROUPS * (b + 1)].rearrange("g q t e -> t q g e")[4 * jc + t],
                                     v_sb[:, t, :].rearrange("p (g e) -> p g e", e=P)).then_inc(s_vst, 16)
            sp.wait_ge(s_kst, 128 + 128 * B * CH)
            sp.wait_ge(s_vst, 64 + 64 * B * CH)
            for b in range(B):
                sp.wait_ge(s_raw[b], 16 * (CH + 1))
            for i in range(2):
                sp.wait_ge(s_mask[i], 16 * (MP // 2 * CHUNKS + 1))
            sp.wait_ge(s_rst, 16)

        @block.scalar
        def _(act):
            act.nop().then_inc(s_v, 4)
            act.nop().then_inc(s_top, GROUPS)
            act.nop().then_inc(s_norm, GROUPS)
            for i in range(2):
                act.wait_ge(s_w[i], 16)
                act.activation(w_hi[:, i], w_raw[:, i], ACT.Copy).then_inc(s_whi, 1)
                if i == 0:
                    act.wait_ge(s_raw[0], 16)
                    act.activation(c_hi[0][:], c_raw[0][:], ACT.Copy).then_inc(s_hi, 1)
            with act.Fori(0, CH) as jc:
                for b in range(B):
                    n = B * jc + b
                    act.wait_ge(s_raw[1 - b], 16 * jc + 16 + 16 * b)
                    act.wait_ge(s_mm, 8 * n + 16)
                    act.activation(c_hi[1 - b][:], c_raw[1 - b][:], ACT.Copy).then_inc(s_hi, 1)
                    act.wait_ge(s_kst, 128 * n + 128)
                    for g in range(GROUPS):
                        act.wait_ge(s_mm, 8 * n + g + 17)
                        act.activation(k_hi[:, g, :], ps[g][:], ACT.Copy).then_inc(s_khi, 1)
                    for g in range(GROUPS):
                        act.wait_ge(s_norm, GROUPS * n + g - 1 + GROUPS)
                        act.wait_ge(s_khi, GROUPS * n + g + 1)
                        act.activation(k_sq[:, g % 2, :], words(k_hi[:, g, :]), ACT.Square).then_inc(s_ksq, 1)
                    act.wait_ge(s_vst, 64 * n + 64)
                    for t in range(4):
                        act.wait_ge(s_mm, 8 * n + 4 + t + 17)
                        act.activation(v_sb[:, t, :], ps[4 + t][:], ACT.Copy).then_inc(s_v, 1)
                    if b == 0:
                        act.wait_ge(s_ahead, 16 * jc + 16)
                        act.activation(ahead[0][:, bass.ds(SHARE * jc, SHARE), :], ahead_raw[:], ACT.Copy).then_inc(s_ahi, 1)

        @block.vector
        def _(dve):
            def mask_minimum(n, i):
                dve.wait_ge(s_mask[i % 2], 8 * MP * n + 16 * (i // 2) + 16)
                dve.tensor_reduce(mask_min[:, i, bass.ds(n, 1)], mask_sb[i % 2][:].bitcast(mybir.dt.uint32), AX_X,
                                  ALU.min).then_inc(s_min, 1)

            dve.nop().then_inc(s_alo, 1)
            for i in range(2):
                dve.wait_ge(s_whi, i + 1)
                dve.tensor_tensor(w_lo[:, i], w_raw[:, i], w_hi[:, i].bitcast(F32), ALU.subtract).then_inc(s_wlo, 1)
                if i == 0:
                    dve.wait_ge(s_hi, 1)
                    dve.tensor_tensor(c_lo[0][:], c_raw[0][:], c_hi[0][:].bitcast(F32), ALU.subtract).then_inc(s_lo, 1)
            dve.wait_ge(s_den, 16)
            dve.reciprocal(rden[:], den[:]).then_inc(s_rden, 1)
            with dve.Fori(0, CH) as jc:
                for b in range(B):
                    n = B * jc + b
                    dve.wait_ge(s_hi, n + 2)
                    dve.tensor_tensor(c_lo[1 - b][:], c_raw[1 - b][:], c_hi[1 - b][:].bitcast(F32),
                                      ALU.subtract).then_inc(s_lo, 1)
                    mask_minimum(n, 0)
                    mask_minimum(n, 1)
                    dve.wait_ge(s_kst, 128 * n + 128)
                    for g in range(GROUPS):
                        dve.wait_ge(s_khi, GROUPS * n + g + 1)
                        dve.tensor_tensor(k_lo[:, g, :], ps[g][:], k_hi[:, g, :].bitcast(F32),
                                          ALU.subtract).then_inc(s_klo, 1)
                    for g in range(GROUPS):
                        dve.wait_ge(s_norm, GROUPS * n + g + 1 + GROUPS)
                        dve.tensor_reduce(norm2_k[:, b, bass.ds(jc, 1), g], ps[g][:], AX_X, ALU.max).then_inc(s_top, 1)
                    if b == 0:
                        dve.wait_ge(s_ahi, jc + 1)
                        dve.tensor_tensor(ahead[1][:, bass.ds(SHARE * jc, SHARE), :], ahead_raw[:],
                                          words(ahead[0][:, bass.ds(SHARE * jc, SHARE), :]), ALU.subtract).then_inc(s_alo, 1)
                    mask_minimum(n, 2)
                    mask_minimum(n, 3)

        @block.tensor
        def _(pe):
            pe.nop().then_inc(s_mm, 16)
            pe.wait_ge(s_whi, 1)
            pe.wait_ge(s_wlo, 1)
            with pe.Fori(0, CH) as jc:
                for b in range(B):
                    n = B * jc + b
                    pe.wait_ge(s_hi, n + 1)
                    pe.wait_ge(s_lo, n + 1)
                    for g in range(GROUPS):
                        pe.wait_ge(s_top, GROUPS * n + g + 1)
                        e = slice(g * P, (g + 1) * P)
                        for c in range(DC):
                            pe.matmul(ps[g][:], w_hi[:, 0, c, e], c_hi[b][:, c, :], start=(c == 0), stop=False)
                            pe.matmul(ps[g][:], w_hi[:, 0, c, e], c_lo[b][:, c, :], start=False, stop=False)
                            last = pe.matmul(ps[g][:], w_lo[:, 0, c, e], c_hi[b][:, c, :], start=False, stop=(c == DC - 1))
                        last.then_inc(s_mm, 1)
                    pe.wait_ge(s_wlo, 2)
                    for t in range(4):
                        pe.wait_ge(s_v, 4 * n + t + 1)
                        tok = slice(t * P, (t + 1) * P)
                        for c in range(DC):
                            pe.matmul(ps[4 + t][:], c_hi[b][:, c, tok], w_hi[:, 1, c, :], start=(c == 0), stop=False)
                            pe.matmul(ps[4 + t][:], c_hi[b][:, c, tok], w_lo[:, 1, c, :], start=False, stop=False)
                            last = pe.matmul(ps[4 + t][:], c_lo[b][:, c, tok], w_hi[:, 1, c, :], start=False,
                                             stop=(c == DC - 1))
                        last.then_inc(s_mm, 1)
                        if t == 1:
                            pe.wait_ge(s_klo, GROUPS * n + GROUPS)
                            for g in range(GROUPS):
                                pe.wait_ge(s_ksq, GROUPS * n + g + 1)
                                pe.matmul(ps[g][:], ones_block[:], k_sq[:, g % 2, :], start=True, stop=True).then_inc(s_norm, 1)


def cross_attention(nc, sem, q2_dram, k2_dram, v2_dram, attn2T_dram, sum2_dram, ones,
                    flag_data, ffn_drams, ffn_tiles, s_ffn):
    with ExitStack() as ctx:
        def sb(name, shape, dt=F32):
            return ctx.enter_context(nc.sbuf_tensor(name, shape, dt))

        k_st = [[sb(f"d_k{i}{h}", [P, L], F32R) for h in range(4)] for i in range(2)]
        q_st = [[sb(f"d_q{i}{h}", [P, N], F32R) for h in range(4)] for i in range(2)]
        v_sb = [sb(f"d_v{i}", [P, JT, P]) for i in range(2)]
        NP = 4
        probs = [sb(f"d_p{i}", [P, 4 * HALF]) for i in range(NP)]
        acc = [sb(f"d_acc{f}", [P, 4 * HALF]) for f in range(NH)]
        o_sb = [sb(f"d_o{f}", [P, HALF]) for f in range(NH)]
        den_sb = [sb(f"d_den{f}", [P, HALF]) for f in range(NH)]
        NS = 3
        sc_ps = [ctx.enter_context(nc.psum_tensor(f"d_sc{i}", [P, 2 * HALF], F32)) for i in range(NS)]
        o_ps = ctx.enter_context(nc.psum_tensor("d_ops", [P, HALF], F32))
        den_ps = ctx.enter_context(nc.psum_tensor("d_dps", [P, HALF], F32))

        s_in = [[sem(f"d_in{i}{k}") for k in range(3)] for i in range(2)]
        s_sc, s_pr, s_pv = sem("d_sc"), sem("d_pr"), sem("d_pv")
        s_pd = sem("d_pd")
        s_acc, s_den = sem("d_acc"), sem("d_den")
        s_osb, s_dsb = sem("d_osb"), sem("d_dsb")
        s_b2z = sem("d_b2z")
        s_ost, s_dst = ([sem(f"d_{k}{f}") for f in range(NH)] for k in ("ost", "dst"))
        flag_on_dve, flag_on_pool, s_flag = cross_flag(nc, ctx, sem, flag_data)
        block = ctx.enter_context(nc.Block())

        ITS, STEPS = B * GROUPS, NH * JT
        LOADS = 16 * 2 * 3
        on_pe = [7, 13]
        on_dve = [j for j in range(1, JT) if j not in on_pe]
        ADDS = 2 * len(on_dve)


        def exps_done(it, q):
            return NS + 2 * STEPS * it + q + 1

        def added(it, f, j, pair):
            return 2 * NP + NH * ADDS * it + ADDS * f + 2 * on_dve.index(max(j, 1)) + pair + 1

        @block.sync
        def _(sp):
            for f in range(NH):
                sp.nop().then_inc(s_ost[f], 16)
                sp.nop().then_inc(s_dst[f], 16)

            def load(it, par):
                for h in range(4):
                    for i in range(2):
                        sp.dma_start(words(k_st[par][h][64 * i:64 * i + 64, :]),
                                     k2_dram[it, h, i].unsqueeze(0).to_broadcast([2, DK, L])).then_inc(s_in[par][h // 2], 16)
                    sp.dma_start(words(q_st[par][h][:]), q2_dram[it, h].rearrange("s q t -> (s q) t").unsqueeze(0)
                                 .to_broadcast([2, 2 * DK, N])).then_inc(s_in[par][h // 2], 16)
                sp.dma_start(v_sb[par][:], v2_dram[it]).then_inc(s_in[par][2], 16)

            def store(it, f):
                sp.wait_ge(s_osb, NH * it + f + 3)
                sp.dma_start(attn2T_dram.rearrange("b g q t -> (b g) q t")[it, :, f * HALF:(f + 1) * HALF],
                             o_sb[f][:]).then_inc(s_ost[f], 16)
                sp.wait_ge(s_dsb, NH * it + f + 3)
                sp.dma_start(sum2_dram.rearrange("b g h t -> (b g) h t")[it, :, f * HALF:(f + 1) * HALF],
                             den_sb[f][0:P:32, :]).then_inc(s_dst[f], 16)

            def body(i, last):
                for par in range(2):
                    it = 2 * i + par
                    store(it, 0)
                    store(it, 1)
                    if not last:
                        load(it + 2, par)

            load(0, 0)
            load(1, 1)
            load_ffn_constants(sp, ffn_drams, ffn_tiles, s_ffn, s_b2z)
            with sp.Fori(0, ITS // 2 - 1) as i:
                body(i, False)
            body(ITS // 2 - 1, True)
            for f in range(NH):
                sp.wait_ge(s_ost[f], 16 + 16 * ITS)
                sp.wait_ge(s_dst[f], 16 + 16 * ITS)

        @block.gpsimd
        def _(pool):
            pool.memset(ffn_tiles[3][:], 0.0).then_inc(s_b2z, 1)
            pool.wait_ge(s_b2z, 1)
            flag_on_pool(pool)

        @block.tensor
        def _(pe):
            pe.nop().then_inc(s_pv, NP)
            pe.nop().then_inc(s_pd, NH * len(on_pe))

            def scores(it, par, s, nth=None, first=False):
                f, j = divmod(s, JT)
                for pair in range(2):
                    if s == 0:
                        pe.wait_ge(s_in[par][pair], LOADS * nth)
                    q = 2 * s + pair
                    if q >= NS:
                        pe.wait_ge(s_pr, exps_done(it, q - NS))
                    elif not first:
                        pe.wait_ge(s_pr, exps_done(it - 1, max(r for r in range(2 * STEPS) if r % NS == q)))
                    for h in range(2):
                        last = pe.matmul(sc_ps[q % NS][:, h * HALF:(h + 1) * HALF],
                                         k_st[par][2 * pair + h][:, j * P:(j + 1) * P],
                                         q_st[par][2 * pair + h][:, f * HALF:(f + 1) * HALF], start=True, stop=True)
                    last.then_inc(s_sc, 1)

            def values(it, par, s, nth):
                f, j = divmod(s, JT)
                if s == 0:
                    pe.wait_ge(s_in[par][2], 16 * nth)
                pe.wait_ge(s_pr, exps_done(it, 2 * s + 1))
                if j == 0:
                    pe.wait_ge(s_osb, NH * it + f + 2)
                for h in range(4):
                    last = pe.matmul(o_ps[32 * h:32 * h + 32, :], v_sb[par][:, j, 32 * h:32 * h + 32],
                                     probs[s % NP][:, h * HALF:(h + 1) * HALF],
                                     start=(j == 0), stop=(j == JT - 1), skip_group_check=True)
                last.then_inc(s_pv, 1)
                if j in on_pe:
                    if j == on_pe[0]:
                        pe.wait_ge(s_dsb, NH * it + f + 2)
                    for h in range(4):
                        last = pe.matmul(den_ps[32 * h:32 * h + 32, :], ones[:], probs[s % NP][:, h * HALF:(h + 1) * HALF],
                                         start=(j == on_pe[0]), stop=False, skip_group_check=True)
                    last.then_inc(s_pd, 1)

            def sums(it, f):
                pe.wait_ge(s_acc, added(it, f, on_dve[-1], 1))
                for h in range(4):
                    last = pe.matmul(den_ps[32 * h:32 * h + 32, :], ones[:], acc[f][:, h * HALF:(h + 1) * HALF],
                                     start=False, stop=True, skip_group_check=True)
                last.then_inc(s_den, 1)

            def body(i, last):
                for par in range(2):
                    it = 2 * i + par
                    for s in range(1, STEPS):
                        scores(it, par, s)
                        values(it, par, s - 1, i + 1)
                        if s == JT + 1:
                            sums(it, 0)
                    if not (last and par == 1):
                        scores(it + 1, 1 - par, 0, nth=i + 1 + par)
                    values(it, par, STEPS - 1, i + 1)
                    sums(it, 1)

            scores(0, 0, 0, nth=1, first=True)
            with pe.Fori(0, ITS // 2 - 1) as i:
                body(i, False)
            body(ITS // 2 - 1, True)

        @block.scalar
        def _(act):
            act.nop().then_inc(s_pr, NS)

            def exps(it, s):
                f, j = divmod(s, JT)
                before = it if s >= NP else it - 1
                bf, bj = divmod((s - NP) % STEPS, JT)
                for pair in range(2):
                    q = 2 * s + pair
                    act.wait_ge(s_sc, 2 * STEPS * it + q + 1)
                    act.wait_ge(s_pv, STEPS * it + s + 1)
                    if bj in on_pe:
                        act.wait_ge(s_pd, NH * len(on_pe) * (before + 1) + len(on_pe) * bf + on_pe.index(bj) + 1)
                    else:
                        act.wait_ge(s_acc, added(before, bf, bj, pair))
                    act.activation(probs[s % NP][:, pair * 2 * HALF:(pair + 1) * 2 * HALF], sc_ps[q % NS][:],
                                   ACT.Exp, scale=DK ** -0.5).then_inc(s_pr, 1)

            with act.Fori(0, ITS) as it:
                for s in range(STEPS):
                    exps(it, s)

        @block.vector
        def _(dve):
            dve.nop().then_inc(s_acc, 2 * NP)
            dve.nop().then_inc(s_osb, 2)
            dve.nop().then_inc(s_dsb, 2)

            flag_on_dve(dve)

            def add(it, f, j):
                s = JT * f + j
                for pair in range(2):
                    cols = slice(pair * 2 * HALF, (pair + 1) * 2 * HALF)
                    dve.wait_ge(s_pr, exps_done(it, 2 * s + pair))
                    if j == 1:
                        dve.wait_ge(s_dsb, NH * it + f + 1)
                        dve.tensor_tensor(acc[f][:, cols], probs[(s - 1) % NP][:, cols], probs[s % NP][:, cols],
                                          ALU.add).then_inc(s_acc, 1)
                    else:
                        dve.wait_ge(s_acc, added(it, f, on_dve[on_dve.index(j) - 1], pair))
                        dve.tensor_tensor(acc[f][:, cols], acc[f][:, cols], probs[s % NP][:, cols],
                                          ALU.add).then_inc(s_acc, 1)

            def collect(it, f):
                dve.wait_ge(s_pv, STEPS * it + JT * (f + 1) + NP)
                dve.wait_ge(s_ost[f], 16 * (it + 1))
                dve.tensor_copy(o_sb[f][:], o_ps[:]).then_inc(s_osb, 1)

            def collect_sums(it, f):
                dve.wait_ge(s_den, NH * it + f + 1)
                dve.wait_ge(s_dst[f], 16 * (it + 1))
                dve.tensor_copy(den_sb[f][:], den_ps[:]).then_inc(s_dsb, 1)

            with dve.Fori(0, ITS) as it:
                for j in on_dve:
                    add(it, 0, j)
                collect(it, 0)
                add(it, 1, on_dve[0])
                collect_sums(it, 0)
                for j in on_dve[1:]:
                    add(it, 1, j)
                collect(it, 1)
                collect_sums(it, 1)
            dve.wait_ge(s_flag, 1)


def output_projection(nc, sem, tag, attn_dram, sum_dram, rsum_dram, w, bias, res_dram, keep_dram, ident, query=None, ffn=None):
    C, HP = rsum_dram.shape[1], rsum_dram.shape[2]
    W = P // HP
    CH = N // HALF
    CHUNKS = B * CH
    TC = HALF // P
    NY = 1 if ffn is None else 3
    with ExitStack() as ctx:
        def sb(name, shape, dt=F32):
            return ctx.enter_context(nc.sbuf_tensor(tag + name, shape, dt))

        w_hi, w_lo = w
        o_raw = sb("oraw", [P, C, HALF])
        r_bc = sb("rbc", [P, C, HALF])
        NO = 1 if ffn is None else 2
        o_hi = [sb(f"ohi{i}", [P, C, HALF], F32R) for i in range(NO)]
        o_lo = [sb(f"olo{i}", [P, C, HALF], F32R) for i in range(NO)]
        res = sb("res", [P, TC, D])
        y = sb("y", [P, NY, TC, D])
        xn = sb("xn", [P, TC, D])
        stats = sb("stats", [P, TC, 6])
        mv = sb("mv", [P, TC, 2])
        var = sb("var", [P, TC])
        rstd = sb("rstd", [P, TC])
        mhalf = sb("mhalf", [P, TC])
        xT_hi = sb("xThi", [P, DC, HALF], F32R)
        xT_lo = sb("xTlo", [P, DC, HALF], F32R)
        o_ps = [ctx.enter_context(nc.psum_tensor(f"{tag}o_ps{i}", [P, HALF], F32)) for i in range(TC)]
        t_ps = [ctx.enter_context(nc.psum_tensor(f"{tag}t_ps{i}", [P, HALF], F32)) for i in range(2)]
        z_ps = [ctx.enter_context(nc.psum_tensor(f"{tag}z_ps{i}", [P, HALF], F32)) for i in range(2)]
        if sum_dram is not None:
            den = sb("den", [P, SUMS])
            rden = sb("rden", [P, SUMS])
        if bias is not None:
            bias_bc = sb("bias", [P, D])
        if query is not None:
            (wq_hi, wq_lo), q2_dram, ones_block, norm2_q, ahead_dram, ahead = query
            ahead_raw = sb("ahead", [P, DC, D])
            q_hi = sb("qhi", [P, GROUPS, HALF], F32R)
            q_lo = sb("qlo", [P, GROUPS, HALF], F32R)
            q_sq = sb("qsq", [P, 2, HALF], F32R)
        else:
            (wi_raw, small, bin_sb, b2_sb, wo2, bout_bc), s_small, out = ffn
            HH = HID // 2
            NR = 4
            wi_hi = sb("wihi", [P, DC, P], F32R)
            wi_lo = sb("wilo", [P, DC, P], F32R)
            s_sb = sb("ssb", [P, HALF])
            relu = sb("relu", [P, NR, HALF])
            g_sb = sb("gsb", [P, 2, HALF])
            fin = sb("fin", [P, 2, D])

        turned = t_ps + z_ps

        def s(name):
            return sem(tag + "_" + name)

        s_den, s_rden, s_rst = s("den"), s("rden"), s("rst")
        s_bias, s_mhalf = s("bias"), s("mhalf")
        s_o = [s(f"o{i}") for i in range(2)]
        s_rb = [s(f"rb{i}") for i in range(2)]
        s_res = s("res")
        s_resb = s("resb")
        s_div, s_divp = s("div"), s("divp")
        s_hi, s_lo = s("hi"), s("lo")
        s_mm = s("mm")
        s_y, s_yst = s("y"), s("yst")
        s_st, s_ag, s_var, s_rstd = s("st"), s("ag"), s("var"), s("rstd")
        s_xn, s_tr, s_thi, s_tlo = s("xn"), s("tr"), s("thi"), s("tlo")
        s_z = s("z")
        if query is not None:
            s_qhi, s_qlo, s_qst = s("qhi"), s("qlo"), s("qst")
            s_ahead, s_ahi = s("ahead"), s("ahi")
            s_qsq, s_norm, s_top = s("qsq"), s("norm"), s("top")
        else:
            s_wi = s("wi")
            s_s, s_relu, s_g = s("s"), s("relu"), s("g")
            s_f, s_yb, s_fin, s_fst = s("f"), s("yb"), s("fin"), [s("fst0"), s("fst1")]
        block = ctx.enter_context(nc.Block())

        def part(k):
            return slice(k * HALF // 2, (k + 1) * HALF // 2)

        def divide(eng, n, k):
            eng.wait_ge(s_o[k], 16 * (n + 1))
            eng.wait_ge(s_rb[k], 16 * HP * (n + 1))
            eng.tensor_tensor(o_raw[:, :, part(k)], o_raw[:, :, part(k)], r_bc[:, :, part(k)], ALU.mult)\
                .then_inc(s_div if n == 0 else s_divp, 1)

        def wait_divided(eng, n, k):
            if n == 0:
                eng.wait_ge(s_div, k + 1)
            else:
                eng.wait_ge(s_divp, 2 * (n - 1) + k + 1)

        def tokens(dram, n):
            return dram[n // CH].rearrange("(c t q) d -> c q t d", q=P, t=TC)[n % CH]

        @block.sync
        def _(sp):
            def load_sums(n, k):
                for h in range(HP):
                    sp.dma_start(r_bc[h * W:(h + 1) * W, :, part(k)],
                                 rsum_dram[n // CH].rearrange("c h t -> h c t")[h]
                                 .rearrange("c (n t) -> c n t", n=2 * CH)[:, n % CH * 2 + k, :]
                                 .unsqueeze(0).to_broadcast([W, C, HALF // 2])).then_inc(s_rb[k], 16)

            def load_outputs(n, k):
                sp.dma_start(o_raw[:, :, part(k)], attn_dram[n // CH].rearrange("c q t -> q c t")
                             .rearrange("q c (n t) -> q c n t", n=2 * CH)[:, :, n % CH * 2 + k, :]).then_inc(s_o[k], 16)

            def store_queries(n):
                for g in range(GROUPS):
                    sp.wait_ge(s_qlo, GROUPS * n + g + 1)
                    for i, part in enumerate((q_hi, q_lo)):
                        sp.dma_start(q2_dram.rearrange("(b g) h s q t -> b g h s q t", g=GROUPS)
                                     [n // CH, g, :, i, :, n % CH * HALF:(n % CH + 1) * HALF],
                                     words(part[:, g, :])).then_inc(s_qst, 16)

            def store_result(n):
                for t in range(TC):
                    sp.wait_ge(s_fin, TC * n + t + 1)
                    sp.dma_start(tokens(out, n)[:, t, :], fin[:, t % 2, :]).then_inc(s_fst[t % 2], 16)

            if sum_dram is not None:
                sp.dma_start(den[:], by_partition(sum_dram)).then_inc(s_den, 16)
            load_outputs(0, 0)
            if sum_dram is not None:
                sp.wait_ge(s_rden, 1)
                sp.dma_start(by_partition(rsum_dram), rden[:]).then_inc(s_rst, 16)
                load_outputs(0, 1)
                sp.wait_ge(s_rst, 16)
                load_sums(0, 0)
                load_sums(0, 1)
                sp.dma_start(res[:], tokens(res_dram, 0)).then_inc(s_res, 16)
            else:
                load_sums(0, 0)
                load_outputs(0, 1)
                load_sums(0, 1)
                sp.dma_start(res[:], tokens(res_dram, 0)).then_inc(s_res, 16)
            if bias is not None:
                sp.dma_start(bias_bc[:], bias.partition_broadcast(P)).then_inc(s_bias, 16)
            if query is not None:
                sp.dma_start(ahead_raw[:], ahead_dram.rearrange("(c q) e -> q c e", q=P)).then_inc(s_ahead, 16)
            for n in range(CHUNKS + 2):
                if n + 1 < CHUNKS:
                    for k in range(2):
                        wait_divided(sp, n, k)
                        load_sums(n + 1, k)
                        sp.wait_ge(s_lo, 2 * n + k + 1)
                        load_outputs(n + 1, k)
                if ffn is not None and n >= 2:
                    store_result(n - 2)
                if n < CHUNKS:
                    sp.wait_ge(s_y, TC * (n + 1))
                    if n + 1 < CHUNKS:
                        sp.dma_start(res[:], tokens(res_dram, n + 1)).then_inc(s_res, 16)
                    if keep_dram is not None:
                        sp.dma_start(tokens(keep_dram, n), y[:, 0]).then_inc(s_yst, 16)
                if query is not None and 1 <= n <= CHUNKS:
                    store_queries(n - 1)
            if keep_dram is not None:
                sp.wait_ge(s_yst, 16 * CHUNKS)
            if query is not None:
                sp.wait_ge(s_qst, 16 * 2 * GROUPS * CHUNKS)
            else:
                for i in range(2):
                    sp.wait_ge(s_fst[i], 8 * TC * CHUNKS)

        @block.gpsimd
        def _(pool):
            pool.memset(mhalf[:], -0.5).then_inc(s_mhalf, 1)
            pool.wait_ge(s_mhalf, 1)
            for n in range(CHUNKS):
                if bias is not None:
                    pool.wait_ge(s_bias, 16)
                    pool.wait_ge(s_res, 16 * (n + 1))
                    pool.tensor_tensor(res[:], res[:], bias_bc[:].unsqueeze(1).to_broadcast([P, TC, D]), ALU.add)\
                        .then_inc(s_resb, 1)
                    pool.wait_ge(s_resb, n + 1)
                if n + 1 < CHUNKS:
                    for k in range(2):
                        divide(pool, n + 1, k)
                        wait_divided(pool, n + 1, k)
                pool.wait_ge(s_var, n + 1)
                pool.tensor_tensor(rstd[:], var[:], mhalf[:], ALU.pow).then_inc(s_rstd, 1)
                if ffn is not None:
                    pool.wait_ge(s_small, FFN_LOADS)
                    pool.wait_ge(s_rstd, n + 1)
                    pool.wait_ge(s_xn, TC * (n + 1))
                    pool.tensor_tensor(y[:, n % NY], y[:, n % NY], bout_bc[:].unsqueeze(1).to_broadcast([P, TC, D]),
                                       ALU.add).then_inc(s_yb, 1)
                    pool.wait_ge(s_yb, n + 1)

        @block.vector
        def _(dve):
            def low(n, k):
                dve.wait_ge(s_hi, 2 * n + k + 1)
                dve.tensor_tensor(o_lo[n % NO][:, :, part(k)], o_raw[:, :, part(k)], words(o_hi[n % NO][:, :, part(k)]),
                                  ALU.subtract)\
                    .then_inc(s_lo, 1)

            def residual(n, t):
                if t == 0:
                    if bias is not None:
                        dve.wait_ge(s_resb, n + 1)
                    else:
                        dve.wait_ge(s_res, 16 * (n + 1))
                    if keep_dram is not None and n >= 1:
                        dve.wait_ge(s_yst, 16 * n)
                    if n >= 1:
                        dve.wait_ge(s_xn, TC * n)
                    if ffn is not None and n >= NY:
                        dve.wait_ge(s_fin, TC * (n - NY + 1))
                dve.wait_ge(s_mm, TC * n + t + 1)
                dve.tensor_tensor(y[:, n % NY, t, :], o_ps[t][:], res[:, t, :], ALU.add).then_inc(s_y, 1)
                dve.wait_ge(s_y, TC * n + t + 1)
                dve.bn_stats(stats[:, t, :], y[:, n % NY, t, :]).then_inc(s_st, 1)
                dve.wait_ge(s_st, TC * n + t + 1)
                dve.bn_aggr(mv[:, t, :], stats[:, t, :]).then_inc(s_ag, 1)

            def variance(n):
                dve.wait_ge(s_ag, TC * (n + 1))
                dve.tensor_scalar(var[:], mv[:, :, 1], LN_EPS, None, ALU.add).then_inc(s_var, 1)

            def normalise(n):
                dve.wait_ge(s_rstd, n + 1)
                if n >= 1:
                    dve.wait_ge(s_tr, TC * n)
                for t in range(TC):
                    dve.tensor_scalar(xn[:, t, :], y[:, n % NY, t, :], mv[:, t, 0:1], rstd[:, t:t + 1],
                                      ALU.subtract, ALU.mult).then_inc(s_xn, 1)

            def low_transposed(n):
                for t in range(TC):
                    dve.wait_ge(s_thi, TC * n + t + 1)
                    cols = slice(t * P, (t + 1) * P)
                    dve.tensor_tensor(xT_lo[:, :, cols], turned[t][:].rearrange("p (c t) -> p c t", c=DC),
                                      xT_hi[:, :, cols].bitcast(F32), ALU.subtract).then_inc(s_tlo, 1)

            def low_queries(n, g):
                if g == 0 and n >= 1:
                    dve.wait_ge(s_qst, 16 * 2 * GROUPS * n)
                dve.wait_ge(s_qhi, GROUPS * n + g + 1)
                dve.tensor_tensor(q_lo[:, g, :], z_ps[g % 2][:], q_hi[:, g, :].bitcast(F32),
                                  ALU.subtract).then_inc(s_qlo, 1)

            def top_norm(n, g):
                dve.wait_ge(s_norm, GROUPS * n + g + 1)
                dve.tensor_reduce(norm2_q[:, n // CH, n % CH, g:g + 1], t_ps[g % 2][:], AX_X, ALU.max).then_inc(s_top, 1)

            def units_in(n):
                dve.wait_ge(s_small, FFN_LOADS)
                dve.wait_ge(s_z, n + 1)
                if n >= 1:
                    dve.wait_ge(s_relu, HH * n)
                dve.tensor_scalar(s_sb[:], z_ps[0][:], bin_sb[:, 0:1], None, ALU.add).then_inc(s_s, 1)

            def units_out(n):
                if n >= 2:
                    dve.wait_ge(s_f, TC * (n - 1))
                g = g_sb[:, n % 2, :]
                for j in range(HH):
                    dve.wait_ge(s_relu, HH * n + j + 1)
                    if j == 0:
                        dve.tensor_scalar(g, relu[:, 0, :], small[:, 2 * HH:2 * HH + 1], b2_sb[:, 0:1],
                                          ALU.mult, ALU.add).then_inc(s_g, 1)
                    else:
                        dve.wait_ge(s_g, HH * n + j)
                        dve.scalar_tensor_tensor(out=g, in0=relu[:, j % NR, :],
                                                 scalar=small[:, 2 * HH + j:2 * HH + j + 1], in1=g,
                                                 op0=ALU.mult, op1=ALU.add).then_inc(s_g, 1)

            def result(n, t):
                dve.wait_ge(s_yb, n + 1)
                dve.wait_ge(s_f, TC * n + t + 1)
                stores = n * TC // 2 + t // 2
                if stores:
                    dve.wait_ge(s_fst[t % 2], 16 * stores)
                dve.tensor_tensor(fin[:, t % 2, :], z_ps[(t + 1) % 2][:], y[:, n % NY, t, :], ALU.add)\
                    .then_inc(s_fin, 1)

            if sum_dram is not None:
                dve.wait_ge(s_den, 16)
                dve.reciprocal(rden[:], den[:]).then_inc(s_rden, 1)
            for k in range(2):
                divide(dve, 0, k)
                low(0, k)
            if query is not None:
                dve.wait_ge(s_ahi, 1)
                dve.tensor_tensor(ahead[1][:], ahead_raw[:], words(ahead[0][:]), ALU.subtract)
            if ffn is not None:
                dve.wait_ge(s_wi, 1)
                dve.tensor_tensor(wi_lo[:], wi_raw[:], wi_hi[:].bitcast(F32), ALU.subtract).then_inc(s_wi, 1)
            for n in range(CHUNKS + 2):
                if n < CHUNKS:
                    for t in range(TC):
                        residual(n, t)
                        if t == 1 and n >= 1:
                            low_transposed(n - 1)
                        if ffn is not None and t == 2 and n + 1 < CHUNKS:
                            low(n + 1, 0)
                            low(n + 1, 1)
                        if ffn is not None and n >= 2 and t >= 2:
                            result(n - 2, 2 * t - 4)
                            result(n - 2, 2 * t - 3)
                        if t == 0 and ffn is None and n >= 2:
                            top_norm(n - 2, 2)
                            top_norm(n - 2, 3)
                    variance(n)
                elif ffn is None:
                    for g in range(2, GROUPS):
                        top_norm(n - 2, g)
                elif n > CHUNKS:
                    for t in range(TC):
                        result(n - 2, t)
                if n == CHUNKS:
                    low_transposed(n - 1)
                if 1 <= n <= CHUNKS:
                    if ffn is None:
                        low_queries(n - 1, 0)
                    else:
                        units_in(n - 1)
                        if n == CHUNKS:
                            for t in range(TC):
                                result(n - 2, t)
                if ffn is None and n + 1 < CHUNKS:
                    low(n + 1, 0)
                    low(n + 1, 1)
                if 1 <= n <= CHUNKS:
                    if ffn is None:
                        for g in range(1, GROUPS):
                            low_queries(n - 1, g)
                    else:
                        if n < CHUNKS:
                            normalise(n)
                        units_out(n - 1)
                if n < CHUNKS and (ffn is None or n == 0):
                    normalise(n)
                if ffn is None and 1 <= n <= CHUNKS:
                    for g in range(2):
                        top_norm(n - 1, g)

        @block.scalar
        def _(act):
            def high(n):
                for k in range(2):
                    wait_divided(act, n, k)
                    if n >= NO:
                        act.wait_ge(s_mm, TC * (n - NO + 1))
                    act.activation(o_hi[n % NO][:, :, part(k)], o_raw[:, :, part(k)], ACT.Copy).then_inc(s_hi, 1)

            def high_transposed(n):
                for t in range(TC):
                    act.wait_ge(s_tr, TC * n + t + 1)
                    act.activation(xT_hi[:, :, t * P:(t + 1) * P],
                                   turned[t][:].rearrange("p (c t) -> p c t", c=DC), ACT.Copy).then_inc(s_thi, 1)

            def high_queries(n):
                if n >= 1:
                    act.wait_ge(s_qst, 16 * 2 * GROUPS * n)
                for g in range(GROUPS):
                    act.wait_ge(s_z, GROUPS * n + g + 1)
                    act.activation(q_hi[:, g, :], z_ps[g % 2][:], ACT.Copy).then_inc(s_qhi, 1)
                    act.wait_ge(s_qhi, GROUPS * n + g + 1)
                    if GROUPS * n + g >= 2:
                        act.wait_ge(s_norm, GROUPS * n + g - 1)
                    act.activation(q_sq[:, g % 2, :], words(q_hi[:, g, :]), ACT.Square).then_inc(s_qsq, 1)

            def relus(n):
                act.wait_ge(s_s, n + 1)
                for j in range(HH):
                    if HH * n + j >= NR:
                        act.wait_ge(s_g, HH * n + j - NR + 1)
                    act.activation(relu[:, j % NR, :], s_sb[:], ACT.Relu, bias=small[:, HH + j:HH + j + 1],
                                   scale=small[:, j:j + 1]).then_inc(s_relu, 1)

            high(0)
            if query is not None:
                act.wait_ge(s_ahead, 16)
                act.activation(ahead[0][:], ahead_raw[:], ACT.Copy).then_inc(s_ahi, 1)
            if ffn is not None:
                act.wait_ge(s_small, FFN_LOADS)
                act.activation(wi_hi[:], wi_raw[:], ACT.Copy).then_inc(s_wi, 1)
            for n in range(CHUNKS + 1):
                if n >= 1:
                    high_transposed(n - 1)
                if n + 1 < CHUNKS:
                    high(n + 1)
                if n >= 1:
                    if ffn is None:
                        high_queries(n - 1)
                    else:
                        relus(n - 1)

        @block.tensor
        def _(pe):
            def project(n, then):
                for t in range(TC):
                    if t % 2 == 0:
                        pe.wait_ge(s_hi, 2 * n + t // 2 + 1)
                        pe.wait_ge(s_lo, 2 * n + t // 2 + 1)
                    if n >= 1:
                        pe.wait_ge(s_y, TC * (n - 1) + t + 1)
                    tok = slice(t * P, (t + 1) * P)
                    for c in range(C):
                        pe.matmul(o_ps[t][:], o_hi[n % NO][:, c, tok], w_hi[:, c, :], start=(c == 0), stop=False)
                        pe.matmul(o_ps[t][:], o_hi[n % NO][:, c, tok], w_lo[:, c, :], start=False, stop=False)
                        last = pe.matmul(o_ps[t][:], o_lo[n % NO][:, c, tok], w_hi[:, c, :], start=False, stop=(c == C - 1))
                    last.then_inc(s_mm, 1)
                    if t == 0 and query is not None and n >= 2:
                        norm(n - 2, 2)
                        norm(n - 2, 3)
                    then(t)

            def transpose(n):
                if query is not None and n >= 1:
                    pe.wait_ge(s_top, GROUPS * n)
                for t in range(TC):
                    pe.wait_ge(s_xn, TC * n + t + 1)
                    if t < 2 and n >= 1:
                        pe.wait_ge(s_tlo, TC * n)
                    if t == 2 and n >= 1:
                        if query is not None:
                            pe.wait_ge(s_qlo, GROUPS * n)
                        else:
                            pe.wait_ge(s_s, n)
                            if n >= 2:
                                pe.wait_ge(s_fin, TC * (n - 1))
                    for c in range(DC):
                        last = pe.transpose(turned[t][:, c * P:(c + 1) * P], xn[:, t, c * P:(c + 1) * P], ident[:])
                    last.then_inc(s_tr, 1)

            def three(ps, a_hi, a_lo):
                for c in range(DC):
                    pe.matmul(ps, a_hi(c), xT_hi[:, c, :], start=(c == 0), stop=False)
                    pe.matmul(ps, a_hi(c), xT_lo[:, c, :], start=False, stop=False)
                    last = pe.matmul(ps, a_lo(c), xT_hi[:, c, :], start=False, stop=(c == DC - 1))
                last.then_inc(s_z, 1)

            def norm(n, g):
                pe.wait_ge(s_qsq, GROUPS * n + g + 1)
                if g >= 2:
                    pe.wait_ge(s_top, GROUPS * n + g - 1)
                pe.matmul(t_ps[g % 2][:], ones_block[:], q_sq[:, g % 2, :], start=True, stop=True).then_inc(s_norm, 1)

            def queries(n):
                pe.wait_ge(s_tlo, TC * (n + 1))
                for g in range(GROUPS):
                    if GROUPS * n + g >= 2:
                        pe.wait_ge(s_qlo, GROUPS * n + g - 1)
                    e = slice(g * P, (g + 1) * P)
                    three(z_ps[g % 2][:], lambda c: wq_hi[:, c, e], lambda c: wq_lo[:, c, e])
                    if g in (1, 2):
                        norm(n, g - 1)

            def units(n):
                pe.wait_ge(s_tlo, TC * (n + 1))
                if n == 0:
                    pe.wait_ge(s_wi, 2)
                done = n if n < CHUNKS - 1 else n - 1
                if done > 0:
                    pe.wait_ge(s_fin, TC * done)
                three(z_ps[0][:], lambda c: wi_hi[:, c, :], lambda c: wi_lo[:, c, :])

            def last_product(n, t):
                if t == 0:
                    pe.wait_ge(s_g, HH * (n + 1))
                    pe.wait_ge(s_tlo, TC * min(n + 2, CHUNKS))
                    pe.wait_ge(s_s, n + 1 if n + 2 < CHUNKS else CHUNKS)
                if TC * n + t >= 2:
                    pe.wait_ge(s_fin, TC * n + t - 1)
                pe.matmul(z_ps[(t + 1) % 2][:], g_sb[:, n % 2, t * P:(t + 1) * P], wo2[:], start=True, stop=True)\
                    .then_inc(s_f, 1)

            for n in range(CHUNKS + 2):
                def then(t):
                    if t == 1 and 1 <= n <= CHUNKS:
                        transpose(n - 1)
                        if ffn is not None and n == CHUNKS:
                            units(n - 1)
                    if ffn is not None and n >= 2 and t >= 2:
                        last_product(n - 2, 2 * t - 4)
                        last_product(n - 2, 2 * t - 3)

                if n < CHUNKS:
                    project(n, then)
                else:
                    if query is not None:
                        for g in range(2, GROUPS):
                            norm(n - 2, g)
                    for t in range(TC):
                        then(t)
                if 1 <= n <= CHUNKS:
                    if ffn is None:
                        queries(n - 1)
                    elif n < CHUNKS:
                        units(n - 1)


def kernel(**inputs):
    import numpy as np
    import concourse.bacc as bacc
    from concourse.bass_utils import run_bass_kernel_spmd

    a = {k: np.asarray(v) for k, v in inputs.items()}

    def t(name):
        return a[name].T

    wqkv = np.stack([t("L0_attn_Wq").reshape(D, PAIRS, P), t("L0_attn_Wk").reshape(D, PAIRS, P),
                     t("L0_attn_Wv").reshape(D, PAIRS, P)], axis=2)
    arrays = {
        "x": a["x"],
        "ctxT": a["ctx_1024"].reshape(B, L // HALF, HALF, D).transpose(0, 1, 3, 2),
        "mask": a["mask_BxSxS2_if1"].transpose(0, 2, 1),
        "wqkv": wqkv.transpose(1, 0, 2, 3).reshape(PAIRS, D, 3 * P),
        "wo_xwqT": np.concatenate([t("L0_attn_Wo"), t("L0_xattn_w_q")]),
        "bo": a["L0_attn_bo"],
        "qk_scale": np.stack([a["L0_attn_q_scale"].reshape(PAIRS, P), a["L0_attn_k_scale"].reshape(PAIRS, P)], axis=2),
        "xwkvT": np.stack([t("L0_xattn_w_k"), t("L0_xattn_w_v")]),
        "xwoT": t("L0_xattn_w_o"),
        "win": a["L0_ffn_Win"], "bin_": a["L0_ffn_bin_"], "w1": a["L0_ffn_W1"], "b1": a["L0_ffn_b1"],
        "w2": a["L0_ffn_W2"], "b2": a["L0_ffn_b2"], "wout": a["L0_ffn_Wout"], "bout": a["L0_ffn_bout"],
    }
    nc = bacc.Bacc("TRN2", target_bir_lowering=False, num_devices=1)
    args = {}
    for name, value in arrays.items():
        arrays[name] = np.ascontiguousarray(value)
        args[name] = nc.dram_tensor(name, value.shape, mybir.dt.from_np(value.dtype), kind="ExternalInput").ap()
    args["out"] = nc.dram_tensor("out", (B, N, D), F32, kind="ExternalOutput").ap()
    decoder_layer(nc, **args)
    return run_bass_kernel_spmd(nc, [arrays], core_ids=[0]).results[0]["out"]
```
